# Optimizing a Trainium2 kernel written in Bass

```python
import numpy as np
import jax
import jax.numpy as jnp

def _softmax(x, axis=-1):
    return jax.nn.softmax(x, axis=axis)

def _gelu(x):
    return jax.nn.gelu(x, approximate=True)

def _silu(x):
    return jax.nn.silu(x)

def _sigmoid(x):
    return jax.nn.sigmoid(x)

def _layernorm(x, axis=-1, eps=1e-05):
    m = jnp.mean(x, axis=axis, keepdims=True)
    v = jnp.var(x, axis=axis, keepdims=True)
    return (x - m) / jnp.sqrt(v + eps)

def _scatter_add(tgt, idx, src, axis=0):
    return tgt.at[idx].add(src)

def _segment_sum(src, seg, n):
    return jax.ops.segment_sum(src, seg, n)
kernel_name = 'mk_xattn_seq_d2_seqx_r8_09b8d9'

def setup_inputs(seed: int=0):
    np.random.seed(seed)
    _w = jnp.asarray

    def _rec_inputs():
        import jax
        import jax.numpy as jnp
        _rk = jax.random.key(seed)
        x = -0.0002928 + 1 * jax.random.normal(jax.random.fold_in(_rk, 1), (16, 128, 256), jnp.float32)
        _lenS = 128 - jax.random.randint(jax.random.fold_in(_rk, 7), (16,), 0, max(1, 128 // 4) + 1, jnp.int32)
        _lenS2 = 128 - jax.random.randint(jax.random.fold_in(_rk, 8), (16,), 0, max(1, 128 // 4) + 1, jnp.int32)
        _ctx_2048P = jax.random.normal(jax.random.fold_in(_rk, 11), (16, 16, 256), jnp.float32)
        _ctx_2048c = jax.random.dirichlet(jax.random.fold_in(_rk, 511), 0.3 * jnp.ones((16,), jnp.float32), (16, 128))
        _ctx_2048t = jnp.einsum('bsk,bkd->bsd', _ctx_2048c, _ctx_2048P)
        _ctx_2048t = _ctx_2048t * jax.lax.rsqrt(jnp.mean(jnp.square(_ctx_2048t)) + 1e-12) * 0.953939
        ctx_2048 = -1.39393e-06 + 0.999914 * (_ctx_2048t + 0.3 * jax.random.normal(jax.random.fold_in(_rk, 611), (16, 128, 256), jnp.float32))
        return (x, ctx_2048)
    x, ctx_2048 = _rec_inputs()

    def _L0_xattn_setup():
        import math
        import jax, jax.numpy as jnp
        import numpy as np
        C = 128
        H = 16
        DH = C // H
        EPS = 1e-05

        def pos_enc(c, T, dtype):
            pos = jnp.arange(T, dtype=jnp.float32)[:, None]
            div = jnp.exp(jnp.arange(0, c, 2, dtype=jnp.float32) * (-math.log(10000.0) / c))
            ang = pos * div
            pe = jnp.zeros((T, c), dtype=jnp.float32)
            pe = pe.at[:, 0::2].set(jnp.sin(ang)).at[:, 1::2].set(jnp.cos(ang))
            return pe.T.astype(dtype)

        def layer_norm(x, g, b):
            mu = jnp.mean(x, axis=-1, keepdims=True)
            var = jnp.mean(jnp.square(x - mu), axis=-1, keepdims=True)
            return (x - mu) * jax.lax.rsqrt(var + EPS) * g + b
        key = jax.random.key(seed)
        ks = jax.random.split(key, 16)
        s = 1.0 / math.sqrt(C)
        inp = {'zt_prev': jax.random.normal(ks[0], (2, C, 256), jnp.float32), 'za': jax.random.normal(ks[1], (2, C, 256), jnp.float32), 'Wq': jax.random.normal(ks[2], (C, C), jnp.float32) * s, 'Wk': jax.random.normal(ks[3], (C, C), jnp.float32) * s, 'Wv': jax.random.normal(ks[4], (C, C), jnp.float32) * s, 'Wo': jax.random.normal(ks[5], (C, C), jnp.float32) * s, 'ln_q_g': jnp.ones((C,), jnp.float32), 'ln_q_b': jnp.zeros((C,), jnp.float32), 'ln_kv_g': jnp.ones((C,), jnp.float32), 'ln_kv_b': jnp.zeros((C,), jnp.float32), 'ffn_ln_g': jnp.ones((C,), jnp.float32), 'ffn_ln_b': jnp.zeros((C,), jnp.float32), 'W1': jax.random.normal(ks[6], (C, 2 * C), jnp.float32) * s, 'b1': jnp.zeros((2 * C,), jnp.float32), 'W2': jax.random.normal(ks[7], (2 * C, C), jnp.float32) * (1.0 / math.sqrt(2 * C)), 'b2': jnp.zeros((C,), jnp.float32)}
        return inp
    _L0_xattn_all = _L0_xattn_setup()
    _L0_xattn_in = {k: v for k, v in _L0_xattn_all.items() if k in ('Wq', 'Wk', 'Wv', 'Wo', 'ln_q_g', 'ln_q_b', 'ln_kv_g', 'ln_kv_b', 'ffn_ln_g', 'ffn_ln_b', 'W1', 'b1', 'W2', 'b2')}
    del _L0_xattn_all

    def _L1_xattn_setup():
        import jax, jax.numpy as jnp
        import numpy as np
        E, H, L, B = (256, 32, 128, 4)
        S = E // H
        DM, DD = (32, 64)

        def _ln(x, w, b, eps=1e-05):
            m = x.mean(-1, keepdims=True)
            v = ((x - m) ** 2).mean(-1, keepdims=True)
            return (x - m) / jnp.sqrt(v + eps) * w + b

        def _block(x, state, ln1_w, ln1_b, ln2_w, ln2_b, maa_x, maa_w1, maa_w2, maa_stack, time_decay, td_w1, td_w2, u, Wr, Wk, Wv, Wg, Wo, gn_w, gn_b, ffn_maa_k, ffn_maa_r, Wfk, Wfr, Wfv):
            b, l, e = x.shape
            h = u.shape[0]
            s_ = e // h
            xa = _ln(x, ln1_w, ln1_b)
            sx = jnp.concatenate([state[:, 1:2] - xa[:, :1], xa[:, :-1] - xa[:, 1:]], axis=1)
            xxx = jnp.tanh((xa + sx * maa_x) @ maa_w1).reshape(b, l, 5, DM)
            xxx = jnp.einsum('blfd,fde->blfe', xxx, maa_w2)
            xm = xa[:, :, None] + sx[:, :, None] * (maa_stack + xxx)
            xk, xw, xv, xr, xg = (xm[:, :, j] for j in range(5))
            w = jnp.exp(-jnp.exp(time_decay + jnp.tanh(xw @ td_w1) @ td_w2)).reshape(b, l, h, s_)
            r = (xr @ Wr.T).reshape(b, l, h, s_)
            k = (xk @ Wk.T).reshape(b, l, h, s_)
            v = (xv @ Wv.T).reshape(b, l, h, s_)
            g = jax.nn.silu(xg @ Wg.T)
            s0 = state[:, 2:2 + s_].reshape(b, h, s_, s_)

            def step(s, rkvw):
                r_t, k_t, v_t, w_t = rkvw
                a = k_t[..., :, None] * v_t[..., None, :]
                out = jnp.einsum('bhi,bhij->bhj', r_t, u * a + s)
                s = a + w_t[..., :, None] * s
                return (s, out)
            rkvw = tuple((jnp.moveaxis(t, 1, 0) for t in (r, k, v, w)))
            _, out = jax.lax.scan(step, s0, rkvw)
            out = jnp.moveaxis(out, 0, 1).reshape(b, l, e)
            og = out.reshape(b, l, h, s_)
            m = og.mean(-1, keepdims=True)
            va = ((og - m) ** 2).mean(-1, keepdims=True)
            og = ((og - m) / jnp.sqrt(va + 1e-05)).reshape(b, l, e) * gn_w + gn_b
            x1 = x + og * g @ Wo.T
            xc = _ln(x1, ln2_w, ln2_b)
            sx2 = jnp.concatenate([state[:, 0:1] - xc[:, :1], xc[:, :-1] - xc[:, 1:]], axis=1)
            xk2 = xc + sx2 * ffn_maa_k
            xr2 = xc + sx2 * ffn_maa_r
            rr = jax.nn.sigmoid(xr2 @ Wfr.T)
            kk = jnp.square(jax.nn.relu(xk2 @ Wfk.T))
            return x1 + rr * (kk @ Wfv.T)
        key = jax.random.key(seed)
        ks = jax.random.split(key, 24)
        sc = 0.02
        d = {'x': jax.random.normal(ks[0], (B, L, E), jnp.float32), 'state': jax.random.normal(ks[1], (B, 2 + S, E), jnp.float32) * 0.1, 'ln1_w': jnp.ones((E,), jnp.float32), 'ln1_b': jnp.zeros((E,), jnp.float32), 'ln2_w': jnp.ones((E,), jnp.float32), 'ln2_b': jnp.zeros((E,), jnp.float32), 'maa_x': jax.random.normal(ks[2], (E,), jnp.float32) * 0.1, 'maa_w1': jax.random.normal(ks[3], (E, 5 * DM), jnp.float32) * sc, 'maa_w2': jax.random.normal(ks[4], (5, DM, E), jnp.float32) * sc, 'maa_stack': jax.random.normal(ks[5], (1, 5, E), jnp.float32) * 0.1, 'time_decay': jax.random.normal(ks[6], (E,), jnp.float32) * 0.5, 'td_w1': jax.random.normal(ks[7], (E, DD), jnp.float32) * sc, 'td_w2': jax.random.normal(ks[8], (DD, E), jnp.float32) * sc, 'u': jax.random.normal(ks[9], (H, S, 1), jnp.float32) * 0.1, 'Wr': jax.random.normal(ks[10], (E, E), jnp.float32) * sc, 'Wk': jax.random.normal(ks[11], (E, E), jnp.float32) * sc, 'Wv': jax.random.normal(ks[12], (E, E), jnp.float32) * sc, 'Wg': jax.random.normal(ks[13], (E, E), jnp.float32) * sc, 'Wo': jax.random.normal(ks[14], (E, E), jnp.float32) * sc, 'gn_w': jnp.ones((E,), jnp.float32), 'gn_b': jnp.zeros((E,), jnp.float32), 'ffn_maa_k': jax.random.normal(ks[15], (E,), jnp.float32) * 0.1, 'ffn_maa_r': jax.random.normal(ks[16], (E,), jnp.float32) * 0.1, 'Wfk': jax.random.normal(ks[17], (E, E), jnp.float32) * sc, 'Wfr': jax.random.normal(ks[18], (E, E), jnp.float32) * sc, 'Wfv': jax.random.normal(ks[19], (E, E), jnp.float32) * sc}
        return d
    _L1_xattn_all = _L1_xattn_setup()
    _L1_xattn_in = {k: v for k, v in _L1_xattn_all.items() if k in ('ln1_w', 'ln1_b', 'ln2_w', 'ln2_b', 'maa_x', 'maa_w1', 'maa_w2', 'maa_stack', 'time_decay', 'td_w1', 'td_w2', 'u', 'Wr', 'Wk', 'Wv', 'Wg', 'Wo', 'gn_w', 'gn_b', 'ffn_maa_k', 'ffn_maa_r', 'Wfk', 'Wfr', 'Wfv')}
    del _L1_xattn_all
    return {'x': x, 'ctx_2048': ctx_2048, 'L0_xattn_Wq': _L0_xattn_in['Wq'], 'L0_xattn_Wk': _L0_xattn_in['Wk'], 'L0_xattn_Wv': _L0_xattn_in['Wv'], 'L0_xattn_Wo': _L0_xattn_in['Wo'], 'L0_xattn_ln_q_g': _L0_xattn_in['ln_q_g'], 'L0_xattn_ln_q_b': _L0_xattn_in['ln_q_b'], 'L0_xattn_ln_kv_g': _L0_xattn_in['ln_kv_g'], 'L0_xattn_ln_kv_b': _L0_xattn_in['ln_kv_b'], 'L0_xattn_ffn_ln_g': _L0_xattn_in['ffn_ln_g'], 'L0_xattn_ffn_ln_b': _L0_xattn_in['ffn_ln_b'], 'L0_xattn_W1': _L0_xattn_in['W1'], 'L0_xattn_b1': _L0_xattn_in['b1'], 'L0_xattn_W2': _L0_xattn_in['W2'], 'L0_xattn_b2': _L0_xattn_in['b2'], 'L1_xattn_ln1_w': _L1_xattn_in['ln1_w'], 'L1_xattn_ln1_b': _L1_xattn_in['ln1_b'], 'L1_xattn_ln2_w': _L1_xattn_in['ln2_w'], 'L1_xattn_ln2_b': _L1_xattn_in['ln2_b'], 'L1_xattn_maa_x': _L1_xattn_in['maa_x'], 'L1_xattn_maa_w1': _L1_xattn_in['maa_w1'], 'L1_xattn_maa_w2': _L1_xattn_in['maa_w2'], 'L1_xattn_maa_stack': _L1_xattn_in['maa_stack'], 'L1_xattn_time_decay': _L1_xattn_in['time_decay'], 'L1_xattn_td_w1': _L1_xattn_in['td_w1'], 'L1_xattn_td_w2': _L1_xattn_in['td_w2'], 'L1_xattn_u': _L1_xattn_in['u'], 'L1_xattn_Wr': _L1_xattn_in['Wr'], 'L1_xattn_Wk': _L1_xattn_in['Wk'], 'L1_xattn_Wv': _L1_xattn_in['Wv'], 'L1_xattn_Wg': _L1_xattn_in['Wg'], 'L1_xattn_Wo': _L1_xattn_in['Wo'], 'L1_xattn_gn_w': _L1_xattn_in['gn_w'], 'L1_xattn_gn_b': _L1_xattn_in['gn_b'], 'L1_xattn_ffn_maa_k': _L1_xattn_in['ffn_maa_k'], 'L1_xattn_ffn_maa_r': _L1_xattn_in['ffn_maa_r'], 'L1_xattn_Wfk': _L1_xattn_in['Wfk'], 'L1_xattn_Wfr': _L1_xattn_in['Wfr'], 'L1_xattn_Wfv': _L1_xattn_in['Wfv']}

def reference(x, ctx_2048, L0_xattn_Wq, L0_xattn_Wk, L0_xattn_Wv, L0_xattn_Wo, L0_xattn_ln_q_g, L0_xattn_ln_q_b, L0_xattn_ln_kv_g, L0_xattn_ln_kv_b, L0_xattn_ffn_ln_g, L0_xattn_ffn_ln_b, L0_xattn_W1, L0_xattn_b1, L0_xattn_W2, L0_xattn_b2, L1_xattn_ln1_w, L1_xattn_ln1_b, L1_xattn_ln2_w, L1_xattn_ln2_b, L1_xattn_maa_x, L1_xattn_maa_w1, L1_xattn_maa_w2, L1_xattn_maa_stack, L1_xattn_time_decay, L1_xattn_td_w1, L1_xattn_td_w2, L1_xattn_u, L1_xattn_Wr, L1_xattn_Wk, L1_xattn_Wv, L1_xattn_Wg, L1_xattn_Wo, L1_xattn_gn_w, L1_xattn_gn_b, L1_xattn_ffn_maa_k, L1_xattn_ffn_maa_r, L1_xattn_Wfk, L1_xattn_Wfr, L1_xattn_Wfv):
    import jax
    import jax.numpy as jnp

    def _L0_xattn_ref(zt_prev, za, Wq, Wk, Wv, Wo, ln_q_g, ln_q_b, ln_kv_g, ln_kv_b, ffn_ln_g, ffn_ln_b, W1, b1, W2, b2):
        import math
        import jax, jax.numpy as jnp
        import numpy as np
        C = 128
        H = 16
        DH = C // H
        EPS = 1e-05

        def pos_enc(c, T, dtype):
            pos = jnp.arange(T, dtype=jnp.float32)[:, None]
            div = jnp.exp(jnp.arange(0, c, 2, dtype=jnp.float32) * (-math.log(10000.0) / c))
            ang = pos * div
            pe = jnp.zeros((T, c), dtype=jnp.float32)
            pe = pe.at[:, 0::2].set(jnp.sin(ang)).at[:, 1::2].set(jnp.cos(ang))
            return pe.T.astype(dtype)

        def layer_norm(x, g, b):
            mu = jnp.mean(x, axis=-1, keepdims=True)
            var = jnp.mean(jnp.square(x - mu), axis=-1, keepdims=True)
            return (x - mu) * jax.lax.rsqrt(var + EPS) * g + b
        B, _, Tq = zt_prev.shape
        Tk = za.shape[-1]
        q = jnp.transpose(zt_prev + pos_enc(C, Tq, zt_prev.dtype)[None], (0, 2, 1))
        kv = jnp.transpose(za + pos_enc(C, Tk, za.dtype)[None], (0, 2, 1))
        q = layer_norm(q, ln_q_g, ln_q_b)
        kv = layer_norm(kv, ln_kv_g, ln_kv_b)

        def split(x):
            Bt, T, _ = x.shape
            return jnp.transpose(x.reshape(Bt, T, H, DH), (0, 2, 1, 3))
        Q = split(q @ Wq)
        K = split(kv @ Wk)
        V = split(kv @ Wv)
        attn = jnp.einsum('bhqd,bhkd->bhqk', Q, K) / math.sqrt(DH)
        ctx = jnp.einsum('bhqk,bhkd->bhqd', jax.nn.softmax(attn, axis=-1), V)
        ctx = jnp.transpose(ctx, (0, 2, 1, 3)).reshape(B, Tq, C)
        y = ctx @ Wo
        r = y + q
        h = layer_norm(r, ffn_ln_g, ffn_ln_b)
        h = jax.nn.gelu(h @ W1 + b1, approximate=False) @ W2 + b2
        out = h + r
        return jnp.transpose(out, (0, 2, 1))

    def _L1_xattn_ref(x, state, ln1_w, ln1_b, ln2_w, ln2_b, maa_x, maa_w1, maa_w2, maa_stack, time_decay, td_w1, td_w2, u, Wr, Wk, Wv, Wg, Wo, gn_w, gn_b, ffn_maa_k, ffn_maa_r, Wfk, Wfr, Wfv):
        import jax, jax.numpy as jnp
        import numpy as np
        E, H, L, B = (256, 32, 128, 4)
        S = E // H
        DM, DD = (32, 64)

        def _ln(x, w, b, eps=1e-05):
            m = x.mean(-1, keepdims=True)
            v = ((x - m) ** 2).mean(-1, keepdims=True)
            return (x - m) / jnp.sqrt(v + eps) * w + b

        def _block(x, state, ln1_w, ln1_b, ln2_w, ln2_b, maa_x, maa_w1, maa_w2, maa_stack, time_decay, td_w1, td_w2, u, Wr, Wk, Wv, Wg, Wo, gn_w, gn_b, ffn_maa_k, ffn_maa_r, Wfk, Wfr, Wfv):
            b, l, e = x.shape
            h = u.shape[0]
            s_ = e // h
            xa = _ln(x, ln1_w, ln1_b)
            sx = jnp.concatenate([state[:, 1:2] - xa[:, :1], xa[:, :-1] - xa[:, 1:]], axis=1)
            xxx = jnp.tanh((xa + sx * maa_x) @ maa_w1).reshape(b, l, 5, DM)
            xxx = jnp.einsum('blfd,fde->blfe', xxx, maa_w2)
            xm = xa[:, :, None] + sx[:, :, None] * (maa_stack + xxx)
            xk, xw, xv, xr, xg = (xm[:, :, j] for j in range(5))
            w = jnp.exp(-jnp.exp(time_decay + jnp.tanh(xw @ td_w1) @ td_w2)).reshape(b, l, h, s_)
            r = (xr @ Wr.T).reshape(b, l, h, s_)
            k = (xk @ Wk.T).reshape(b, l, h, s_)
            v = (xv @ Wv.T).reshape(b, l, h, s_)
            g = jax.nn.silu(xg @ Wg.T)
            s0 = state[:, 2:2 + s_].reshape(b, h, s_, s_)

            def step(s, rkvw):
                r_t, k_t, v_t, w_t = rkvw
                a = k_t[..., :, None] * v_t[..., None, :]
                out = jnp.einsum('bhi,bhij->bhj', r_t, u * a + s)
                s = a + w_t[..., :, None] * s
                return (s, out)
            rkvw = tuple((jnp.moveaxis(t, 1, 0) for t in (r, k, v, w)))
            _, out = jax.lax.scan(step, s0, rkvw)
            out = jnp.moveaxis(out, 0, 1).reshape(b, l, e)
            og = out.reshape(b, l, h, s_)
            m = og.mean(-1, keepdims=True)
            va = ((og - m) ** 2).mean(-1, keepdims=True)
            og = ((og - m) / jnp.sqrt(va + 1e-05)).reshape(b, l, e) * gn_w + gn_b
            x1 = x + og * g @ Wo.T
            xc = _ln(x1, ln2_w, ln2_b)
            sx2 = jnp.concatenate([state[:, 0:1] - xc[:, :1], xc[:, :-1] - xc[:, 1:]], axis=1)
            xk2 = xc + sx2 * ffn_maa_k
            xr2 = xc + sx2 * ffn_maa_r
            rr = jax.nn.sigmoid(xr2 @ Wfr.T)
            kk = jnp.square(jax.nn.relu(xk2 @ Wfk.T))
            return x1 + rr * (kk @ Wfv.T)
        return _block(x, state, ln1_w, ln1_b, ln2_w, ln2_b, maa_x, maa_w1, maa_w2, maa_stack, time_decay, td_w1, td_w2, u, Wr, Wk, Wv, Wg, Wo, gn_w, gn_b, ffn_maa_k, ffn_maa_r, Wfk, Wfr, Wfv)
    x = _L0_xattn_ref(x, ctx_2048, L0_xattn_Wq, L0_xattn_Wk, L0_xattn_Wv, L0_xattn_Wo, L0_xattn_ln_q_g, L0_xattn_ln_q_b, L0_xattn_ln_kv_g, L0_xattn_ln_kv_b, L0_xattn_ffn_ln_g, L0_xattn_ffn_ln_b, L0_xattn_W1, L0_xattn_b1, L0_xattn_W2, L0_xattn_b2)
    x = _L1_xattn_ref(x, ctx_2048, L1_xattn_ln1_w, L1_xattn_ln1_b, L1_xattn_ln2_w, L1_xattn_ln2_b, L1_xattn_maa_x, L1_xattn_maa_w1, L1_xattn_maa_w2, L1_xattn_maa_stack, L1_xattn_time_decay, L1_xattn_td_w1, L1_xattn_td_w2, L1_xattn_u, L1_xattn_Wr, L1_xattn_Wk, L1_xattn_Wv, L1_xattn_Wg, L1_xattn_Wo, L1_xattn_gn_w, L1_xattn_gn_b, L1_xattn_ffn_maa_k, L1_xattn_ffn_maa_r, L1_xattn_Wfk, L1_xattn_Wfr, L1_xattn_Wfv)
    return x

_drawn_inputs = setup_inputs


def setup_inputs(seed=0):
    import zlib

    import numpy as np

    out = dict(_drawn_inputs(seed))
    spreads = {'L0_xattn_ln_q_g': (1.0, 0.2),
     'L0_xattn_ln_q_b': (0.0, 0.1),
     'L0_xattn_ln_kv_g': (1.0, 0.2),
     'L0_xattn_ln_kv_b': (0.0, 0.1),
     'L0_xattn_ffn_ln_g': (1.0, 0.2),
     'L0_xattn_ffn_ln_b': (0.0, 0.1),
     'L0_xattn_b1': (0.0, 0.1),
     'L0_xattn_b2': (0.0, 0.501),
     'L1_xattn_ln1_w': (1.0, 0.6),
     'L1_xattn_ln1_b': (0.0, 0.731),
     'L1_xattn_ln2_w': (1.0, 0.6),
     'L1_xattn_ln2_b': (0.0, 0.8),
     'L1_xattn_gn_w': (1.0, 0.6),
     'L1_xattn_gn_b': (0.0, 0.8)}
    factors = {'L1_xattn_maa_x': 8.0,
     'L1_xattn_maa_w1': 8.0,
     'L1_xattn_maa_w2': 8.0,
     'L1_xattn_maa_stack': 3.545,
     'L1_xattn_time_decay': 3.636,
     'L1_xattn_td_w1': 8.0,
     'L1_xattn_td_w2': 8.0,
     'L1_xattn_u': 7.535,
     'L1_xattn_ffn_maa_k': 8.0,
     'L1_xattn_ffn_maa_r': 8.0,
     'L1_xattn_Wfk': 3.629,
     'L1_xattn_Wfr': 8.0,
     'L1_xattn_Wfv': 3.334}
    for name, (base, spread) in spreads.items():
        noise = np.random.default_rng([zlib.crc32(name.encode()), seed]).standard_normal(out[name].shape)
        drawn = base * np.exp(spread * noise) if base else spread * noise
        out[name] = jnp.asarray(drawn.astype(out[name].dtype))
    for name, factor in factors.items():
        out[name] = (out[name] * factor).astype(out[name].dtype)
    return out
```

```python
import math
import numpy as np
import concourse.bass as bass
from concourse import mybir
from contextlib import ExitStack

F32 = mybir.dt.float32
BF16 = mybir.dt.bfloat16
ACT = mybir.ActivationFunctionType
ALU = mybir.AluOpType
AX_X = mybir.AxisListType.X

NB, C, T = 16, 128, 256
H0, D0 = 16, 8
NQB = T // 128
EPS = 1e-5

NPART = 3
NTERM = 6
ROWS = D0 * NTERM
MROWS = 2
NTILE = H0 // 2
UNITS = 16
PV_LAG = 2
NPROB = 8
LAG = 8
SLOTS = 4


class Turn:

    def __init__(self, it, c):
        self.n = it * SLOTS + c
        self.slot = c % SLOTS
        self.use = it + c // SLOTS


def need(engine, sem, value):
    if isinstance(value, int) and value <= 0:
        return
    engine.wait_ge(sem, value)


def attention(nc, env):
    sb, pb, sem, W = env["sb"], env["pb"], env["sem"], env["in"]
    scr = env["dram"]

    xin = [sb(f"xin{s}", [128, 2, T], F32) for s in range(2)] * 2
    xpe = [sb(f"xpe{s}", [128, 2, T], F32) for s in range(2)] * 2
    pe_tab = sb("pe_tab", [128, 2, T], F32)
    wq, wk, wv = sb("wq", [128, 128], F32), sb("wk", [128, 128], F32), sb("wv", [128, 128], F32)
    lnc = sb("ln_consts", [128, 4], F32)
    stats = sb("stats", [128, 4, 6], F32)
    mv = sb("mv", [128, 4, 2], F32)
    rstd = sb("rstd", [128, 4], F32)
    xn = sb("xn", [128, 4, 128], F32)
    qkvT = [sb(f"qkvT{s}", [128, 2, T], F32) for s in range(2)] * 2
    parts = [sb(f"parts{s}", [128, 2, NPART, T], BF16) for s in range(2)] * 2
    rest = sb("rest", [128, 2, T], F32)
    QK = [sb(f"QK{s}", [128, 2, NTILE, T], BF16) for s in range(SLOTS)]
    QS = [QK[s][:, 0, :, :] for s in range(SLOTS)]
    KS = [QK[s][:, 1, :, :] for s in range(SLOTS)]
    VA = [sb(f"VA{s}", [128, NQB, H0, 32], F32) for s in range(SLOTS)]
    mx = sb("mx", [128, NQB, H0], F32)
    mparts = sb("mparts", [128, NQB, MROWS, H0], BF16)
    mT = [sb(f"mT{s}", [32, T], BF16) for s in range(2)] * 2
    prob = [sb(f"prob{s}", [128, 2, T], F32) for s in range(NPROB)]
    raw = [sb(f"raw{s}", [128, 4, T], F32) for s in range(2)] * 2
    ident, ident_b, half, epst, zero = env["ident"], env["ident_b"], env["half"], env["epst"], env["zero"]

    SM, SC, VB = pb[0:2], pb[2:4], pb[4:6]
    M0, M1 = pb[6], pb[7]
    m0 = M0[:, :].rearrange("p (a t) -> p a t", a=4)
    m1 = M1[:, :].rearrange("p (a t) -> p a t", a=4)
    m1b = M1[:, 0:128].bitcast(BF16)

    consts_in, const_set = env["consts_in"], env["const_set"]
    NCONST, NSET = env["nconst"], env["nset"]
    x_in = [sem(f"x_in{s}") for s in range(SLOTS)]
    pos_added = sem("pos_added")
    tokens_ready = sem("tokens_ready")
    stats_done, aggr_done, var_done = sem("stats_done"), sem("aggr_done"), sem("var_done")
    rstd_ready, normed = sem("rstd_ready"), sem("normed")
    channels_ready, qkvT_ready = sem("channels_ready"), sem("qkvT_ready")
    qk_ready, v_ready = sem("qk_ready"), sem("v_ready")
    part1_done, rest_done, part2_done, part3_done = sem("part1_done"), sem("rest_done"), sem("part2_done"), sem("part3_done")
    va_ready = sem("va_ready")
    q_kept = [sem(f"q_kept{s}") for s in range(SLOTS)]
    stack_out = [sem(f"stack_out{s}") for s in range(SLOTS)]
    stack_in = [sem(f"stack_in{s}") for s in range(SLOTS)]
    m_in = [sem(f"m_in{s}") for s in range(SLOTS)]
    raw_out = [sem(f"raw_out{s}") for s in range(SLOTS)]
    smax_ready, max_done = sem("smax_ready"), sem("max_done")
    mhigh_done, mparts_ready, mT_psum, mT_ready = sem("mhigh_done"), sem("mparts_ready"), sem("mT_psum"), sem("mT_ready")
    scores_ready, exp_done, pv_done, raw_ready = sem("scores_ready"), sem("exp_done"), sem("pv_done"), sem("raw_ready")

    STACK_OUT, STACK_IN, M_IN, RAW_OUT = 6 * 16, 4 * 16, 4 * 16, 16

    def in_range(v, c_off, static):
        return not static or 0 <= v + c_off < NB

    def plan(it, c, static):
        def turn(off):
            return Turn(it, c + off) if in_range(c, off, static) else None
        return {"x": turn(2), "a": turn(2), "l": turn(1), "b": turn(0), "h": turn(-1), "t": turn(-2)}

    def stream(p, s):
        return (p["t"], s + UNITS - LAG) if s < LAG else (p["h"], s - LAG)

    def iterations(engine, run):
        for v in range(-2, 2):
            run(plan(0, v, True))
        with engine.Fori(0, 3) as it:
            for c in range(2, 2 + SLOTS):
                run(plan(it, c, False))
        for v in range(14, 18):
            run(plan(0, v, True))

    def unit(u):
        return u // 8, (u % 8) // 2, u % 2

    def cunit(u):
        return (u % 4) // 2, u // 4, u % 2

    def tensor(pe):
        def run(p):
            for s in range(UNITS):
                if p["b"]:
                    b = p["b"]
                    if s == 0:
                        pe.wait_ge(stack_in[b.slot], b.use * STACK_IN + STACK_IN)
                    qb, tp, hh = unit(s)
                    need(pe, max_done, b.n * UNITS + s - 1)
                    for a in range(2):
                        r = slice(64 * hh, 64 * hh + ROWS)
                        last = nc.tensor.matmul(SM[hh][:, a * T:(a + 1) * T], QS[b.slot][r, 2 * tp + a, qb * 128:(qb + 1) * 128],
                                                KS[b.slot][r, 2 * tp + a, :], start=True, stop=True)
                    last.then_inc(smax_ready, 1)
                cur, u = stream(p, s)
                if cur:
                    kb, tp, hh = cunit(u)
                    if u == 0:
                        pe.wait_ge(m_in[cur.slot], cur.use * M_IN + M_IN)
                    need(pe, exp_done, cur.n * UNITS + u - 1)
                    for a in range(2):
                        r = slice(64 * hh, 64 * hh + ROWS + MROWS)
                        last = nc.tensor.matmul(SC[hh][:, a * T:(a + 1) * T], KS[cur.slot][r, 2 * tp + a, kb * 128:(kb + 1) * 128],
                                                QS[cur.slot][r, 2 * tp + a, :], start=True, stop=True)
                    last.then_inc(scores_ready, 1)
                prev, u = stream(p, s - PV_LAG)
                if prev and u % 2 == 1:
                    kb, tp, _ = cunit(u)
                    if u == 1:
                        pe.wait_ge(va_ready, prev.n + 1)
                    if u % 8 == 1:
                        need(pe, raw_ready, prev.n * 2 - 1 + u // 8)
                    pe.wait_ge(exp_done, prev.n * UNITS + u + 1)
                    for j in range(4):
                        hh, a = j // 2, j % 2
                        last = nc.tensor.matmul(VB[tp // 2][32 * j:32 * j + 32, (tp % 2) * T:(tp % 2 + 1) * T],
                                                VA[prev.slot][:, kb, 2 * tp + a + NTILE * hh, :], prob[(u - 1 + hh) % NPROB][:, a, :],
                                                start=(kb == 0), stop=(kb == 1))
                    last.then_inc(pv_done, 2)
                a_ = p["a"]
                if s == 4 and a_:
                    pe.wait_ge(pos_added, a_.n + 1)
                    need(pe, rest_done, a_.n)
                    for j in range(4):
                        last = nc.tensor.transpose(m0[:, j, :], xpe[a_.slot][:, j // 2, (j % 2) * 128:(j % 2 + 1) * 128], ident[:, :])
                    last.then_inc(tokens_ready, 1)
                if s == 2 and p["h"]:
                    h = p["h"]
                    pe.wait_ge(mparts_ready, h.n + 1)
                    need(pe, va_ready, h.n + (3 if p["l"] else 2 if p["b"] else 1))
                    for qb in range(NQB):
                        last = nc.tensor.transpose(m1b[0:32, qb * 128:(qb + 1) * 128], mparts[:, qb, :, :], ident_b[:, :])
                    last.then_inc(mT_psum, 1)
                if s == 8 and a_:
                    pe.wait_ge(normed, a_.n + 1)
                    need(pe, mT_ready, a_.n - 2)
                    need(pe, va_ready, a_.n)
                    for j in range(4):
                        last = nc.tensor.transpose(m1[:, j, :], xn[:, j, :], ident[:, :])
                    last.then_inc(channels_ready, 1)
                if s == 10 and a_:
                    pe.wait_ge(qkvT_ready, a_.n + 1)
                    src = qkvT[a_.slot]
                    nc.tensor.matmul(M0[:, 0:T], wq[:, :], src[:, 0, :], start=True, stop=True)
                    nc.tensor.matmul(M0[:, T:2 * T], wk[:, :], src[:, 1, :], start=True, stop=True).then_inc(qk_ready, 1)
                    for kb in range(NQB):
                        last = nc.tensor.matmul(M1[:, kb * 128:(kb + 1) * 128], src[:, 1, kb * 128:(kb + 1) * 128], wv[:, :],
                                                start=True, stop=True)
                    last.then_inc(v_ready, 1)
        iterations(pe, run)

    def scalar(act):
        def run(p):
            if p["x"]:
                x = p["x"]
                need(act, pos_added, x.n - 1)
                act.dma_start(xin[x.slot][:, :, :], W["x_ctx"][bass.ds(x.n, 1), :, :, :].rearrange("o c w t -> (o c) w t")).then_inc(x_in[x.slot], 16)
            for s in range(UNITS):
                cur, u = stream(p, s)
                if cur:
                    act.wait_ge(scores_ready, cur.n * UNITS + u + 1)
                    need(act, pv_done, cur.n * UNITS + u - NPROB + 1 + u % 2)
                    nc.scalar.activation(prob[u % NPROB][:, :, :].rearrange("p a t -> p (a t)"), SC[u % 2][:, :], ACT.Exp,
                                         scale=1.0 / math.sqrt(D0)).then_inc(exp_done, 1)
                if s in (PV_LAG, LAG + PV_LAG) and p["t"]:
                    t, half_ = p["t"], s // LAG
                    act.wait_ge(pv_done, t.n * UNITS + 8 * half_ + 8)
                    if half_ == 0:
                        need(act, raw_out[(t.slot + 2) % SLOTS], (t.use + (t.slot + 2) // SLOTS) * RAW_OUT)
                    nc.scalar.activation(raw[t.slot][:, 2 * half_:2 * half_ + 2, :].rearrange("p a t -> p (a t)"), VB[half_][:, :],
                                         ACT.Copy).then_inc(raw_ready, 1)
                if s == 3 and p["h"]:
                    h = p["h"]
                    act.wait_ge(mT_psum, h.n + 1)
                    need(act, m_in[(h.slot + 2) % SLOTS], (h.use + (h.slot + 2) // SLOTS) * M_IN)
                    nc.scalar.activation(mT[h.slot][:, :], m1b[0:32, :], ACT.Copy).then_inc(mT_ready, 1)
                if s == 4 and p["h"]:
                    h = p["h"]
                    act.wait_ge(mT_ready, h.n + 1)
                    for hh in range(2):
                        for part in range(MROWS):
                            row = 64 * hh + ROWS + part
                            act.dma_start(QS[h.slot][row:row + 1, :, :].rearrange("o t q -> o (t q)"),
                                          mT[h.slot][H0 * part + NTILE * hh:H0 * part + NTILE * hh + NTILE, :]).then_inc(m_in[h.slot], 16)
                a = p["a"]
                if s == 9 and a:
                    act.wait_ge(channels_ready, a.n + 1)
                    need(act, q_kept[(a.slot + 2) % SLOTS], (a.use + (a.slot + 2) // SLOTS) * 16)
                    for w in range(2):
                        last = nc.scalar.activation(qkvT[a.slot][:, w, :], M1[:, w * T:(w + 1) * T], ACT.Identity,
                                                    bias=lnc[:, 2 * w + 1:2 * w + 2], scale=lnc[:, 2 * w:2 * w + 1])
                    last.then_inc(qkvT_ready, 1)
                if s == 11 and a:
                    act.wait_ge(qk_ready, a.n + 1)
                    need(act, stack_out[(a.slot + 2) % SLOTS], (a.use + (a.slot + 2) // SLOTS) * STACK_OUT)
                    nc.scalar.activation(parts[a.slot][:, :, 0, :], M0[:, :].rearrange("p (w t) -> p w t", w=2),
                                         ACT.Copy).then_inc(part1_done, 1)
                if s == 12 and a:
                    act.wait_ge(v_ready, a.n + 1)
                    if isinstance(a.n, int) and a.n < SLOTS:
                        act.wait_ge(const_set, NSET)
                    need(act, pv_done, a.n * UNITS - (SLOTS - 1) * UNITS)
                    nc.scalar.activation(VA[a.slot][:, :, :, 0:D0], M1[:, 0:T].rearrange("p (k h d) -> p k h d", k=NQB, h=H0),
                                         ACT.Copy).then_inc(va_ready, 1)
        iterations(act, run)

    def vector(dve):
        def run(p):
            for s in range(UNITS):
                a = p["a"]
                if s == 6 and a:
                    dve.wait_ge(stats_done, a.n + 1)
                    need(dve, rstd_ready, a.n)
                    need(dve, normed, a.n)
                if p["b"]:
                    b = p["b"]
                    qb, tp, hh = unit(s)
                    dve.wait_ge(smax_ready, b.n * UNITS + s + 1)
                    if s == 0:
                        need(dve, mparts_ready, b.n)
                    nc.vector.tensor_reduce(mx[:, qb, NTILE * hh + 2 * tp:NTILE * hh + 2 * tp + 2], SM[hh][:, :].rearrange("p (a t) -> p a t", a=2),
                                            AX_X, ALU.max, negate=True).then_inc(max_done, 1)
                if s == 5 and a:
                    dve.wait_ge(tokens_ready, a.n + 1)
                    need(dve, aggr_done, a.n)
                    for j in range(4):
                        last = nc.vector.bn_stats(stats[:, j, :], m0[:, j, :])
                    last.then_inc(stats_done, 1)
                if s == 6 and a:
                    for j in range(4):
                        last = nc.vector.bn_aggr(mv[:, j, :], stats[:, j, :])
                    last.then_inc(aggr_done, 1)
                if s == 7 and a:
                    dve.wait_ge(rstd_ready, a.n + 1)
                    need(dve, channels_ready, a.n)
                    for j in range(4):
                        last = nc.vector.tensor_scalar(xn[:, j, :], m0[:, j, :], mv[:, j, 0:1], rstd[:, j:j + 1], ALU.subtract, ALU.mult)
                    last.then_inc(normed, 1)
                if s == 12 and a:
                    dve.wait_ge(part1_done, a.n + 1)
                    need(dve, part3_done, a.n)
                    nc.vector.tensor_tensor(rest[:, :, :], M0[:, :].rearrange("p (w t) -> p w t", w=2),
                                            parts[a.slot][:, :, 0, :], ALU.subtract).then_inc(rest_done, 1)
                if s == UNITS - 1 and p["b"]:
                    b = p["b"]
                    dve.wait_ge(max_done, b.n * UNITS + UNITS)
                    need(dve, mT_psum, b.n)
                    nc.vector.tensor_copy(mparts[:, :, 0, :], mx[:, :, :]).then_inc(mhigh_done, 1)
                    dve.wait_ge(mhigh_done, b.n + 1)
                    nc.vector.tensor_tensor(mparts[:, :, 1, :], mx[:, :, :], mparts[:, :, 0, :], ALU.subtract).then_inc(mparts_ready, 1)
        iterations(dve, run)

    def gpsimd(pool):
        def run(p):
            a, x2 = p["a"], p["x"]
            if x2:
                pool.wait_ge(x_in[x2.slot], x2.use * 16 + 16)
                if isinstance(x2.n, int) and x2.n == 0:
                    pool.wait_ge(consts_in, NCONST)
                need(pool, tokens_ready, x2.n - 2)
                nc.gpsimd.tensor_tensor(xpe[x2.slot][:, :, :], xin[x2.slot][:, :, :], pe_tab[:, :, :], ALU.add).then_inc(pos_added, 1)
            if a:
                pool.wait_ge(aggr_done, a.n + 1)
                need(pool, normed, a.n)
                nc.gpsimd.tensor_tensor(rstd[:, :], mv[:, :, 1], epst[:, 0:4], ALU.add).then_inc(var_done, 1)
                pool.wait_ge(var_done, a.n + 1)
                nc.gpsimd.tensor_tensor(rstd[:, :], rstd[:, :], half[:, 0:4], ALU.pow).then_inc(rstd_ready, 1)
                pool.wait_ge(rest_done, a.n + 1)
                part = parts[a.slot]
                nc.gpsimd.tensor_tensor(part[:, :, 1, :], rest[:, :, :], zero[:, :, :].broadcast_to((128, 2, T)), ALU.add).then_inc(part2_done, 1)
                pool.wait_ge(part2_done, a.n + 1)
                nc.gpsimd.tensor_tensor(part[:, :, 2, :], rest[:, :, :], part[:, :, 1, :], ALU.subtract).then_inc(part3_done, 1)
        iterations(pool, run)

    def tables(sp):
        for w in range(2):
            sp.dma_start(pe_tab[:, w, :], W["pos"]).then_inc(consts_in, 16)
        for dst, src in ((wq, "L0_xattn_Wq"), (wk, "L0_xattn_Wk"), (wv, "L0_xattn_Wv")):
            sp.dma_start(dst[:, :], W[src]).then_inc(consts_in, 16)
        for j, name in enumerate(("ln_q_g", "ln_q_b", "ln_kv_g", "ln_kv_b")):
            sp.dma_start(lnc[:, j:j + 1], W["L0_xattn_" + name].unsqueeze(1)).then_inc(consts_in, 16)

    def sync(sp):
        def run(p):
            a, t, l = p["a"], p["t"], p["l"]
            raw_dst = scr["raw"][bass.ds(t.n, 1), :, :, :].rearrange("o p g q -> (o p) g q") if t else None
            q_dst = scr["q"][bass.ds(a.n, 1), :, :].rearrange("o c t -> (o c) t") if a else None
            if l:
                sp.wait_ge(stack_out[l.slot], l.use * STACK_OUT + STACK_OUT)
                need(sp, scores_ready, l.n * UNITS - (SLOTS - 1) * UNITS)
                if isinstance(l.n, int) and l.n < SLOTS:
                    sp.wait_ge(const_set, NSET)
                for w in range(2):
                    view = scr["stack"][l.slot, w].rearrange("(hh t d) m q -> hh (d m) t q", hh=2, d=D0)
                    for hh in range(2):
                        sp.dma_start(QK[l.slot][64 * hh:64 * hh + ROWS, w, :, :], view[hh]).then_inc(stack_in[l.slot], 16)
            if t:
                sp.wait_ge(raw_ready, t.n * 2 + 2)
                sp.dma_start(raw_dst, raw[t.slot][:, :, :]).then_inc(raw_out[t.slot], 16)
            if a:
                sp.wait_ge(qkvT_ready, a.n + 1)
                sp.dma_start(q_dst, qkvT[a.slot][:, 0, :]).then_inc(q_kept[a.slot], 16)
                sp.wait_ge(part3_done, a.n + 1)
                need(sp, stack_in[a.slot], a.use * STACK_IN)
                dst, part = scr["stack"][a.slot], parts[a.slot]
                for w, m, n, p0 in ((0, 0, 3, 0), (0, 3, 2, 1), (0, 5, 1, 2), (1, 0, 3, None), (1, 3, 2, None), (1, 5, 1, None)):
                    src = part[:, w, 0:n, :] if p0 is None else part[:, w, p0:p0 + 1, :].broadcast_to((128, n, T))
                    sp.dma_start(dst[w, :, m:m + n, :], src).then_inc(stack_out[a.slot], 16)
        iterations(sp, run)
        for s in range(SLOTS):
            uses = (NB - s + SLOTS - 1) // SLOTS
            sp.wait_ge(raw_out[s], uses * RAW_OUT)
            sp.wait_ge(q_kept[s], uses * 16)

    def set_consts(pool, done):
        pieces = [(VA[s][:, :, :, :], 0.0) for s in range(SLOTS)]
        pieces += [(KS[s][r:r + 32, :, :], 1.0) for s in range(SLOTS) for r in (32, 96)]
        pieces += [(VA[s][:, :, :, D0:D0 + 1], 1.0) for s in range(SLOTS)]
        for piece, value in pieces:
            pool.wait_ge(const_set, done)
            nc.gpsimd.memset(piece, value).then_inc(const_set, 1)
            done += 1
        pool.wait_ge(const_set, done)

    return {"tensor": tensor, "scalar": scalar, "vector": vector, "gpsimd": gpsimd, "sync": sync, "set": set_consts, "tables": tables}


FP = 2
NPAIR = NB // FP
F0 = 2 * C // 128


class Pair:

    def __init__(self, it, c):
        self.n = it * 2 + c
        self.slot = c % 2
        self.use = it + c // 2


def feed_forward(nc, env):
    sb, pb, sem, W, scr = env["sb"], env["pb"], env["sem"], env["in"], env["dram"]
    ident, half, epst = env["ident"], env["half"], env["epst"]
    wo, w1, w2, fvec = env["f_wo"], env["f_w1"], env["f_w2"], env["f_vec"]

    den = sb("den", [128, 512], F32)
    ctx_t = [sb(f"f_ctx{s}", [128, FP, T], F32) for s in range(2)]
    rden = [sb(f"f_rden{s}", [128, FP, T], F32) for s in range(2)]
    q_t = [sb(f"f_q{s}", [128, FP, T], F32) for s in range(2)]
    cn = [sb(f"f_cn{s}", [128, FP * T], F32) for s in range(2)]
    xn = sb("f_xn", [128, 4, 128], F32)
    hT = [sb(f"f_h{s}", [128, FP * T], F32) for s in range(2)]
    ge = [sb(f"f_ge{s}", [128, F0, FP * T], F32) for s in range(2)]
    o = [sb(f"f_o{s}", [128, FP, T], F32) for s in range(2)]
    r = [sb(f"f_res{s}", [128, FP * T], F32) for s in range(2)]
    rk = [sb(f"f_resk{s}", [128, FP * T], F32) for s in range(2)]
    stats, mv, rstd = sb("f_stats", [128, 4, 6], F32), sb("f_mv", [128, 4, 2], F32), sb("f_rstd", [128, 4], F32)
    Y, T1, T2, FF, O = pb[0], pb[1], pb[2], pb[3:5], pb[5]
    t1, t2 = (b[:, :].rearrange("p (a t) -> p a t", a=4) for b in (T1, T2))

    den_in, den_done, den_out = sem("den_in"), sem("den_done"), sem("den_out")
    f_in = [sem(f"f_in{s}") for s in range(2)]
    f_kept = [sem(f"f_kept{s}") for s in range(2)]
    f_ctx, f_y, f_r, f_tok = sem("f_ctx_ready"), sem("f_y_ready"), sem("f_r_ready"), sem("f_tokens_ready")
    f_stats, f_aggr, f_var, f_rstd = sem("f_stats_done"), sem("f_aggr_done"), sem("f_var_done"), sem("f_rstd_ready")
    f_normed, f_chan, f_h = sem("f_normed"), sem("f_channels_ready"), sem("f_h_ready")
    f_hid, f_ge, f_ff, f_out, f_rk = sem("f_hidden_ready"), sem("f_gelu_ready"), sem("f_ff_ready"), sem("f_out_ready"), sem("f_r_biased")
    IN = 6 * 16

    def plan(it, c, static):
        def pair(off):
            return Pair(it, c + off) if not static or 0 <= c + off < NPAIR else None
        return pair(0), pair(-1), pair(-2)

    def iterations(engine, run):
        for v in (0, 1):
            run(*plan(0, v, True))
        with engine.Fori(1, NPAIR // 2) as it:
            for c in (0, 1):
                run(*plan(it, c, False))
        for v in (NPAIR, NPAIR + 1):
            run(*plan(0, v, True))

    def sync(sp):
        for g2 in range(2):
            src = scr["raw"].rearrange("b (j r) g q -> (b j) r g q", j=4)[:, D0, 2 * g2:2 * g2 + 2, :]
            sp.dma_start(den[64 * g2:64 * g2 + 64, :].rearrange("p (g q) -> p g q", g=2), src).then_inc(den_in, 16)
        sp.wait_ge(den_done, 1)
        view = scr["rden"].rearrange("b j d (h g) q -> h (b j) d (g q)", h=2)
        for g2 in range(2):
            sp.dma_start(view[g2], den[64 * g2:64 * g2 + 64, :].unsqueeze(1).broadcast_to((64, D0, 512))).then_inc(den_out, 16)
        sp.wait_ge(den_out, 32)

        def run(a, b, c):
            if a:
                need(sp, f_ctx, a.n - 1)
                need(sp, f_r, a.n - 1)
                raw = scr["raw"][bass.ds(a.n * 2, 2), :, :, :].rearrange("b (j r) g q -> j r g b q", j=4)
                for j in range(4):
                    sp.dma_start(ctx_t[a.slot][32 * j:32 * j + 32, :, :], raw[j, 0:D0].rearrange("r g b q -> (r g) b q")).then_inc(f_in[a.slot], 16)
                sp.dma_start(rden[a.slot][:, :, :], scr["rden"][bass.ds(a.n * 2, 2)].rearrange("b j d g q -> (j d g) b q")).then_inc(f_in[a.slot], 16)
                sp.dma_start(q_t[a.slot][:, :, :], scr["q"][bass.ds(a.n * 2, 2), :, :].rearrange("b c q -> c b q")).then_inc(f_in[a.slot], 16)
        iterations(sp, run)
        for s in range(2):
            sp.wait_ge(f_kept[s], NPAIR // 2 * 16)

    def gpsimd(pool):
        def run(a, b, c):
            if a:
                pool.wait_ge(f_in[a.slot], a.use * IN + IN)
                need(pool, f_y, a.n - 1)
                nc.gpsimd.tensor_tensor(cn[a.slot][:, :], ctx_t[a.slot][:, :, :].rearrange("p b q -> p (b q)"),
                                        rden[a.slot][:, :, :].rearrange("p b q -> p (b q)"), ALU.mult).then_inc(f_ctx, 1)
                pool.wait_ge(f_aggr, a.n + 1)
                nc.gpsimd.tensor_tensor(rstd[:, :], mv[:, :, 1], epst[:, 0:4], ALU.add).then_inc(f_var, 1)
                pool.wait_ge(f_var, a.n + 1)
                nc.gpsimd.tensor_tensor(rstd[:, :], rstd[:, :], half[:, 0:4], ALU.pow).then_inc(f_rstd, 1)
        iterations(pool, run)

    def tensor(pe):
        def run(a, b, c):
            if a:
                pe.wait_ge(f_ctx, a.n + 1)
                need(pe, f_r, a.n)
                nc.tensor.matmul(Y[:, :], wo[:, :], cn[a.slot][:, :], start=True, stop=True).then_inc(f_y, 1)
            if c:
                pe.wait_ge(f_ge, c.n + 1)
                need(pe, f_out, c.n)
                for f in range(F0):
                    last = nc.tensor.matmul(O[:, :], w2[:, f, :], ge[c.slot][:, f, :], start=(f == 0), stop=(f == F0 - 1))
                last.then_inc(f_ff, 1)
            if b:
                pe.wait_ge(f_normed, b.n + 1)
                need(pe, f_h, b.n)
                for j in range(4):
                    last = nc.tensor.transpose(t2[:, j, :], xn[:, j, :], ident[:, :])
                last.then_inc(f_chan, 1)
            if a:
                pe.wait_ge(f_r, a.n + 1)
                for j in range(4):
                    last = nc.tensor.transpose(t1[:, j, :], r[a.slot][:, j * 128:(j + 1) * 128], ident[:, :])
                last.then_inc(f_tok, 1)
            if b:
                pe.wait_ge(f_h, b.n + 1)
                need(pe, f_ge, b.n)
                for f in range(F0):
                    last = nc.tensor.matmul(FF[f][:, :], w1[:, f * 128:(f + 1) * 128], hT[b.slot][:, :], start=True, stop=True)
                last.then_inc(f_hid, 1)
        iterations(pe, run)

    def scalar(act):
        def run(a, b, c):
            if b:
                act.wait_ge(f_chan, b.n + 1)
                nc.scalar.activation(hT[b.slot][:, :], T2[:, :], ACT.Identity, bias=fvec[:, 1:2], scale=fvec[:, 0:1]).then_inc(f_h, 1)
            if c:
                act.wait_ge(f_out, c.n + 1)
                act.dma_start(scr["x1"][bass.ds(c.n * 2, 2), :, :].rearrange("b c q -> c b q"), o[c.slot][:, :, :]).then_inc(f_kept[c.slot], 16)
            if b:
                act.wait_ge(f_hid, b.n + 1)
                need(act, f_ff, b.n - 1)
                for f in range(F0):
                    last = nc.scalar.activation(ge[b.slot][:, f, :], FF[f][:, :], ACT.Gelu, bias=fvec[:, 3 + f:4 + f])
                last.then_inc(f_ge, 1)
        iterations(act, run)

    def vector(dve):
        dve.wait_ge(den_in, 32)
        nc.vector.reciprocal(den[:, :], den[:, :]).then_inc(den_done, 1)

        def run(a, b, c):
            if a:
                dve.wait_ge(f_y, a.n + 1)
                nc.vector.tensor_tensor(r[a.slot][:, :], Y[:, :], q_t[a.slot][:, :, :].rearrange("p b q -> p (b q)"), ALU.add).then_inc(f_r, 1)
            if c:
                dve.wait_ge(f_ff, c.n + 1)
                dve.wait_ge(f_rk, c.n + 1)
                need(dve, f_kept[c.slot], c.use * 16)
                nc.vector.tensor_tensor(o[c.slot][:, :, :].rearrange("p b q -> p (b q)"), O[:, :], rk[c.slot][:, :], ALU.add).then_inc(f_out, 1)
            if a:
                dve.wait_ge(f_tok, a.n + 1)
                for j in range(4):
                    last = nc.vector.bn_stats(stats[:, j, :], t1[:, j, :])
                last.then_inc(f_stats, 1)
                dve.wait_ge(f_stats, a.n + 1)
                need(dve, f_rstd, a.n)
                need(dve, f_normed, a.n)
                need(dve, f_out, a.n - 1)
                dve.wait_ge(f_r, a.n + 1)
                nc.vector.tensor_scalar(rk[a.slot][:, :], r[a.slot][:, :], fvec[:, 2:3], None, ALU.add).then_inc(f_rk, 1)
                for j in range(4):
                    last = nc.vector.bn_aggr(mv[:, j, :], stats[:, j, :])
                last.then_inc(f_aggr, 1)
                dve.wait_ge(f_rstd, a.n + 1)
                need(dve, f_chan, a.n)
                for j in range(4):
                    last = nc.vector.tensor_scalar(xn[:, j, :], t1[:, j, :], mv[:, j, 0:1], rstd[:, j:j + 1], ALU.subtract, ALU.mult)
                last.then_inc(f_normed, 1)
        iterations(dve, run)

    return {"tensor": tensor, "scalar": scalar, "vector": vector, "gpsimd": gpsimd, "sync": sync}


L1, E1, H1, S1 = 128, 256, 32, 8
EB = E1 // 128
GB = 4
NG = NB // GB
NMIX, DM, DD = 5, 32, 64
JH = 4
VECS = ("ln1_w", "ln1_b", "maa_x", "stack0", "stack1", "stack2", "stack3", "stack4", "time_decay", "u", "gn_w", "gn_b",
        "ln2_w", "ln2_b", "ffn_maa_k", "ffn_maa_r")
MIX_K, MIX_W, MIX_V, MIX_R, MIX_G = range(NMIX)
MIX_ORDER = (MIX_W, MIX_K, MIX_V, MIX_R, MIX_G)


def recurrent(nc, env):
    sb, pb, sem, W, scr = env["sb"], env["pb"], env["sem"], env["in"], env["dram"]
    ident, half, epst = env["ident"], env["half"], env["epst"]
    w, vec, hvec = env["g_w"], env["g_vec"], env["g_hvec"]
    maa1, maa2, maa2b, td1, td2 = env["g_maa1"], env["g_maa2"], env["g_maa2b"], env["g_td1"], env["g_td2"]
    hsel = env["g_hsel"]
    esum, blk, cmat, blkh = env["g_esum"], env["g_blk"], env["g_cmat"], env["g_blkh"]
    N = GB * L1

    def v(name, eb):
        return vec[:, eb, VECS.index(name):VECS.index(name) + 1]

    def t3(name):
        return sb(name, [128, EB, N], F32)

    def bl(ap):
        return ap.rearrange("p (b l) -> p b l", b=GB)

    x_in = sb("g_x", [128, GB, E1], F32)
    st = sb("g_st", [128, EB, 2, GB], F32)
    s0 = sb("g_s0", [128, EB, S1, GB], F32)
    xn = sb("g_xn", [128, GB, E1], F32)
    xa = sb("g_xa", [128, EB, GB, L1 + 1], F32)
    sx = t3("g_sx")
    mixin = t3("g_mixin")
    th5, th5b = sb("g_th5", [128, N], F32), sb("g_th5b", [DM, N], F32)
    z = [sb(f"g_z{i}", [128, N], F32) for i in range(2)]
    xm = [t3(f"g_xm{f}") for f in range(NMIX)]
    tdh = sb("g_tdh", [DD, N], F32)
    ew = t3("g_ew")
    wS = t3("g_wS")
    kT, vT, rT, gs = t3("g_k"), t3("g_v"), t3("g_r"), t3("g_gs")
    gth = sb("g_gth", [128, N], F32)
    vbc = [sb(f"g_vbc{i}", [128, JH, N], F32) for i in range(2)]
    aS = [sb(f"g_a{i}", [128, JH, N], F32) for i in range(2)]
    SS = [sb(f"g_S{i}", [128, JH, N], F32) for i in range(2)]
    ruk, og = t3("g_ruk"), t3("g_og")
    x1 = sb("g_x1", [128, GB, E1], F32)
    xk, xr, kk = t3("g_xk"), t3("g_xr"), t3("g_kk")
    stats, mv, rstd = sb("g_stats", [128, GB, 6], F32), sb("g_mv", [128, GB, 2], F32), sb("g_rstd", [128, GB], F32)
    rg, rgT = sb("g_rg", [128, GB, H1], F32), sb("g_rgT", [H1, N], F32)
    cent, sq, on, gated = xm[0], xm[1], xm[2], xm[3]
    th2 = xm[4][:, :, :].rearrange("p a n -> p (a n)").rearrange("p (b e) -> p b e", b=GB)
    y = xm[0][:, :, :].rearrange("p a n -> p (a n)").rearrange("p (b e) -> p b e", b=GB)
    out_t = xm[1][:, :, :].rearrange("p a n -> p (a n)").rearrange("p (b e) -> p b e", b=GB)

    decay_set = sem("g_decay_set")
    g_in, g_out, g_vout = sem("g_in"), sem("g_out"), sem("g_vout")
    g_vin = [sem(f"g_vin{i}") for i in range(2)]
    names = ("stats aggr var rstd normed feat featc xa edge sx mixin maa th5 xxx z xm proj evac gsd ewd kv edge2 scan rs summed ruk cb "
             "cv og cent sq var2 vg pow2 rgt rgtc rb on on2 gated wo x1 "
             "stats2 aggr2 var3 rstd2 normed2 feat2 xc edgec sx2 xk kkp kkr kk rrp th2 fvp y fin").split()
    s = {n: sem("g_" + n) for n in names}

    def groups(engine, run):
        run(0)
        with engine.Fori(1, NG) as n:
            run(n)

    UN = [(hb, jq) for hb in range(EB) for jq in range(S1 // JH)]
    NU = len(UN)
    PJ = 11

    def sync(sp):
        def run(n):
            need(sp, s["edge2"], n * NU)
            need(sp, s["edgec"], n)
            need(sp, s["fin"], n)
            sp.dma_start(x_in[:, :, :], scr["x1"][bass.ds(n * GB, GB), :, :].rearrange("b l e -> l b e")).then_inc(g_in, 16)
            sp.dma_start(st[:, :, :, :].rearrange("p a w b -> p (a w b)"), W["st"][bass.ds(n, 1), :, :].rearrange("o p x -> (o p) x")).then_inc(g_in, 16)
            sp.dma_start(s0[:, :, :, :].rearrange("p a j b -> p (a j b)"), W["s0"][bass.ds(n, 1), :, :].rearrange("o p x -> (o p) x")).then_inc(g_in, 16)
            sp.wait_ge(s["evac"], n * PJ + 7)
            sp.dma_start(scr["v"].rearrange("a p n -> p a n"), vT[:, :, :]).then_inc(g_vout, 16)
            sp.wait_ge(g_vout, n * 16 + 16)
            for i, (hb, jq) in enumerate(UN):
                if i >= 2:
                    sp.wait_ge(s["kv"], n * NU + i - 1)
                else:
                    need(sp, s["kv"], n * NU)
                src = scr["v"][hb].rearrange("(h q j) n -> q h (j n)", h=16, q=S1 // JH)[jq]
                sp.dma_start(vbc[i % 2][:, :, :].rearrange("p j n -> p (j n)"), src.unsqueeze(1).broadcast_to((16, S1, JH * N))).then_inc(g_vin[i % 2], 16)
            sp.wait_ge(s["fin"], n + 1)
            sp.dma_start(W["out"][bass.ds(n * GB, GB), :, :].rearrange("b l e -> l b e"), out_t).then_inc(g_out, 16)
        groups(sp, run)
        sp.wait_ge(g_out, NG * 16)

    def gpsimd(pool):
        def rsqrt(n, aggr, var, done):
            pool.wait_ge(s[aggr], n + 1)
            nc.gpsimd.tensor_tensor(rstd[:, :], mv[:, :, 1], epst[:, 0:GB], ALU.add).then_inc(s[var], 1)
            pool.wait_ge(s[var], n + 1)
            nc.gpsimd.tensor_tensor(rstd[:, :], rstd[:, :], half[:, 0:GB], ALU.pow).then_inc(s[done], 1)

        def shift(n, ready, edge, done):
            pool.wait_ge(s[ready], n + 1)
            pool.wait_ge(s[edge], n + 1)
            for eb in range(EB):
                last = nc.gpsimd.tensor_tensor(bl(sx[:, eb, :]), xa[:, eb, :, 0:L1], xa[:, eb, :, 1:L1 + 1], ALU.subtract)
            last.then_inc(s[done], 1)

        def run(n):
            need(pool, s["normed2"], n)
            rsqrt(n, "aggr", "var", "rstd")
            need(pool, s["xk"], n)
            shift(n, "xa", "edge", "sx")
            need(pool, s["evac"], n * PJ)
            need(pool, g_out, n * 16)
            for i in range(NMIX * EB):
                f, eb = MIX_ORDER[i // EB], i % EB
                pool.wait_ge(s["z"], n * NMIX * EB + i + 1)
                nc.gpsimd.tensor_tensor(bl(xm[f][:, eb, :]), bl(z[i % 2][:, :]), xa[:, eb, :, 1:L1 + 1], ALU.add).then_inc(s["xm"], 1)
            for i, (hb, jq) in enumerate(UN):
                pool.wait_ge(g_vin[i % 2], n * 32 + 16 * (i // 2) + 16)
                if i >= 2:
                    pool.wait_ge(s["summed"], n * NU + i - 1)
                else:
                    need(pool, s["summed"], n * NU)
                key = bl(kT[:, hb, :])[:, :, 0:L1 - 1].unsqueeze(1).broadcast_to((128, JH, GB, L1 - 1))
                a4 = aS[i % 2][:, :, :].rearrange("p j (b l) -> p j b l", b=GB)
                v4 = vbc[i % 2][:, :, :].rearrange("p j (b l) -> p j b l", b=GB)
                nc.gpsimd.tensor_tensor(a4[:, :, :, 1:L1], v4[:, :, :, 0:L1 - 1], key, ALU.mult).then_inc(s["kv"], 1)
            pool.wait_ge(s["vg"], n + 1)
            nc.gpsimd.tensor_tensor(rg[:, :, :].rearrange("p b h -> p (b h)"), rg[:, :, :].rearrange("p b h -> p (b h)"),
                                    half[:, 0:GB * H1], ALU.pow).then_inc(s["pow2"], 1)
            pool.wait_ge(s["on2"], n + 1)
            pool.wait_ge(s["gsd"], n * EB + EB)
            nc.gpsimd.tensor_tensor(gated[:, :, :], on[:, :, :], gs[:, :, :], ALU.mult).then_inc(s["gated"], 1)
            pool.wait_ge(s["normed"], n + 1)
            rsqrt(n, "aggr2", "var3", "rstd2")
            shift(n, "xc", "edgec", "sx2")
            pool.wait_ge(s["kkr"], n + 1)
            nc.gpsimd.tensor_tensor(kk[:, :, :], kk[:, :, :], kk[:, :, :], ALU.mult).then_inc(s["kk"], 1)
        groups(pool, run)

    def tensor(pe):
        def to_features(n, normed, done, free):
            pe.wait_ge(s[normed], n + 1)
            free()
            for eb in range(EB):
                for b in range(GB):
                    last = nc.tensor.transpose(pb[eb][:, b * L1:(b + 1) * L1], xn[:, b, eb * 128:(eb + 1) * 128], ident[:, :])
            last.then_inc(s[done], 1)

        def run(n):
            to_features(n, "normed", "feat", lambda: need(pe, s["xc"], n))
            pe.wait_ge(s["mixin"], n + 1)
            need(pe, s["kkr"], n)
            for eb in range(EB):
                nc.tensor.matmul(pb[2][:, :], maa1[:, eb, 0:128], mixin[:, eb, :], start=(eb == 0), stop=(eb == EB - 1))
            for eb in range(EB):
                last = nc.tensor.matmul(pb[3][0:DM, :], maa1[:, eb, 128:160], mixin[:, eb, :], start=(eb == 0), stop=(eb == EB - 1))
            last.then_inc(s["maa"], 1)
            pe.wait_ge(s["th5"], n + 1)
            need(pe, s["th2"], n)

            def mixes(f):
                i0 = MIX_ORDER.index(f) * EB
                for eb in range(EB):
                    i = i0 + eb
                    if i >= 2:
                        pe.wait_ge(s["z"], n * NMIX * EB + i - 1)
                    else:
                        need(pe, s["z"], n * NMIX * EB)
                    src = th5b[:, :] if f == 4 else th5[32 * f:32 * f + 32, :]
                    wt = maa2b[:, eb * 128:(eb + 1) * 128] if f == 4 else maa2[32 * f:32 * f + 32, eb * 128:(eb + 1) * 128]
                    if f == 4:
                        nc.tensor.matmul(pb[4 + i % 2][:, :], wt, src, start=True, stop=True).then_inc(s["xxx"], 1)
                    else:
                        nc.tensor.matmul(pb[4 + i % 2][:, :], wt, src, start=True, stop=True, tile_position=(32 * f, 0)).then_inc(s["xxx"], 1)

            def project(i0, f, wt):
                pe.wait_ge(s["xm"], n * NMIX * EB + (MIX_ORDER.index(f) + 1) * EB)
                for ob in range(EB):
                    bank_free(i0 + ob)
                    for eb in range(EB):
                        last = nc.tensor.matmul(pb[6 + (i0 + ob) % 2][:, :], wt[:, eb, ob * 128:(ob + 1) * 128], xm[f][:, eb, :],
                                                start=(eb == 0), stop=(eb == EB - 1))
                    last.then_inc(s["proj"], 1)

            def bank_free(i):
                if i >= 2:
                    pe.wait_ge(s["evac"], n * PJ + i - 1)
                else:
                    need(pe, s["y"], n * 2)

            mixes(MIX_W)
            mixes(MIX_K)
            pe.wait_ge(s["xm"], n * NMIX * EB + EB)
            bank_free(0)
            for eb in range(EB):
                last = nc.tensor.matmul(pb[6][0:DD, :], td1[:, eb, :], xm[MIX_W][:, eb, :], start=(eb == 0), stop=(eb == EB - 1))
            last.then_inc(s["proj"], 1)
            mixes(MIX_V)
            pe.wait_ge(s["evac"], n * PJ + 1)
            for ob in range(EB):
                bank_free(1 + ob)
                nc.tensor.matmul(pb[6 + (1 + ob) % 2][:, :], td2[:, ob * 128:(ob + 1) * 128], tdh[:, :], start=True, stop=True).then_inc(s["proj"], 1)
            project(3, MIX_K, w["Wk"])
            mixes(MIX_R)
            project(5, MIX_V, w["Wv"])
            mixes(MIX_G)
            project(7, MIX_R, w["Wr"])
            project(9, MIX_G, w["Wg"])
            pe.wait_ge(s["ruk"], n + 1)
            for hb in range(EB):
                last = nc.tensor.matmul(pb[2 + hb][:, :], blk[:, :], ruk[:, hb, :], start=True, stop=True)
            last.then_inc(s["cb"], 1)
            for i, (hb, jq) in enumerate(UN):
                pe.wait_ge(s["rs"], n * NU + i + 1)
                for j in range(JH):
                    last = nc.tensor.matmul(pb[hb][:, :], esum[:, jq * JH + j, :], aS[i % 2][:, j, :],
                                            start=(jq == 0 and j == 0), stop=(jq == S1 // JH - 1 and j == JH - 1))
                last.then_inc(s["summed"], 1)
            pe.wait_ge(s["og"], n + 1)
            for hb in range(EB):
                last = nc.tensor.matmul(pb[4 + hb][:, :], cmat[:, :], og[:, hb, :], start=True, stop=True)
            last.then_inc(s["cent"], 1)
            pe.wait_ge(s["sq"], n + 1)
            pe.wait_ge(s["gsd"], n * EB + EB)
            for b in range(GB):
                for hb in range(EB):
                    last = nc.tensor.matmul(pb[6][:, b * H1 + hb * 16:b * H1 + hb * 16 + 16], sq[:, hb, b * L1:(b + 1) * L1], blkh[:, :],
                                            start=True, stop=True)
            last.then_inc(s["var2"], 1)
            pe.wait_ge(s["pow2"], n + 1)
            pe.wait_ge(s["cv"], n + 1)
            for b in range(GB):
                last = nc.tensor.transpose(pb[7][0:H1, b * L1:(b + 1) * L1], rg[:, b, :], ident[:, :])
            last.then_inc(s["rgt"], 1)
            pe.wait_ge(s["rgtc"], n + 1)
            for hb in range(EB):
                last = nc.tensor.matmul(pb[2 + hb][:, :], hsel[:, hb, :], rgT[:, :], start=True, stop=True)
            last.then_inc(s["rb"], 1)

            def to_positions(src, wt, banks, done):
                for b in range(GB):
                    for eb in range(EB):
                        last = nc.tensor.matmul(banks[b // 2][:, (b % 2) * E1:(b % 2 + 1) * E1], src[:, eb, b * L1:(b + 1) * L1], wt[:, eb, :],
                                                start=(eb == 0), stop=(eb == EB - 1))
                last.then_inc(s[done], 1)

            pe.wait_ge(s["gated"], n + 1)
            to_positions(gated, w["Wo"], pb[6:8], "wo")
            to_features(n, "normed2", "feat2", lambda: None)
            pe.wait_ge(s["xk"], n + 1)
            for ob in range(EB):
                for eb in range(EB):
                    last = nc.tensor.matmul(pb[2 + ob][:, :], w["Wfk"][:, eb, ob * 128:(ob + 1) * 128], xk[:, eb, :],
                                            start=(eb == 0), stop=(eb == EB - 1))
            last.then_inc(s["kkp"], 1)
            to_positions(xr, w["Wfr"], pb[4:6], "rrp")
            pe.wait_ge(s["kk"], n + 1)
            to_positions(kk, w["Wfv"], pb[6:8], "fvp")
        groups(pe, run)

    def scalar(act):
        def run(n):
            act.wait_ge(s["feat"], n + 1)
            need(act, s["sx2"], n)
            need(act, s["xk"], n)
            for eb in range(EB):
                last = nc.scalar.activation(xa[:, eb, :, 1:L1 + 1], bl(pb[eb][:, :]), ACT.Identity, bias=v("ln1_b", eb), scale=v("ln1_w", eb))
            last.then_inc(s["xa"], 1)
            act.wait_ge(s["maa"], n + 1)
            need(act, s["xxx"], n * NMIX * EB)
            nc.scalar.activation(th5b[:, :], pb[3][0:DM, :], ACT.Tanh)
            nc.scalar.activation(th5[:, :], pb[2][:, :], ACT.Tanh).then_inc(s["th5"], 1)

            def ready(i):
                act.wait_ge(s["proj"], n * PJ + i + 1)
            ready(0)
            nc.scalar.activation(tdh[:, :], pb[6][0:DD, :], ACT.Tanh).then_inc(s["evac"], 1)
            for eb in range(EB):
                ready(1 + eb)
                if eb == 0:
                    need(act, s["scan"], n * NU)
                nc.scalar.activation(ew[:, eb, :], pb[6 + (1 + eb) % 2][:, :], ACT.Exp, bias=v("time_decay", eb)).then_inc(s["evac"], 1)
            act.wait_ge(s["evac"], n * PJ + 3)
            act.wait_ge(decay_set, 1)
            for eb in range(EB):
                last = nc.scalar.activation(bl(wS[:, eb, :])[:, :, 1:L1], bl(ew[:, eb, :])[:, :, 0:L1 - 1], ACT.Exp, scale=-1.0)
            last.then_inc(s["ewd"], 1)
            need(act, s["ruk"], n)
            need(act, s["cv"], n)
            need(act, s["kv"], n * NU)
            need(act, s["rs"], n * NU)
            need(act, g_vout, n * 16)
            for k, dst in enumerate((kT, vT, rT)):
                for eb in range(EB):
                    i = 3 + 2 * k + eb
                    ready(i)
                    nc.scalar.activation(dst[:, eb, :], pb[6 + i % 2][:, :], ACT.Copy).then_inc(s["evac"], 1)
            for eb in range(EB):
                ready(9 + eb)
                if eb:
                    act.wait_ge(s["gsd"], n * EB + eb)
                else:
                    need(act, s["gsd"], n * EB)
                nc.scalar.activation(gth[:, :], pb[6 + (9 + eb) % 2][:, :], ACT.Tanh, scale=0.5).then_inc(s["evac"], 1)
            act.wait_ge(s["cent"], n + 1)
            for hb in range(EB):
                nc.scalar.activation(sq[:, hb, :], pb[4 + hb][:, :], ACT.Square)
                last = nc.scalar.activation(cent[:, hb, :], pb[4 + hb][:, :], ACT.Copy)
            last.then_inc(s["sq"], 1)
            act.wait_ge(s["rgt"], n + 1)
            nc.scalar.activation(rgT[:, :], pb[7][0:H1, :], ACT.Copy).then_inc(s["rgtc"], 1)
            act.wait_ge(s["on"], n + 1)
            for hb in range(EB):
                last = nc.scalar.activation(on[:, hb, :], on[:, hb, :], ACT.Identity, bias=hvec[:, hb, 1:2], scale=hvec[:, hb, 0:1])
            last.then_inc(s["on2"], 1)
            act.wait_ge(s["feat2"], n + 1)
            for eb in range(EB):
                last = nc.scalar.activation(xa[:, eb, :, 1:L1 + 1], bl(pb[eb][:, :]), ACT.Identity, bias=v("ln2_b", eb), scale=v("ln2_w", eb))
            last.then_inc(s["xc"], 1)
            act.wait_ge(s["kkp"], n + 1)
            need(act, s["fvp"], n)
            for ob in range(EB):
                last = nc.scalar.activation(kk[:, ob, :], pb[2 + ob][:, :], ACT.Relu)
            last.then_inc(s["kkr"], 1)
            act.wait_ge(s["rrp"], n + 1)
            for i in range(2):
                last = nc.scalar.activation(th2[:, 2 * i:2 * i + 2, :].rearrange("p b e -> p (b e)"), pb[4 + i][:, :], ACT.Tanh, scale=0.5)
            last.then_inc(s["th2"], 1)
        groups(act, run)

    def vector(dve):
        dve.wait_ge(g_in, 48)
        nc.vector.memset(wS[:, :, :], 0.0).then_inc(decay_set, 1)

        def norm(n, src, names_, free, edge):
            st_, ag, rs_, nm = names_
            for b in range(GB):
                last = nc.vector.bn_stats(stats[:, b, :], src[:, b, :])
            last.then_inc(s[st_], 1)
            dve.wait_ge(s[st_], n + 1)
            edge()
            for b in range(GB):
                last = nc.vector.bn_aggr(mv[:, b, :], stats[:, b, :])
            last.then_inc(s[ag], 1)
            dve.wait_ge(s[rs_], n + 1)
            free()
            for b in range(GB):
                last = nc.vector.tensor_scalar(xn[:, b, :], src[:, b, :], mv[:, b, 0:1], rstd[:, b:b + 1], ALU.subtract, ALU.mult)
            last.then_inc(s[nm], 1)

        def run(n):
            dve.wait_ge(g_in, n * 48 + 48)

            def edge1():
                need(dve, s["sx2"], n)
                nc.vector.tensor_copy(xa[:, :, :, 0], st[:, :, 1, :]).then_inc(s["edge"], 1)
            norm(n, x_in, ("stats", "aggr", "rstd", "normed"), lambda: need(dve, s["feat2"], n), edge1)
            dve.wait_ge(s["sx"], n + 1)
            dve.wait_ge(s["xa"], n + 1)
            for eb in range(EB):
                last = nc.vector.scalar_tensor_tensor(bl(mixin[:, eb, :]), bl(sx[:, eb, :]), v("maa_x", eb), xa[:, eb, :, 1:L1 + 1], ALU.mult, ALU.add)
            last.then_inc(s["mixin"], 1)
            for i in range(NMIX * EB):
                f, eb = MIX_ORDER[i // EB], i % EB
                dve.wait_ge(s["xxx"], n * NMIX * EB + i + 1)
                if i >= 2:
                    dve.wait_ge(s["xm"], n * NMIX * EB + i - 1)
                else:
                    need(dve, s["xm"], n * NMIX * EB)
                nc.vector.scalar_tensor_tensor(z[i % 2][:, :], pb[4 + i % 2][:, :], v(f"stack{f}", eb), sx[:, eb, :], ALU.add, ALU.mult).then_inc(s["z"], 1)
            dve.wait_ge(s["evac"], n * PJ + 9)
            for hb in range(EB):
                last = nc.vector.scalar_tensor_tensor(ruk[:, hb, :], rT[:, hb, :], v("u", hb), kT[:, hb, :], ALU.mult, ALU.mult)
            last.then_inc(s["ruk"], 1)
            for eb in range(EB):
                dve.wait_ge(s["evac"], n * PJ + 10 + eb)
                nc.vector.scalar_tensor_tensor(gs[:, eb, :], gth[:, :], 1.0, pb[6 + (9 + eb) % 2][:, :], ALU.add, ALU.mult).then_inc(s["gsd"], 1)
            dve.wait_ge(s["ewd"], n + 1)
            for i, (hb, jq) in enumerate(UN):
                dve.wait_ge(s["kv"], n * NU + i + 1)
                a4 = aS[i % 2][:, :, :].rearrange("p j (b l) -> p j b l", b=GB)
                nc.vector.tensor_copy(a4[:, :, :, 0], s0[:, hb, jq * JH:(jq + 1) * JH, :]).then_inc(s["edge2"], 1)
                dve.wait_ge(s["edge2"], n * NU + i + 1)
                for j in range(JH):
                    last = nc.vector.tensor_tensor_scan(SS[i % 2][:, j, :], wS[:, hb, :], aS[i % 2][:, j, :], 0.0, ALU.mult, ALU.add)
                last.then_inc(s["scan"], 1)
                dve.wait_ge(s["scan"], n * NU + i + 1)
                nc.vector.tensor_tensor(aS[i % 2][:, :, :], SS[i % 2][:, :, :], rT[:, hb:hb + 1, :].broadcast_to((128, JH, N)), ALU.mult).then_inc(s["rs"], 1)
            dve.wait_ge(s["cb"], n + 1)
            need(dve, s["cent"], n)
            for hb in range(EB):
                last = nc.vector.tensor_tensor(og[:, hb, :], pb[2 + hb][:, :], vT[:, hb, :], ALU.mult)
            last.then_inc(s["cv"], 1)
            dve.wait_ge(s["cv"], n + 1)
            dve.wait_ge(s["summed"], n * NU + NU)
            for hb in range(EB):
                last = nc.vector.tensor_tensor(og[:, hb, :], pb[hb][:, :], og[:, hb, :], ALU.add)
            last.then_inc(s["og"], 1)
            dve.wait_ge(s["var2"], n + 1)
            need(dve, s["rb"], n)
            nc.vector.tensor_scalar(rg[:, :, :].rearrange("p b h -> p (b h)"), pb[6][:, 0:GB * H1], EPS, None, ALU.add).then_inc(s["vg"], 1)
            dve.wait_ge(s["rb"], n + 1)
            dve.wait_ge(s["sq"], n + 1)
            for hb in range(EB):
                last = nc.vector.tensor_tensor(on[:, hb, :], cent[:, hb, :], pb[2 + hb][:, :], ALU.mult)
            last.then_inc(s["on"], 1)
            dve.wait_ge(s["wo"], n + 1)
            for i in range(2):
                last = nc.vector.tensor_tensor(x1[:, 2 * i:2 * i + 2, :].rearrange("p b e -> p (b e)"), pb[6 + i][:, :],
                                               x_in[:, 2 * i:2 * i + 2, :].rearrange("p b e -> p (b e)"), ALU.add)
            last.then_inc(s["x1"], 1)
            dve.wait_ge(s["x1"], n + 1)
            dve.wait_ge(s["sx"], n + 1)

            def edge2():
                nc.vector.tensor_copy(xa[:, :, :, 0], st[:, :, 0, :]).then_inc(s["edgec"], 1)
            norm(n, x1, ("stats2", "aggr2", "rstd2", "normed2"), lambda: dve.wait_ge(s["feat"], n + 1), edge2)
            dve.wait_ge(s["sx2"], n + 1)
            dve.wait_ge(s["xc"], n + 1)
            for dst, name in ((xk, "ffn_maa_k"), (xr, "ffn_maa_r")):
                for eb in range(EB):
                    last = nc.vector.scalar_tensor_tensor(bl(dst[:, eb, :]), bl(sx[:, eb, :]), v(name, eb), xa[:, eb, :, 1:L1 + 1], ALU.mult, ALU.add)
            last.then_inc(s["xk"], 1)
            dve.wait_ge(s["th2"], n + 1)
            dve.wait_ge(s["fvp"], n + 1)
            for i in range(2):
                last = nc.vector.scalar_tensor_tensor(y[:, 2 * i:2 * i + 2, :].rearrange("p b e -> p (b e)"), th2[:, 2 * i:2 * i + 2, :].rearrange("p b e -> p (b e)"),
                                                      1.0, pb[6 + i][:, :], ALU.add, ALU.mult).then_inc(s["y"], 1)
            dve.wait_ge(s["y"], n * 2 + 2)
            nc.vector.scalar_tensor_tensor(out_t.rearrange("p b e -> p (b e)"), y.rearrange("p b e -> p (b e)"), 0.5,
                                           x1[:, :, :].rearrange("p b e -> p (b e)"), ALU.mult, ALU.add).then_inc(s["fin"], 1)
        groups(dve, run)

    return {"tensor": tensor, "scalar": scalar, "vector": vector, "gpsimd": gpsimd, "sync": sync}


def program(nc, W):
    persistent = ExitStack()
    with persistent:
        sem = lambda name: persistent.enter_context(nc.semaphore(name))
        sb = lambda name, shape, dt: persistent.enter_context(nc.sbuf_tensor(name, shape, dt))
        env = {"sem": sem, "in": W, "sb": sb}
        env["pb"] = [persistent.enter_context(nc.psum_tensor(f"bank{i}", [128, 512], F32)) for i in range(8)]
        env["dram"] = {
            "stack": nc.dram_tensor("stack_scratch", [SLOTS, 2, 128, NTERM, T], BF16).ap(),
            "q": nc.dram_tensor("q_scratch", [NB, C, T], F32).ap(),
            "raw": nc.dram_tensor("raw_scratch", [NB, 128, 4, T], F32).ap(),
            "rden": nc.dram_tensor("rden_scratch", [NB, 4, D0, 4, T], F32).ap(),
            "x1": nc.dram_tensor("x1_scratch", [NB, C, T], F32).ap(),
            "v": nc.dram_tensor("v_scratch", [EB, 128, GB * L1], F32).ap(),
        }
        ident, ident_b = sb("ident", [128, 128], F32), sb("ident_b", [128, 128], BF16)
        half, epst = sb("minus_half", [128, 128], F32), sb("eps", [128, 16], F32)
        zero = sb("zero", [128, 1, 1], F32)
        env.update(ident=ident, ident_b=ident_b, half=half, epst=epst, zero=zero)
        shapes = {
            "f_wo": [128, C], "f_w1": [128, 2 * C], "f_w2": [128, F0, C], "f_vec": [128, 3 + F0],
            "g_vec": [128, EB, len(VECS)], "g_maa1": [128, EB, NMIX * DM], "g_maa2": [128, E1], "g_maa2b": [DM, E1],
            "g_td1": [128, EB, DD], "g_td2": [DD, E1], "g_esum": [128, S1, 128], "g_blk": [128, 128], "g_cmat": [128, 128],
            "g_blkh": [128, 16], "g_hsel": [H1, EB, 128],
        }
        for name, shape in shapes.items():
            env[name] = sb(name, shape, F32)
        env["g_w"] = {name: sb("g_" + name, [128, EB, E1], F32) for name in MATS}
        env["g_hvec"] = sb("g_hvec", [128, EB, 2], F32)
        loads = [(env[name], W[name]) for name in shapes] + [(env["g_w"][name], W["g_" + name]) for name in MATS]
        weights_in, consts_in, const_set, hvec_set = sem("weights_in"), sem("consts_in"), sem("const_set"), sem("hvec_set")
        ident_cast = sem("ident_cast")
        env.update(consts_in=consts_in, const_set=const_set, nconst=16 * 10, nset=4 * SLOTS + 3)
        phases = []
        for phase in (attention, feed_forward, recurrent):
            with ExitStack() as arena:
                env["sb"] = lambda name, shape, dt: arena.enter_context(nc.sbuf_tensor(name, shape, dt))
                phases.append(phase(nc, env))
        block = persistent.enter_context(nc.Block())

        @block.sync
        def _(sp):
            sp.dma_start(ident[:, :], W["ident"]).then_inc(consts_in, 16)
            phases[0]["tables"](sp)
            for tile, src in loads:
                sp.dma_start(tile[tuple(slice(None) for _ in tile.shape)], src).then_inc(weights_in, 16)
            for phase in phases:
                phase["sync"](sp)

        @block.gpsimd
        def _(pool):
            nc.gpsimd.memset(half[:, :], -0.5).then_inc(const_set, 1)
            nc.gpsimd.memset(epst[:, :], EPS).then_inc(const_set, 1)
            nc.gpsimd.memset(zero[:, :, :], 0.0).then_inc(const_set, 1)
            phases[0]["set"](pool, 3)
            for phase in phases:
                phase["gpsimd"](pool)

        @block.tensor
        def _(pe):
            pe.wait_ge(consts_in, env["nconst"])
            pe.wait_ge(ident_cast, 1)
            phases[0]["tensor"](pe)
            pe.wait_ge(weights_in, 16 * len(loads))
            phases[1]["tensor"](pe)
            phases[2]["tensor"](pe)

        @block.scalar
        def _(act):
            act.wait_ge(consts_in, env["nconst"])
            phases[0]["scalar"](act)
            act.wait_ge(weights_in, 16 * len(loads))
            act.wait_ge(hvec_set, 1)
            phases[1]["scalar"](act)
            phases[2]["scalar"](act)

        @block.vector
        def _(dve):
            dve.wait_ge(consts_in, env["nconst"])
            nc.vector.tensor_copy(ident_b[:, :], ident[:, :]).then_inc(ident_cast, 1)
            phases[0]["vector"](dve)
            dve.wait_ge(weights_in, 16 * len(loads))
            i = VECS.index("gn_w")
            nc.vector.tensor_scalar(env["g_hvec"][:, :, :], env["g_vec"][:, :, i:i + 2], 0.5, None, ALU.mult).then_inc(hvec_set, 1)
            phases[1]["vector"](dve)
            phases[2]["vector"](dve)


MATS = ("Wk", "Wv", "Wr", "Wg", "Wo", "Wfk", "Wfr", "Wfv")


def arrays_for(inputs):
    a = {k: np.asarray(v) for k, v in inputs.items()}
    p0, p1 = "L0_xattn_", "L1_xattn_"
    out = {k: a[k] for k in (p0 + "Wq", p0 + "Wk", p0 + "Wv", p0 + "ln_q_g", p0 + "ln_q_b", p0 + "ln_kv_g", p0 + "ln_kv_b")}
    x, ctx = a["x"], a["ctx_2048"]
    out["x_ctx"] = np.stack([x, ctx], axis=2)
    pos = np.arange(T, dtype=np.float32)[:, None]
    ang = pos * np.exp(np.arange(0, C, 2, dtype=np.float32) * np.float32(-math.log(10000.0) / C))
    table = np.zeros((T, C), np.float32)
    table[:, 0::2], table[:, 1::2] = np.sin(ang), np.cos(ang)
    out["pos"] = np.ascontiguousarray(table.T)
    out["ident"] = np.eye(128, dtype=np.float32)
    rows = [(2 * g + j % 2 + NTILE * (j // 2)) * D0 + d for j in range(4) for d in range(D0) for g in range(4)]
    out["f_wo"] = a[p0 + "Wo"][rows]
    out["f_w1"] = a[p0 + "W1"]
    out["f_w2"] = np.ascontiguousarray(a[p0 + "W2"].reshape(F0, 128, C).transpose(1, 0, 2))
    out["f_vec"] = np.stack([a[p0 + "ffn_ln_g"], a[p0 + "ffn_ln_b"], a[p0 + "b2"], *a[p0 + "b1"].reshape(F0, 128)], axis=1)

    def halves(m):
        return np.ascontiguousarray(m.reshape(EB, 128, -1).transpose(1, 0, 2))
    vecs = {n: a[p1 + n] for n in VECS if p1 + n in a}
    vecs["u"] = a[p1 + "u"].reshape(E1)
    vecs.update({f"stack{f}": a[p1 + "maa_stack"][0, f] for f in range(NMIX)})
    out["g_vec"] = halves(np.stack([vecs[n] for n in VECS], axis=1))
    out["g_maa1"] = halves(a[p1 + "maa_w1"])
    out["g_maa2"] = a[p1 + "maa_w2"][0:4].reshape(128, E1)
    out["g_maa2b"] = a[p1 + "maa_w2"][4]
    out["g_td1"], out["g_td2"] = halves(a[p1 + "td_w1"]), a[p1 + "td_w2"]
    for n in MATS:
        out["g_" + n] = halves(a[p1 + n].T)
    r = np.arange(128)
    same = r[:, None] // S1 == r[None, :] // S1
    out["g_esum"] = np.stack([(same & (r[None, :] % S1 == j)) for j in range(S1)], axis=1).astype(np.float32)
    out["g_blk"] = same.astype(np.float32)
    out["g_cmat"] = (np.eye(128) - same / S1).astype(np.float32)
    out["g_blkh"] = ((r[:, None] // S1 == np.arange(16)[None, :]) / S1).astype(np.float32)
    heads = np.arange(H1)[:, None, None] == (np.arange(EB)[None, :, None] * 16 + r[None, None, :] // S1)
    out["g_hsel"] = heads.astype(np.float32)
    out["st"] = np.ascontiguousarray(ctx[:, 0:2].reshape(NG, GB, 2, EB, 128).transpose(0, 4, 3, 2, 1).reshape(NG, 128, -1))
    out["s0"] = np.ascontiguousarray(ctx[:, 2:2 + S1].reshape(NG, GB, EB, 128, S1).transpose(0, 3, 2, 4, 1).reshape(NG, 128, -1))
    return {k: np.ascontiguousarray(v) for k, v in out.items()}


def kernel(**inputs):
    import concourse.bacc as bacc
    from concourse.bass_utils import run_bass_kernel_spmd

    nc = bacc.Bacc("TRN2", target_bir_lowering=False, num_devices=1)
    arrays = {"in_" + k: v for k, v in arrays_for(inputs).items()}
    W = {k[3:]: nc.dram_tensor(k, v.shape, mybir.dt.from_np(v.dtype), kind="ExternalInput").ap() for k, v in arrays.items()}
    W["out"] = nc.dram_tensor("result", (NB, L1, E1), F32, kind="ExternalOutput").ap()
    program(nc, W)
    r = run_bass_kernel_spmd(nc, [arrays], core_ids=[0])
    return r.results[0]["result"]
```

```python
import math
import numpy as np
import concourse.bass as bass
from concourse import mybir
from contextlib import ExitStack

F32 = mybir.dt.float32
BF16 = mybir.dt.bfloat16
ACT = mybir.ActivationFunctionType
ALU = mybir.AluOpType
AX_X = mybir.AxisListType.X

NB, C, T = 16, 128, 256
H0, D0 = 16, 8
NQB = T // 128
EPS = 1e-5

NPART = 3
NTERM = 6
ROWS = D0 * NTERM
NTILE = H0 // 2
SROWS = 64 + ROWS
MROWS = 2
UNITS = 16
PV_LAG = 2
NPROB = 8
LAG = 8
SLOTS = 4


class Turn:

    def __init__(self, it, c):
        self.n = it * SLOTS + c
        self.slot = c % SLOTS
        self.use = it + c // SLOTS


def need(engine, sem, value):
    if isinstance(value, int) and value <= 0:
        return
    engine.wait_ge(sem, value)


def attention(nc, env):
    sb, pb, sem, W = env["sb"], env["pb"], env["sem"], env["in"]
    scr = env["dram"]

    xin = [sb(f"xin{s}", [128, 2, T], F32) for s in range(2)] * 2
    xpe = [sb(f"xpe{s}", [128, 2, T], F32) for s in range(2)] * 2
    pe_tab = sb("pe_tab", [128, 2, T], F32)
    wq, wk, wv = sb("wq", [128, 128], F32), sb("wk", [128, 128], F32), sb("wv", [128, 128], F32)
    lnc = sb("ln_consts", [128, 4], F32)
    stats = sb("stats", [128, 4, 6], F32)
    mv = sb("mv", [128, 4, 2], F32)
    rstd = sb("rstd", [128, 4], F32)
    xn = sb("xn", [128, 4, 128], F32)
    qkvT = [sb(f"qkvT{s}", [128, 2, T], F32) for s in range(2)] * 2
    parts = [sb(f"parts{s}", [128, 2, NPART, T], BF16) for s in range(2)] * 2
    rest = sb("rest", [128, 2, T], F32)
    KS = [sb(f"KS{s}", [128, NTILE, T], BF16) for s in range(SLOTS)]
    QS = [sb(f"QS{s}", [128, 2, NTILE, T], BF16) for s in range(SLOTS)]
    VA = [sb(f"VA{s}", [128, NQB, H0, 32], F32) for s in range(SLOTS)]
    mx = sb("mx", [128, NQB, H0], F32)
    mparts = sb("mparts", [128, NQB, MROWS, H0], BF16)
    mT = [sb(f"mT{s}", [32, T], BF16) for s in range(2)] * 2
    prob = [sb(f"prob{s}", [128, 2, T], F32) for s in range(NPROB)]
    raw = [sb(f"raw{s}", [128, 4, T], F32) for s in range(2)] * 2
    ident, ident_b, half, epst, zero = env["ident"], env["ident_b"], env["half"], env["epst"], env["zero"]

    SM, SC, VB = pb[0:2], pb[2:4], pb[4:6]
    M0, M1 = pb[6], pb[7]
    m0 = M0[:, :].rearrange("p (a t) -> p a t", a=4)
    m1 = M1[:, :].rearrange("p (a t) -> p a t", a=4)
    m1b = M1[:, 0:128].bitcast(BF16)

    consts_in, const_set = env["consts_in"], env["const_set"]
    NCONST = env["nconst"]
    va_zero, va_set, stack_set = sem("va_zero"), sem("va_set"), sem("stack_set")
    x_in = [sem(f"x_in{s}") for s in range(SLOTS)]
    pos_added = sem("pos_added")
    tokens_ready = sem("tokens_ready")
    stats_done, aggr_done, var_done = sem("stats_done"), sem("aggr_done"), sem("var_done")
    rstd_ready, normed = sem("rstd_ready"), sem("normed")
    channels_ready, qkvT_ready = sem("channels_ready"), sem("qkvT_ready")
    qk_ready, v_ready = sem("qk_ready"), sem("v_ready")
    part1_done, rest_done, part2_done, part3_done = sem("part1_done"), sem("rest_done"), sem("part2_done"), sem("part3_done")
    va_ready = sem("va_ready")
    q_kept = [sem(f"q_kept{s}") for s in range(SLOTS)]
    stack_out = [sem(f"stack_out{s}") for s in range(SLOTS)]
    stack_in = [sem(f"stack_in{s}") for s in range(SLOTS)]
    m_in = [sem(f"m_in{s}") for s in range(SLOTS)]
    raw_out = [sem(f"raw_out{s}") for s in range(SLOTS)]
    smax_ready, max_done = sem("smax_ready"), sem("max_done")
    mhigh_done, mparts_ready, mT_psum, mT_ready = sem("mhigh_done"), sem("mparts_ready"), sem("mT_psum"), sem("mT_ready")
    scores_ready, exp_done, pv_done, raw_ready = sem("scores_ready"), sem("exp_done"), sem("pv_done"), sem("raw_ready")

    STACK_OUT, STACK_IN, M_IN, RAW_OUT = 6 * 16, 4 * 16, MROWS * 16, 16

    def in_range(v, c_off, static):
        return not static or 0 <= v + c_off < NB

    def plan(it, c, static):
        def turn(off):
            return Turn(it, c + off) if in_range(c, off, static) else None
        return {"x": turn(2), "a": turn(2), "l": turn(1), "b": turn(0), "h": turn(-1), "t": turn(-2)}

    def stream(p, s):
        return (p["t"], s + UNITS - LAG) if s < LAG else (p["h"], s - LAG)

    def iterations(engine, run):
        for v in range(-2, 2):
            run(plan(0, v, True))
        with engine.Fori(0, 3) as it:
            for c in range(2, 2 + SLOTS):
                run(plan(it, c, False))
        for v in range(14, 18):
            run(plan(0, v, True))

    def unit(u):
        return u // 8, (u % 8) // 2, u % 2

    def cunit(u):
        return (u % 4) // 2, u // 4, u % 2

    def tensor(pe):
        def run(p):
            for s in range(UNITS):
                if p["b"]:
                    b = p["b"]
                    if s == 0:
                        pe.wait_ge(stack_in[b.slot], b.use * STACK_IN + STACK_IN)
                    qb, tp, hh = unit(s)
                    need(pe, max_done, b.n * UNITS + s - 1)
                    for a in range(2):
                        last = nc.tensor.matmul(SM[hh][:, a * T:(a + 1) * T], QS[b.slot][0:SROWS, hh, 2 * tp + a, qb * 128:(qb + 1) * 128],
                                                KS[b.slot][0:SROWS, 2 * tp + a, :], start=True, stop=True)
                    last.then_inc(smax_ready, 1)
                cur, u = stream(p, s)
                if cur:
                    kb, tp, hh = cunit(u)
                    if u == 0:
                        pe.wait_ge(m_in[cur.slot], cur.use * M_IN + M_IN)
                    need(pe, exp_done, cur.n * UNITS + u - 1)
                    for a in range(2):
                        last = nc.tensor.matmul(SC[hh][:, a * T:(a + 1) * T], KS[cur.slot][0:SROWS + MROWS, 2 * tp + a, kb * 128:(kb + 1) * 128],
                                                QS[cur.slot][0:SROWS + MROWS, hh, 2 * tp + a, :], start=True, stop=True)
                    last.then_inc(scores_ready, 1)
                prev, u = stream(p, s - PV_LAG)
                if prev and u % 2 == 1:
                    kb, tp, _ = cunit(u)
                    if u == 1:
                        pe.wait_ge(va_ready, prev.n + 1)
                    if u % 8 == 1:
                        need(pe, raw_ready, prev.n * 2 - 1 + u // 8)
                    pe.wait_ge(exp_done, prev.n * UNITS + u + 1)
                    for j in range(4):
                        hh, a = j // 2, j % 2
                        last = nc.tensor.matmul(VB[tp // 2][32 * j:32 * j + 32, (tp % 2) * T:(tp % 2 + 1) * T],
                                                VA[prev.slot][:, kb, 2 * tp + a + NTILE * hh, :], prob[(u - 1 + hh) % NPROB][:, a, :],
                                                start=(kb == 0), stop=(kb == 1))
                    last.then_inc(pv_done, 2)
                a_ = p["a"]
                if s == 4 and a_:
                    pe.wait_ge(pos_added, a_.n + 1)
                    need(pe, rest_done, a_.n)
                    for j in range(4):
                        last = nc.tensor.transpose(m0[:, j, :], xpe[a_.slot][:, j // 2, (j % 2) * 128:(j % 2 + 1) * 128], ident[:, :])
                    last.then_inc(tokens_ready, 1)
                if s == 2 and p["h"]:
                    h = p["h"]
                    pe.wait_ge(mparts_ready, h.n + 1)
                    need(pe, va_ready, h.n + (3 if p["l"] else 2 if p["b"] else 1))
                    for qb in range(NQB):
                        last = nc.tensor.transpose(m1b[0:32, qb * 128:(qb + 1) * 128], mparts[:, qb, :, :], ident_b[:, :])
                    last.then_inc(mT_psum, 1)
                if s == 8 and a_:
                    pe.wait_ge(normed, a_.n + 1)
                    need(pe, mT_ready, a_.n - 2)
                    need(pe, va_ready, a_.n)
                    for j in range(4):
                        last = nc.tensor.transpose(m1[:, j, :], xn[:, j, :], ident[:, :])
                    last.then_inc(channels_ready, 1)
                if s == 10 and a_:
                    pe.wait_ge(qkvT_ready, a_.n + 1)
                    src = qkvT[a_.slot]
                    nc.tensor.matmul(M0[:, 0:T], wq[:, :], src[:, 0, :], start=True, stop=True)
                    nc.tensor.matmul(M0[:, T:2 * T], wk[:, :], src[:, 1, :], start=True, stop=True).then_inc(qk_ready, 1)
                    for kb in range(NQB):
                        last = nc.tensor.matmul(M1[:, kb * 128:(kb + 1) * 128], src[:, 1, kb * 128:(kb + 1) * 128], wv[:, :],
                                                start=True, stop=True)
                    last.then_inc(v_ready, 1)
        iterations(pe, run)

    def scalar(act):
        def run(p):
            if p["x"]:
                x = p["x"]
                need(act, pos_added, x.n - 1)
                act.dma_start(xin[x.slot][:, :, :], W["x_ctx"][bass.ds(x.n, 1), :, :, :].rearrange("o c w t -> (o c) w t")).then_inc(x_in[x.slot], 16)
            for s in range(UNITS):
                cur, u = stream(p, s)
                if cur:
                    act.wait_ge(scores_ready, cur.n * UNITS + u + 1)
                    need(act, pv_done, cur.n * UNITS + u - NPROB + 1 + u % 2)
                    nc.scalar.activation(prob[u % NPROB][:, :, :].rearrange("p a t -> p (a t)"), SC[u % 2][:, :], ACT.Exp,
                                         scale=1.0 / math.sqrt(D0)).then_inc(exp_done, 1)
                if s in (PV_LAG, LAG + PV_LAG) and p["t"]:
                    t, half_ = p["t"], s // LAG
                    act.wait_ge(pv_done, t.n * UNITS + 8 * half_ + 8)
                    if half_ == 0:
                        need(act, raw_out[(t.slot + 2) % SLOTS], (t.use + (t.slot + 2) // SLOTS) * RAW_OUT)
                    nc.scalar.activation(raw[t.slot][:, 2 * half_:2 * half_ + 2, :].rearrange("p a t -> p (a t)"), VB[half_][:, :],
                                         ACT.Copy).then_inc(raw_ready, 1)
                if s == 3 and p["h"]:
                    h = p["h"]
                    act.wait_ge(mT_psum, h.n + 1)
                    need(act, m_in[(h.slot + 2) % SLOTS], (h.use + (h.slot + 2) // SLOTS) * M_IN)
                    nc.scalar.activation(mT[h.slot][:, :], m1b[0:32, :], ACT.Copy).then_inc(mT_ready, 1)
                if s == 4 and p["h"]:
                    h = p["h"]
                    act.wait_ge(mT_ready, h.n + 1)
                    for part in range(MROWS):
                        row = SROWS + part
                        act.dma_start(QS[h.slot][row:row + 1, :, :, :].rearrange("o h t q -> o (h t q)"),
                                      mT[h.slot][H0 * part:H0 * part + H0, :]).then_inc(m_in[h.slot], 16)
                a = p["a"]
                if s == 9 and a:
                    act.wait_ge(channels_ready, a.n + 1)
                    if isinstance(a.n, int) and a.n == 0:
                        act.wait_ge(consts_in, NCONST)
                    need(act, q_kept[(a.slot + 2) % SLOTS], (a.use + (a.slot + 2) // SLOTS) * 16)
                    for w in range(2):
                        last = nc.scalar.activation(qkvT[a.slot][:, w, :], M1[:, w * T:(w + 1) * T], ACT.Identity,
                                                    bias=lnc[:, 2 * w + 1:2 * w + 2], scale=lnc[:, 2 * w:2 * w + 1])
                    last.then_inc(qkvT_ready, 1)
                if s == 11 and a:
                    act.wait_ge(qk_ready, a.n + 1)
                    need(act, stack_out[(a.slot + 2) % SLOTS], (a.use + (a.slot + 2) // SLOTS) * STACK_OUT)
                    nc.scalar.activation(parts[a.slot][:, :, 0, :], M0[:, :].rearrange("p (w t) -> p w t", w=2),
                                         ACT.Copy).then_inc(part1_done, 1)
                if s == 12 and a:
                    act.wait_ge(v_ready, a.n + 1)
                    if isinstance(a.n, int) and a.n < SLOTS:
                        act.wait_ge(va_set, SLOTS)
                    need(act, pv_done, a.n * UNITS - (SLOTS - 1) * UNITS)
                    nc.scalar.activation(VA[a.slot][:, :, :, 0:D0], M1[:, 0:T].rearrange("p (k h d) -> p k h d", k=NQB, h=H0),
                                         ACT.Copy).then_inc(va_ready, 1)
        iterations(act, run)

    def vector(dve):
        def run(p):
            for s in range(UNITS):
                a = p["a"]
                if s == 6 and a:
                    dve.wait_ge(stats_done, a.n + 1)
                    need(dve, rstd_ready, a.n)
                    need(dve, normed, a.n)
                if p["b"]:
                    b = p["b"]
                    qb, tp, hh = unit(s)
                    dve.wait_ge(smax_ready, b.n * UNITS + s + 1)
                    if s == 0:
                        need(dve, mparts_ready, b.n)
                    nc.vector.tensor_reduce(mx[:, qb, NTILE * hh + 2 * tp:NTILE * hh + 2 * tp + 2], SM[hh][:, :].rearrange("p (a t) -> p a t", a=2),
                                            AX_X, ALU.max, negate=True).then_inc(max_done, 1)
                if s == 5 and a:
                    dve.wait_ge(tokens_ready, a.n + 1)
                    need(dve, aggr_done, a.n)
                    for j in range(4):
                        last = nc.vector.bn_stats(stats[:, j, :], m0[:, j, :])
                    last.then_inc(stats_done, 1)
                if s == 6 and a:
                    for j in range(4):
                        last = nc.vector.bn_aggr(mv[:, j, :], stats[:, j, :])
                    last.then_inc(aggr_done, 1)
                if s == 7 and a:
                    dve.wait_ge(rstd_ready, a.n + 1)
                    need(dve, channels_ready, a.n)
                    for j in range(4):
                        last = nc.vector.tensor_scalar(xn[:, j, :], m0[:, j, :], mv[:, j, 0:1], rstd[:, j:j + 1], ALU.subtract, ALU.mult)
                    last.then_inc(normed, 1)
                if s == 12 and a:
                    dve.wait_ge(part1_done, a.n + 1)
                    need(dve, part3_done, a.n)
                    nc.vector.tensor_tensor(rest[:, :, :], M0[:, :].rearrange("p (w t) -> p w t", w=2),
                                            parts[a.slot][:, :, 0, :], ALU.subtract).then_inc(rest_done, 1)
                if s == UNITS - 1 and p["b"]:
                    b = p["b"]
                    dve.wait_ge(max_done, b.n * UNITS + UNITS)
                    need(dve, mT_psum, b.n)
                    nc.vector.tensor_copy(mparts[:, :, 0, :], mx[:, :, :]).then_inc(mhigh_done, 1)
                    dve.wait_ge(mhigh_done, b.n + 1)
                    nc.vector.tensor_tensor(mparts[:, :, 1, :], mx[:, :, :], mparts[:, :, 0, :], ALU.subtract).then_inc(mparts_ready, 1)
        iterations(dve, run)

    def gpsimd(pool):
        def run(p):
            a, x2 = p["a"], p["x"]
            if x2:
                pool.wait_ge(x_in[x2.slot], x2.use * 16 + 16)
                if isinstance(x2.n, int) and x2.n == 0:
                    pool.wait_ge(consts_in, NCONST)
                need(pool, tokens_ready, x2.n - 2)
                nc.gpsimd.tensor_tensor(xpe[x2.slot][:, :, :], xin[x2.slot][:, :, :], pe_tab[:, :, :], ALU.add).then_inc(pos_added, 1)
            if a:
                pool.wait_ge(aggr_done, a.n + 1)
                need(pool, normed, a.n)
                nc.gpsimd.tensor_tensor(rstd[:, :], mv[:, :, 1], epst[:, 0:4], ALU.add).then_inc(var_done, 1)
                pool.wait_ge(var_done, a.n + 1)
                nc.gpsimd.tensor_tensor(rstd[:, :], rstd[:, :], half[:, 0:4], ALU.pow).then_inc(rstd_ready, 1)
                pool.wait_ge(rest_done, a.n + 1)
                part = parts[a.slot]
                nc.gpsimd.tensor_tensor(part[:, :, 1, :], rest[:, :, :], zero[:, :, :].broadcast_to((128, 2, T)), ALU.add).then_inc(part2_done, 1)
                pool.wait_ge(part2_done, a.n + 1)
                nc.gpsimd.tensor_tensor(part[:, :, 2, :], rest[:, :, :], part[:, :, 1, :], ALU.subtract).then_inc(part3_done, 1)
        iterations(pool, run)

    def tables(sp):
        sp.dma_start(pe_tab[:, :, :], W["pos"].unsqueeze(1).broadcast_to((128, 2, T))).then_inc(consts_in, 16)
        for dst, src in ((wq, "L0_xattn_Wq"), (wk, "L0_xattn_Wk"), (wv, "L0_xattn_Wv")):
            sp.dma_start(dst[:, :], W[src]).then_inc(consts_in, 16)
        sp.dma_start(lnc[:, :], W["ln"]).then_inc(consts_in, 16)

    def sync(sp):
        def run(p):
            a, t, l = p["a"], p["t"], p["l"]
            raw_dst = scr["raw"][bass.ds(t.n, 1), :, :, :].rearrange("o p g q -> (o p) g q") if t else None
            q_dst = scr["q"][bass.ds(a.n, 1), :, :].rearrange("o c t -> (o c) t") if a else None
            if l:
                sp.wait_ge(stack_out[l.slot], l.use * STACK_OUT + STACK_OUT)
                need(sp, scores_ready, l.n * UNITS - (SLOTS - 1) * UNITS)
                if isinstance(l.n, int) and l.n < SLOTS:
                    sp.wait_ge(stack_set, l.n + 1)
                for w in range(2):
                    view = scr["stack"][l.slot, w].rearrange("(hh t d) m q -> hh (d m) t q", hh=2, d=D0)
                    for hh in range(2):
                        rows = slice(64 * hh, 64 * hh + ROWS)
                        dst = KS[l.slot][rows, :, :] if w else QS[l.slot][rows, hh, :, :]
                        sp.dma_start(dst, view[hh]).then_inc(stack_in[l.slot], 16)
            if t:
                sp.wait_ge(raw_ready, t.n * 2 + 2)
                sp.dma_start(raw_dst, raw[t.slot][:, :, :]).then_inc(raw_out[t.slot], 16)
            if a:
                sp.wait_ge(qkvT_ready, a.n + 1)
                sp.dma_start(q_dst, qkvT[a.slot][:, 0, :]).then_inc(q_kept[a.slot], 16)
                sp.wait_ge(part3_done, a.n + 1)
                need(sp, stack_in[a.slot], a.use * STACK_IN)
                dst, part = scr["stack"][a.slot], parts[a.slot]
                for w, m, n, p0 in ((0, 0, 3, 0), (0, 3, 2, 1), (0, 5, 1, 2), (1, 0, 3, None), (1, 3, 2, None), (1, 5, 1, None)):
                    src = part[:, w, 0:n, :] if p0 is None else part[:, w, p0:p0 + 1, :].broadcast_to((128, n, T))
                    sp.dma_start(dst[w, :, m:m + n, :], src).then_inc(stack_out[a.slot], 16)
        iterations(sp, run)
        for s in range(SLOTS):
            uses = (NB - s + SLOTS - 1) // SLOTS
            sp.wait_ge(raw_out[s], uses * RAW_OUT)
            sp.wait_ge(q_kept[s], uses * 16)

    def clear(dve):
        for k in range(SLOTS):
            nc.vector.memset(QS[k][:, :, :, :], 0.0)
            nc.vector.memset(KS[k][:, :, :], 1.0).then_inc(stack_set, 1)
            nc.vector.memset(VA[k][:, :, :, :], 0.0).then_inc(va_zero, 1)
        dve.wait_ge(va_zero, SLOTS)
        for k in range(SLOTS):
            nc.vector.memset(VA[k][:, :, :, D0:D0 + 1], 1.0).then_inc(va_set, 1)

    return {"tensor": tensor, "scalar": scalar, "vector": vector, "gpsimd": gpsimd, "sync": sync, "clear": clear, "tables": tables}


FP = 2
NPAIR = NB // FP
F0 = 2 * C // 128


class Pair:

    def __init__(self, it, c):
        self.n = it * 2 + c
        self.slot = c % 2
        self.use = it + c // 2


def feed_forward(nc, env):
    sb, pb, sem, W, scr = env["sb"], env["pb"], env["sem"], env["in"], env["dram"]
    ident, half, epst = env["ident"], env["half"], env["epst"]
    wo, w1, w2, fvec = env["f_wo"], env["f_w1"], env["f_w2"], env["f_vec"]

    den = sb("den", [128, 512], F32)
    ctx_t = [sb(f"f_ctx{s}", [128, FP, T], F32) for s in range(2)]
    rden = [sb(f"f_rden{s}", [128, FP, T], F32) for s in range(2)]
    q_t = [sb(f"f_q{s}", [128, FP, T], F32) for s in range(2)]
    cn = [sb(f"f_cn{s}", [128, FP * T], F32) for s in range(2)]
    xn = sb("f_xn", [128, 4, 128], F32)
    hT = [sb(f"f_h{s}", [128, FP * T], F32) for s in range(2)]
    ge = [sb(f"f_ge{s}", [128, F0, FP * T], F32) for s in range(2)]
    o = [sb(f"f_o{s}", [128, FP, T], F32) for s in range(2)]
    r = [sb(f"f_res{s}", [128, FP * T], F32) for s in range(2)]
    rk = [sb(f"f_resk{s}", [128, FP * T], F32) for s in range(2)]
    stats, mv, rstd = sb("f_stats", [128, 4, 6], F32), sb("f_mv", [128, 4, 2], F32), sb("f_rstd", [128, 4], F32)
    Y, T1, T2, FF, O = pb[0], pb[1], pb[2], pb[3:5], pb[5]
    t1, t2 = (b[:, :].rearrange("p (a t) -> p a t", a=4) for b in (T1, T2))

    den_in, den_done, den_out = sem("den_in"), sem("den_done"), sem("den_out")
    f_in = [sem(f"f_in{s}") for s in range(2)]
    f_kept = [sem(f"f_kept{s}") for s in range(2)]
    f_ctx, f_y, f_r, f_tok = sem("f_ctx_ready"), sem("f_y_ready"), sem("f_r_ready"), sem("f_tokens_ready")
    f_stats, f_aggr, f_var, f_rstd = sem("f_stats_done"), sem("f_aggr_done"), sem("f_var_done"), sem("f_rstd_ready")
    f_normed, f_chan, f_h = sem("f_normed"), sem("f_channels_ready"), sem("f_h_ready")
    f_hid, f_ge, f_ff, f_out, f_rk = sem("f_hidden_ready"), sem("f_gelu_ready"), sem("f_ff_ready"), sem("f_out_ready"), sem("f_r_biased")
    IN = 6 * 16

    def plan(it, c, static):
        def pair(off):
            return Pair(it, c + off) if not static or 0 <= c + off < NPAIR else None
        return pair(0), pair(-1), pair(-2)

    def iterations(engine, run):
        for v in (0, 1):
            run(*plan(0, v, True))
        with engine.Fori(1, NPAIR // 2) as it:
            for c in (0, 1):
                run(*plan(it, c, False))
        for v in (NPAIR, NPAIR + 1):
            run(*plan(0, v, True))

    def sync(sp):
        for g2 in range(2):
            src = scr["raw"].rearrange("b (j r) g q -> (b j) r g q", j=4)[:, D0, 2 * g2:2 * g2 + 2, :]
            sp.dma_start(den[64 * g2:64 * g2 + 64, :].rearrange("p (g q) -> p g q", g=2), src).then_inc(den_in, 16)
        sp.wait_ge(den_done, 1)
        view = scr["rden"].rearrange("b j d (h g) q -> h (b j) d (g q)", h=2)
        for g2 in range(2):
            sp.dma_start(view[g2], den[64 * g2:64 * g2 + 64, :].unsqueeze(1).broadcast_to((64, D0, 512))).then_inc(den_out, 16)
        sp.wait_ge(den_out, 32)

        def run(a, b, c):
            if a:
                need(sp, f_ctx, a.n - 1)
                need(sp, f_r, a.n - 1)
                raw = scr["raw"][bass.ds(a.n * 2, 2), :, :, :].rearrange("b (j r) g q -> j r g b q", j=4)
                for j in range(4):
                    sp.dma_start(ctx_t[a.slot][32 * j:32 * j + 32, :, :], raw[j, 0:D0].rearrange("r g b q -> (r g) b q")).then_inc(f_in[a.slot], 16)
                sp.dma_start(rden[a.slot][:, :, :], scr["rden"][bass.ds(a.n * 2, 2)].rearrange("b j d g q -> (j d g) b q")).then_inc(f_in[a.slot], 16)
                sp.dma_start(q_t[a.slot][:, :, :], scr["q"][bass.ds(a.n * 2, 2), :, :].rearrange("b c q -> c b q")).then_inc(f_in[a.slot], 16)
        iterations(sp, run)
        for s in range(2):
            sp.wait_ge(f_kept[s], NPAIR // 2 * 16)

    def gpsimd(pool):
        def run(a, b, c):
            if a:
                pool.wait_ge(f_in[a.slot], a.use * IN + IN)
                need(pool, f_y, a.n - 1)
                nc.gpsimd.tensor_tensor(cn[a.slot][:, :], ctx_t[a.slot][:, :, :].rearrange("p b q -> p (b q)"),
                                        rden[a.slot][:, :, :].rearrange("p b q -> p (b q)"), ALU.mult).then_inc(f_ctx, 1)
                pool.wait_ge(f_aggr, a.n + 1)
                nc.gpsimd.tensor_tensor(rstd[:, :], mv[:, :, 1], epst[:, 0:4], ALU.add).then_inc(f_var, 1)
                pool.wait_ge(f_var, a.n + 1)
                nc.gpsimd.tensor_tensor(rstd[:, :], rstd[:, :], half[:, 0:4], ALU.pow).then_inc(f_rstd, 1)
        iterations(pool, run)

    def tensor(pe):
        def run(a, b, c):
            if a:
                pe.wait_ge(f_ctx, a.n + 1)
                need(pe, f_r, a.n)
                nc.tensor.matmul(Y[:, :], wo[:, :], cn[a.slot][:, :], start=True, stop=True).then_inc(f_y, 1)
            if c:
                pe.wait_ge(f_ge, c.n + 1)
                need(pe, f_out, c.n)
                for f in range(F0):
                    last = nc.tensor.matmul(O[:, :], w2[:, f, :], ge[c.slot][:, f, :], start=(f == 0), stop=(f == F0 - 1))
                last.then_inc(f_ff, 1)
            if b:
                pe.wait_ge(f_normed, b.n + 1)
                need(pe, f_h, b.n)
                for j in range(4):
                    last = nc.tensor.transpose(t2[:, j, :], xn[:, j, :], ident[:, :])
                last.then_inc(f_chan, 1)
            if a:
                pe.wait_ge(f_r, a.n + 1)
                for j in range(4):
                    last = nc.tensor.transpose(t1[:, j, :], r[a.slot][:, j * 128:(j + 1) * 128], ident[:, :])
                last.then_inc(f_tok, 1)
            if b:
                pe.wait_ge(f_h, b.n + 1)
                need(pe, f_ge, b.n)
                for f in range(F0):
                    last = nc.tensor.matmul(FF[f][:, :], w1[:, f * 128:(f + 1) * 128], hT[b.slot][:, :], start=True, stop=True)
                last.then_inc(f_hid, 1)
        iterations(pe, run)

    def scalar(act):
        def run(a, b, c):
            if b:
                act.wait_ge(f_chan, b.n + 1)
                nc.scalar.activation(hT[b.slot][:, :], T2[:, :], ACT.Identity, bias=fvec[:, 1:2], scale=fvec[:, 0:1]).then_inc(f_h, 1)
            if c:
                act.wait_ge(f_out, c.n + 1)
                act.dma_start(scr["x1"][bass.ds(c.n * 2, 2), :, :].rearrange("b c q -> c b q"), o[c.slot][:, :, :]).then_inc(f_kept[c.slot], 16)
            if b:
                act.wait_ge(f_hid, b.n + 1)
                need(act, f_ff, b.n - 1)
                for f in range(F0):
                    last = nc.scalar.activation(ge[b.slot][:, f, :], FF[f][:, :], ACT.Gelu, bias=fvec[:, 3 + f:4 + f])
                last.then_inc(f_ge, 1)
        iterations(act, run)

    def vector(dve):
        dve.wait_ge(den_in, 32)
        nc.vector.reciprocal(den[:, :], den[:, :]).then_inc(den_done, 1)

        def run(a, b, c):
            if a:
                dve.wait_ge(f_y, a.n + 1)
                nc.vector.tensor_tensor(r[a.slot][:, :], Y[:, :], q_t[a.slot][:, :, :].rearrange("p b q -> p (b q)"), ALU.add).then_inc(f_r, 1)
            if c:
                dve.wait_ge(f_ff, c.n + 1)
                dve.wait_ge(f_rk, c.n + 1)
                need(dve, f_kept[c.slot], c.use * 16)
                nc.vector.tensor_tensor(o[c.slot][:, :, :].rearrange("p b q -> p (b q)"), O[:, :], rk[c.slot][:, :], ALU.add).then_inc(f_out, 1)
            if a:
                dve.wait_ge(f_tok, a.n + 1)
                for j in range(4):
                    last = nc.vector.bn_stats(stats[:, j, :], t1[:, j, :])
                last.then_inc(f_stats, 1)
                dve.wait_ge(f_stats, a.n + 1)
                need(dve, f_rstd, a.n)
                need(dve, f_normed, a.n)
                need(dve, f_out, a.n - 1)
                dve.wait_ge(f_r, a.n + 1)
                nc.vector.tensor_scalar(rk[a.slot][:, :], r[a.slot][:, :], fvec[:, 2:3], None, ALU.add).then_inc(f_rk, 1)
                for j in range(4):
                    last = nc.vector.bn_aggr(mv[:, j, :], stats[:, j, :])
                last.then_inc(f_aggr, 1)
                dve.wait_ge(f_rstd, a.n + 1)
                need(dve, f_chan, a.n)
                for j in range(4):
                    last = nc.vector.tensor_scalar(xn[:, j, :], t1[:, j, :], mv[:, j, 0:1], rstd[:, j:j + 1], ALU.subtract, ALU.mult)
                last.then_inc(f_normed, 1)
        iterations(dve, run)

    return {"tensor": tensor, "scalar": scalar, "vector": vector, "gpsimd": gpsimd, "sync": sync}


L1, E1, H1, S1 = 128, 256, 32, 8
EB = E1 // 128
GB = 2
NG = NB // GB
NMIX, DM, DD = 5, 32, 64
JH = 4
VECS = ("ln1_w", "ln1_b", "maa_x", "stack0", "stack1", "stack2", "stack3", "stack4", "time_decay", "u", "gn_w", "gn_b",
        "ln2_w", "ln2_b", "ffn_maa_k", "ffn_maa_r")
MIX_K, MIX_W, MIX_V, MIX_R, MIX_G = range(NMIX)
MIX_ORDER = (MIX_W, MIX_K, MIX_V, MIX_R, MIX_G)


def recurrent(nc, env):
    sb, pb, sem, W, scr = env["sb"], env["pb"], env["sem"], env["in"], env["dram"]
    ident, half, epst = env["ident"], env["half"], env["epst"]
    w, vec, hvec = env["g_w"], env["g_vec"], env["g_hvec"]
    maa1, maa2, maa2b, td1, td2 = env["g_maa1"], env["g_maa2"], env["g_maa2b"], env["g_td1"], env["g_td2"]
    hsel = env["g_hsel"]
    esum, blk, cmat, blkh = env["g_esum"], env["g_blk"], env["g_cmat"], env["g_blkh"]
    N = GB * L1

    def v(name, eb):
        return vec[:, eb, VECS.index(name):VECS.index(name) + 1]

    def t3(name):
        return sb(name, [128, EB, N], F32)

    def two(name):
        return [t3(f"{name}{i}") for i in range(2)]

    def bl(ap):
        return ap.rearrange("p (b l) -> p b l", b=GB)

    def cols(tile):
        return tile[:, :, :].rearrange("p a n -> p (a n)")

    x_in = [sb(f"g_xin{i}", [128, GB, E1], F32) for i in range(2)]
    st1 = [sb(f"g_st1_{i}", [128, EB, GB], F32) for i in range(2)]
    xn, sx = sb("g_xn", [128, GB, E1], F32), two("g_sx")
    xa = [sb(f"g_xa_{i}", [128, EB, GB, L1 + 1], F32) for i in range(2)]
    mixin = t3("g_mixin")
    th5, th5b = sb("g_th5", [128, N], F32), sb("g_th5b", [DM, N], F32)
    NZ = 4
    z = [sb(f"g_z{i}", [128, N], F32) for i in range(NZ)]
    xm = [two(f"g_xm{f}_") if f == MIX_G else [t3(f"g_xm{f}")] * 2 for f in range(NMIX)]
    tdh = sb("g_tdh", [DD, N], F32)
    ew = t3("g_ew")
    wS, kT, vT, rT = two("g_wS"), two("g_k"), two("g_v"), two("g_r")
    s0 = [sb(f"g_s0_{i}", [128, EB, S1, GB], F32) for i in range(2)]
    UN = [(hb, jq) for hb in range(EB) for jq in range(S1 // JH)]
    NU = len(UN)
    vbc = [sb(f"g_vbc{i}", [128, JH, N], F32) for i in range(NU)]
    aS = [sb(f"g_a{i}", [128, JH, N], F32) for i in range(2)]
    SS = [sb(f"g_S{i}", [128, JH, N], F32) for i in range(2)]
    gth, ruk = t3("g_gth"), t3("g_ruk")
    gs, og = two("g_gs"), two("g_og")
    xres = [sb(f"g_xres{i}", [128, GB, E1], F32) for i in range(2)]
    st0 = [sb(f"g_st0_{i}", [128, EB, GB], F32) for i in range(2)]
    cent, sq, on, gated = t3("g_cent"), t3("g_sq"), t3("g_on"), t3("g_gated")
    sd, rg, rgT = sb("g_sd", [128, GB * H1], F32), sb("g_rg", [128, GB, H1], F32), sb("g_rgT", [H1, N], F32)
    x1 = sb("g_x1", [128, GB, E1], F32)
    xn2, xa2, sx2 = sb("g_xn2", [128, GB, E1], F32), sb("g_xa2", [128, EB, GB, L1 + 1], F32), t3("g_sx2t")
    xk, xr, kk = t3("g_xk"), t3("g_xr"), t3("g_kk")
    th2, y = sb("g_th2", [128, GB, E1], F32), sb("g_y", [128, GB, E1], F32)
    out_t = [sb(f"g_out{i}", [128, GB, E1], F32) for i in range(2)]
    norms = [(sb(f"g_stats{i}", [128, GB, 6], F32), sb(f"g_mv{i}", [128, GB, 2], F32), sb(f"g_rstd{i}", [128, GB], F32)) for i in range(2)]

    def pair(bank):
        return bank[:, :].rearrange("p (a n) -> p a n", a=EB)
    FEAT, MIX, PROJ_A, PROJ_B, STATE, T6, T7 = pb[0], pb[1:3], pb[3], pb[4], pb[5], pb[6], pb[7]

    NM = NMIX * EB
    def mix_bank(g, i):
        return pair(MIX[((g.slot * NM + i) // EB) % 2])[:, i % EB, :]

    def mix_buffer(g, i):
        return z[(g.slot * NM + i) % NZ][:, :]

    decay_set = sem("g_decay_set")
    x_ready, res_ready, s0_ready = ([sem(f"g_{k}{i}") for i in range(2)] for k in ("x_ready", "res_ready", "s0_ready"))
    g_out, g_vout = [sem(f"g_out{i}") for i in range(2)], [sem(f"g_vout{i}") for i in range(2)]
    g_vin = [sem(f"g_vin{i}") for i in range(NU)]
    names = ("stats aggr var rstd normed feat xa edge sx mixin maa th5 xxx z xm proj evac projg gth gsd ewd kv edge2 scan rs summed ruk cb "
             "cv og cent sq var2 sd vg rgt rgtc rb on on2 gated wo x1 "
             "stats2 aggr2 var3 rstd2 normed2 feat2 xc edgec sx2 xk kkp kkr kk rrp th2 fvp y fin").split()
    s = {n: sem("g_" + n) for n in names}
    PJ = 5
    J_HID, J_DECAY, J_K, J_V, J_R = range(PJ)

    def plan(it, c, static):
        def group(off):
            return Pair(it, c + off) if not static or 0 <= c + off < NG else None
        return group(2), group(1), group(0), group(-1), group(-2)

    def iterations(engine, run):
        for c in range(-1, 4):
            run(*plan(0, c, True))
        with engine.Fori(2, NG // 2 - 1) as it:
            for c in (0, 1):
                run(*plan(it, c, False))
        for c in range(NG - 2, NG + 2):
            run(*plan(0, c, True))

    def sync(sp):
        def x_rows(g):
            return scr["x1"][bass.ds(g.n * GB, GB), :, :].rearrange("b l e -> l b e")

        def small(name, g):
            return W[name][bass.ds(g.n, 1), :, :].rearrange("o p x -> (o p) x")

        def load_front(g):
            src, src_st = x_rows(g), small("st1", g)
            need(sp, s["edge"], g.n - 1)
            need(sp, s["normed"], g.n - 1)
            sp.dma_start(x_in[g.slot][:, :, :], src).then_inc(x_ready[g.slot], 16)
            sp.dma_start(st1[g.slot][:, :, :].rearrange("p a b -> p (a b)"), src_st).then_inc(x_ready[g.slot], 16)

        def run(x, e, f, m, t):
            if m:
                src, src_st = x_rows(m), small("st0", m)
                need(sp, s["edgec"], m.n - 1)
                need(sp, s["x1"], m.n - 1)
                sp.dma_start(xres[m.slot][:, :, :], src).then_inc(res_ready[m.slot], 16)
                sp.dma_start(st0[m.slot][:, :, :].rearrange("p a b -> p (a b)"), src_st).then_inc(res_ready[m.slot], 16)
            if x:
                load_front(x)
            if f:
                src = small("s0", f)
                need(sp, s["edge2"], f.n * NU - NU)
                sp.dma_start(s0[f.slot][:, :, :, :].rearrange("p a j b -> p (a j b)"), src).then_inc(s0_ready[f.slot], 16)
                sp.wait_ge(s["evac"], f.n * PJ + J_V + 1)
                sp.dma_start(scr["v"][f.slot].rearrange("a p n -> p a n"), vT[f.slot][:, :, :]).then_inc(g_vout[f.slot], 16)
                sp.wait_ge(g_vout[f.slot], f.use * 16 + 16)
                for i, (hb, jq) in enumerate(UN):
                    need(sp, s["kv"], f.n * NU - NU + i + 1)
                    src = scr["v"][f.slot, hb].rearrange("(h q j) n -> q h (j n)", h=16, q=S1 // JH)[jq]
                    sp.dma_start(vbc[i][:, :, :].rearrange("p j n -> p (j n)"), src.unsqueeze(1).broadcast_to((16, S1, JH * N))).then_inc(g_vin[i], 16)
            if t:
                dst = W["out"][bass.ds(t.n * GB, GB), :, :].rearrange("b l e -> l b e")
                sp.wait_ge(s["fin"], t.n + 1)
                sp.dma_start(dst, out_t[t.slot][:, :, :]).then_inc(g_out[t.slot], 16)
        load_front(Pair(0, 0))
        iterations(sp, run)
        for i in range(2):
            sp.wait_ge(g_out[i], NG // 2 * 16)

    def gpsimd(pool):
        def rsqrt(n, i, aggr, var, done):
            _, mv, rstd = norms[i]
            pool.wait_ge(s[aggr], n + 1)
            nc.gpsimd.tensor_tensor(rstd[:, :], mv[:, :, 1], epst[:, 0:GB], ALU.add).then_inc(s[var], 1)
            pool.wait_ge(s[var], n + 1)
            nc.gpsimd.tensor_tensor(rstd[:, :], rstd[:, :], half[:, 0:GB], ALU.pow).then_inc(s[done], 1)

        def shift(n, src, dst, ready, edge, done):
            pool.wait_ge(s[ready], n + 1)
            pool.wait_ge(s[edge], n + 1)
            for eb in range(EB):
                last = nc.gpsimd.tensor_tensor(bl(dst[:, eb, :]), src[:, eb, :, 0:L1], src[:, eb, :, 1:L1 + 1], ALU.subtract)
            last.then_inc(s[done], 1)

        def run(x, e, f, m, t):
            def mixed(i0, i1):
                if not f:
                    return
                for i in range(i0, i1):
                    mix, eb = MIX_ORDER[i // EB], i % EB
                    pool.wait_ge(s["z"], f.n * NM + i + 1)
                    nc.gpsimd.tensor_tensor(bl(xm[mix][f.slot][:, eb, :]), bl(mix_buffer(f, i)), xa[f.slot][:, eb, :, 1:L1 + 1], ALU.add).then_inc(s["xm"], 1)

            def key_value(i):
                if not m:
                    return
                hb = UN[i][0]
                if i == 0:
                    pool.wait_ge(s["evac"], m.n * PJ + J_K + 1)
                pool.wait_ge(g_vin[i], m.n * 16 + 16)
                need(pool, s["summed"], m.n * NU + i - 1)
                key = bl(kT[m.slot][:, hb, :])[:, :, 0:L1 - 1].unsqueeze(1).broadcast_to((128, JH, GB, L1 - 1))
                a4 = aS[i % 2][:, :, :].rearrange("p j (b l) -> p j b l", b=GB)
                v4 = vbc[i][:, :, :].rearrange("p j (b l) -> p j b l", b=GB)
                nc.gpsimd.tensor_tensor(a4[:, :, :, 1:L1], v4[:, :, :, 0:L1 - 1], key, ALU.mult).then_inc(s["kv"], 1)

            key_value(0)
            if f:
                need(pool, s["proj"], f.n * PJ)
                need(pool, s["projg"], f.n - 1)
            mixed(0, 4)
            key_value(1)
            if t:
                pool.wait_ge(s["on2"], t.n + 1)
                pool.wait_ge(s["gsd"], t.n * EB + EB)
                need(pool, s["wo"], t.n)
                nc.gpsimd.tensor_tensor(gated[:, :, :], on[:, :, :], gs[t.slot][:, :, :], ALU.mult).then_inc(s["gated"], 1)
            if e:
                rsqrt(e.n, 0, "aggr", "var", "rstd")
            mixed(4, 6)
            key_value(2)
            if t:
                rsqrt(t.n, 1, "aggr2", "var3", "rstd2")
            mixed(6, 8)
            if e:
                need(pool, s["z"], e.n * NM - NM)
                need(pool, s["mixin"], e.n - 1)
                shift(e.n, xa[e.slot], sx[e.slot], "xa", "edge", "sx")
            key_value(3)
            if t:
                need(pool, s["xk"], t.n)
                shift(t.n, xa2, sx2, "xc", "edgec", "sx2")
            mixed(8, 10)
        iterations(pool, run)

    def tensor(pe):
        def to_features(src, bank, ready, n, done):
            pe.wait_ge(s[ready], n + 1)
            for eb in range(EB):
                for b in range(GB):
                    last = nc.tensor.transpose(bank[:, eb * N + b * L1:eb * N + (b + 1) * L1], src[:, b, eb * 128:(eb + 1) * 128], ident[:, :])
            last.then_inc(s[done], 1)

        def run(x, e, f, m, t):
            def mixes(mix):
                i0 = MIX_ORDER.index(mix) * EB
                need(pe, s["z"], f.n * NM + i0 - EB)
                for i in range(i0, i0 + EB):
                    eb = i - i0
                    if mix == 4:
                        last = nc.tensor.matmul(mix_bank(f, i), maa2b[:, eb * 128:(eb + 1) * 128], th5b[:, :], start=True, stop=True)
                    else:
                        r = slice(DM * mix, DM * mix + DM)
                        last = nc.tensor.matmul(mix_bank(f, i), maa2[r, eb * 128:(eb + 1) * 128], th5[r, :], start=True, stop=True, tile_position=(DM * mix, 0))
                last.then_inc(s["xxx"], 1)

            def project(g, mix, wt, bank, done):
                pe.wait_ge(s["xm"], g.n * NM + (MIX_ORDER.index(mix) + 1) * EB)
                for ob in range(EB):
                    for eb in range(EB):
                        last = nc.tensor.matmul(pair(bank)[:, ob, :], wt[:, eb, ob * 128:(ob + 1) * 128], xm[mix][g.slot][:, eb, :],
                                                start=(eb == 0), stop=(eb == EB - 1))
                last.then_inc(s[done], 1)

            def sums(i):
                if not m:
                    return
                hb, jq = UN[i]
                if i == 0:
                    pe.wait_ge(s["cv"], m.n + 1)
                pe.wait_ge(s["rs"], m.n * NU + i + 1)
                for j in range(JH):
                    last = nc.tensor.matmul(pair(STATE)[:, hb, :], esum[:, jq * JH + j, :], aS[i % 2][:, j, :],
                                            start=(jq == 0 and j == 0), stop=(jq == S1 // JH - 1 and j == JH - 1))
                last.then_inc(s["summed"], 1)

            def to_positions(src, wt, bank, done):
                for b in range(GB):
                    for eb in range(EB):
                        last = nc.tensor.matmul(bank[:, b * E1:(b + 1) * E1], src[:, eb, b * L1:(b + 1) * L1], wt[:, eb, :],
                                                start=(eb == 0), stop=(eb == EB - 1))
                last.then_inc(s[done], 1)

            if t:
                pe.wait_ge(s["og"], t.n + 1)
                need(pe, s["th2"], t.n)
                for hb in range(EB):
                    last = nc.tensor.matmul(pair(T6)[:, hb, :], cmat[:, :], og[t.slot][:, hb, :], start=True, stop=True)
                last.then_inc(s["cent"], 1)
            if f:
                pe.wait_ge(s["th5"], f.n + 1)
                mixes(MIX_W)
                mixes(MIX_K)
            if t:
                pe.wait_ge(s["sq"], t.n + 1)
                need(pe, s["y"], t.n)
                for b in range(GB):
                    for hb in range(EB):
                        last = nc.tensor.matmul(T7[:, b * H1 + hb * 16:b * H1 + hb * 16 + 16], sq[:, hb, b * L1:(b + 1) * L1], blkh[:, :],
                                                start=True, stop=True)
                last.then_inc(s["var2"], 1)
            if m:
                pe.wait_ge(s["ruk"], m.n + 1)
                need(pe, s["og"], m.n)
                for hb in range(EB):
                    last = nc.tensor.matmul(pair(STATE)[:, hb, :], blk[:, :], ruk[:, hb, :], start=True, stop=True)
                last.then_inc(s["cb"], 1)
                pe.wait_ge(s["evac"], m.n * PJ + J_V + 1)
                project(m, MIX_G, w["Wg"], PROJ_B, "projg")
            if f:
                mixes(MIX_V)
                pe.wait_ge(s["xm"], f.n * NM + EB)
                need(pe, s["evac"], f.n * PJ)
                for eb in range(EB):
                    last = nc.tensor.matmul(PROJ_A[0:DD, 0:N], td1[:, eb, :], xm[MIX_W][0][:, eb, :], start=(eb == 0), stop=(eb == EB - 1))
                last.then_inc(s["proj"], 1)
            if t:
                pe.wait_ge(s["vg"], t.n + 1)
                for b in range(GB):
                    last = nc.tensor.transpose(T7[0:H1, N + b * L1:N + (b + 1) * L1], rg[:, b, :], ident[:, :])
                last.then_inc(s["rgt"], 1)
            sums(0)
            if t:
                pe.wait_ge(s["rgtc"], t.n + 1)
                for hb in range(EB):
                    last = nc.tensor.matmul(pair(T6)[:, hb, :], hsel[:, hb, :], rgT[:, :], start=True, stop=True)
                last.then_inc(s["rb"], 1)
            if f:
                pe.wait_ge(s["evac"], f.n * PJ + J_HID + 1)
                need(pe, s["gsd"], f.n * EB)
                for ob in range(EB):
                    last = nc.tensor.matmul(pair(PROJ_B)[:, ob, :], td2[:, ob * 128:(ob + 1) * 128], tdh[:, :], start=True, stop=True)
                last.then_inc(s["proj"], 1)
                project(f, MIX_K, w["Wk"], PROJ_A, "proj")
            if f:
                mixes(MIX_R)
            if t:
                pe.wait_ge(s["gated"], t.n + 1)
                to_positions(gated, w["Wo"], T7, "wo")
            sums(1)
            if f:
                pe.wait_ge(s["evac"], f.n * PJ + J_DECAY + 1)
                project(f, MIX_V, w["Wv"], PROJ_B, "proj")
                mixes(MIX_G)
            if e:
                need(pe, s["th5"], e.n)
                to_features(xn, FEAT, "normed", e.n, "feat")
            if t:
                to_features(xn2, T6, "normed2", t.n, "feat2")
            if f:
                pe.wait_ge(s["evac"], f.n * PJ + J_K + 1)
                project(f, MIX_R, w["Wr"], PROJ_A, "proj")
            sums(2)
            if e:
                pe.wait_ge(s["mixin"], e.n + 1)
                for eb in range(EB):
                    nc.tensor.matmul(FEAT[:, 0:N], maa1[:, eb, 0:128], mixin[:, eb, :], start=(eb == 0), stop=(eb == EB - 1))
                for eb in range(EB):
                    last = nc.tensor.matmul(FEAT[0:DM, N:2 * N], maa1[:, eb, 128:160], mixin[:, eb, :], start=(eb == 0), stop=(eb == EB - 1))
                last.then_inc(s["maa"], 1)
            if t:
                pe.wait_ge(s["xk"], t.n + 1)
                for ob in range(EB):
                    for eb in range(EB):
                        last = nc.tensor.matmul(pair(T7)[:, ob, :], w["Wfk"][:, eb, ob * 128:(ob + 1) * 128], xk[:, eb, :],
                                                start=(eb == 0), stop=(eb == EB - 1))
                last.then_inc(s["kkp"], 1)
                to_positions(xr, w["Wfr"], T6, "rrp")
            sums(3)
            if t:
                pe.wait_ge(s["kk"], t.n + 1)
                to_positions(kk, w["Wfv"], T7, "fvp")
        iterations(pe, run)

    def scalar(act):
        def run(x, e, f, m, t):
            def ready(j):
                act.wait_ge(s["proj"], f.n * PJ + j + 1)

            if t:
                act.wait_ge(s["cent"], t.n + 1)
                need(act, s["var2"], t.n)
                nc.scalar.activation(cols(sq), T6[:, :], ACT.Square)
                need(act, s["on"], t.n)
                nc.scalar.activation(cols(cent), T6[:, :], ACT.Copy).then_inc(s["sq"], 1)
                need(act, s["vg"], t.n)
                act.wait_ge(s["var2"], t.n + 1)
                nc.scalar.activation(sd[:, :], T7[:, 0:GB * H1], ACT.Sqrt, bias=epst[:, 0:1]).then_inc(s["sd"], 1)
            if m:
                need(act, s["gsd"], m.n * EB)
                act.wait_ge(s["projg"], m.n + 1)
                nc.scalar.activation(cols(gth), PROJ_B[:, :], ACT.Tanh, scale=0.5).then_inc(s["gth"], 1)
            if t:
                need(act, s["rb"], t.n)
                act.wait_ge(s["rgt"], t.n + 1)
                nc.scalar.activation(rgT[:, :], T7[0:H1, N:2 * N], ACT.Copy).then_inc(s["rgtc"], 1)
            if f:
                ready(J_HID)
                nc.scalar.activation(tdh[:, :], PROJ_A[0:DD, 0:N], ACT.Tanh).then_inc(s["evac"], 1)
            if t:
                act.wait_ge(s["on"], t.n + 1)
                for hb in range(EB):
                    last = nc.scalar.activation(on[:, hb, :], on[:, hb, :], ACT.Identity, bias=hvec[:, hb, 1:2], scale=hvec[:, hb, 0:1])
                last.then_inc(s["on2"], 1)
            if f:
                ready(J_DECAY)
                for eb in range(EB):
                    last = nc.scalar.activation(ew[:, eb, :], pair(PROJ_B)[:, eb, :], ACT.Exp, bias=v("time_decay", eb))
                last.then_inc(s["evac"], 1)
                if isinstance(f.n, int) and f.n == 0:
                    act.wait_ge(decay_set, 1)
                need(act, s["scan"], f.n * NU - NU)
                act.wait_ge(s["evac"], f.n * PJ + J_DECAY + 1)
                for eb in range(EB):
                    last = nc.scalar.activation(bl(wS[f.slot][:, eb, :])[:, :, 1:L1], bl(ew[:, eb, :])[:, :, 0:L1 - 1], ACT.Exp, scale=-1.0)
                last.then_inc(s["ewd"], 1)
                need(act, s["kv"], f.n * NU - NU)
                need(act, s["ruk"], f.n - 1)
                ready(J_K)
                nc.scalar.activation(cols(kT[f.slot]), PROJ_A[:, :], ACT.Copy).then_inc(s["evac"], 1)
                need(act, g_vout[f.slot], f.use * 16)
                need(act, s["cv"], f.n - 1)
                ready(J_V)
                nc.scalar.activation(cols(vT[f.slot]), PROJ_B[:, :], ACT.Copy).then_inc(s["evac"], 1)
            if e:
                need(act, s["sx"], e.n - 1)
                need(act, s["mixin"], e.n - 1)
                need(act, s["xm"], e.n * NM - NM)
                act.wait_ge(s["feat"], e.n + 1)
                for eb in range(EB):
                    last = nc.scalar.activation(xa[e.slot][:, eb, :, 1:L1 + 1], bl(pair(FEAT)[:, eb, :]), ACT.Identity, bias=v("ln1_b", eb), scale=v("ln1_w", eb))
                last.then_inc(s["xa"], 1)
            if t:
                need(act, s["xk"], t.n)
                act.wait_ge(s["feat2"], t.n + 1)
                for eb in range(EB):
                    last = nc.scalar.activation(xa2[:, eb, :, 1:L1 + 1], bl(pair(T6)[:, eb, :]), ACT.Identity, bias=v("ln2_b", eb), scale=v("ln2_w", eb))
                last.then_inc(s["xc"], 1)
            if f:
                need(act, s["rs"], f.n * NU - NU)
                ready(J_R)
                nc.scalar.activation(cols(rT[f.slot]), PROJ_A[:, :], ACT.Copy).then_inc(s["evac"], 1)
            if e:
                need(act, s["xxx"], e.n * NMIX)
                act.wait_ge(s["maa"], e.n + 1)
                nc.scalar.activation(th5b[:, :], FEAT[0:DM, N:2 * N], ACT.Tanh)
                nc.scalar.activation(th5[:, :], FEAT[:, 0:N], ACT.Tanh).then_inc(s["th5"], 1)
            if t:
                need(act, s["fvp"], t.n)
                act.wait_ge(s["kkp"], t.n + 1)
                nc.scalar.activation(cols(kk), T7[:, :], ACT.Relu).then_inc(s["kkr"], 1)
                act.wait_ge(s["kkr"], t.n + 1)
                nc.scalar.activation(cols(kk), cols(kk), ACT.Square).then_inc(s["kk"], 1)
                need(act, s["y"], t.n)
                act.wait_ge(s["rrp"], t.n + 1)
                nc.scalar.activation(cols(th2), T6[:, :], ACT.Tanh, scale=0.5).then_inc(s["th2"], 1)
        iterations(act, run)

    def vector(dve):
        dve.wait_ge(x_ready[0], 32)
        for i in range(2):
            nc.vector.memset(cols(wS[i]), 0.0)
        nc.vector.memset(z[0][:, 0:1], 0.0).then_inc(decay_set, 1)

        def statistics(n, i, src, st_, edge, ag):
            stats, mv, _ = norms[i]
            for b in range(GB):
                last = nc.vector.bn_stats(stats[:, b, :], src[:, b, :])
            last.then_inc(s[st_], 1)
            dve.wait_ge(s[st_], n + 1)
            edge()
            for b in range(GB):
                last = nc.vector.bn_aggr(mv[:, b, :], stats[:, b, :])
            last.then_inc(s[ag], 1)

        def normalise(n, i, src, dst, ready, done):
            _, mv, rstd = norms[i]
            dve.wait_ge(s[ready], n + 1)
            for b in range(GB):
                last = nc.vector.tensor_scalar(dst[:, b, :], src[:, b, :], mv[:, b, 0:1], rstd[:, b:b + 1], ALU.subtract, ALU.mult)
            last.then_inc(s[done], 1)

        def run(x, e, f, m, t):
            def mix(i0, i1):
                if not f:
                    return
                for i in range(i0, i1):
                    kind, eb = MIX_ORDER[i // EB], i % EB
                    need(dve, s["xm"], f.n * NM + i - NZ + 1)
                    if eb == 0:
                        dve.wait_ge(s["xxx"], f.n * NMIX + i // EB + 1)
                    nc.vector.scalar_tensor_tensor(mix_buffer(f, i), mix_bank(f, i), v(f"stack{kind}", eb), sx[f.slot][:, eb, :], ALU.add, ALU.mult).then_inc(s["z"], 1)

            def scan(i):
                if not m:
                    return
                hb, jq = UN[i]
                if i == 0:
                    dve.wait_ge(s0_ready[m.slot], m.use * 16 + 16)
                    dve.wait_ge(s["ewd"], m.n + 1)
                dve.wait_ge(s["kv"], m.n * NU + i + 1)
                a4 = aS[i % 2][:, :, :].rearrange("p j (b l) -> p j b l", b=GB)
                nc.vector.tensor_copy(a4[:, :, :, 0], s0[m.slot][:, hb, jq * JH:(jq + 1) * JH, :]).then_inc(s["edge2"], 1)
                dve.wait_ge(s["edge2"], m.n * NU + i + 1)
                for j in range(JH):
                    last = nc.vector.tensor_tensor_scan(SS[i % 2][:, j, :], wS[m.slot][:, hb, :], aS[i % 2][:, j, :], 0.0, ALU.mult, ALU.add)
                last.then_inc(s["scan"], 1)
                dve.wait_ge(s["scan"], m.n * NU + i + 1)
                nc.vector.tensor_tensor(aS[i % 2][:, :, :], SS[i % 2][:, :, :], rT[m.slot][:, hb:hb + 1, :].broadcast_to((128, JH, N)), ALU.mult).then_inc(s["rs"], 1)

            if m:
                need(dve, s["cb"], m.n)
                dve.wait_ge(s["evac"], m.n * PJ + J_R + 1)
                for hb in range(EB):
                    last = nc.vector.scalar_tensor_tensor(ruk[:, hb, :], rT[m.slot][:, hb, :], v("u", hb), kT[m.slot][:, hb, :], ALU.mult, ALU.mult)
                last.then_inc(s["ruk"], 1)
            mix(0, 4)
            if m:
                need(dve, s["cent"], m.n - 1)
                dve.wait_ge(s["cb"], m.n + 1)
                nc.vector.tensor_tensor(cols(og[m.slot]), STATE[:, :], cols(vT[m.slot]), ALU.mult).then_inc(s["cv"], 1)
            scan(0)
            if t:
                need(dve, s["rgt"], t.n)
                dve.wait_ge(s["sd"], t.n + 1)
                nc.vector.reciprocal(rg[:, :, :].rearrange("p b h -> p (b h)"), sd[:, :]).then_inc(s["vg"], 1)
            if m:
                need(dve, s["gated"], m.n - 1)
                dve.wait_ge(s["gth"], m.n + 1)
                nc.vector.scalar_tensor_tensor(cols(gs[m.slot]), cols(gth), 1.0, PROJ_B[:, :], ALU.add, ALU.mult).then_inc(s["gsd"], EB)
            mix(4, 6)
            if t:
                need(dve, s["gated"], t.n)
                dve.wait_ge(s["sq"], t.n + 1)
                dve.wait_ge(s["rb"], t.n + 1)
                nc.vector.tensor_tensor(cols(on), cols(cent), T6[:, :], ALU.mult).then_inc(s["on"], 1)
            if e:
                dve.wait_ge(x_ready[e.slot], e.use * 32 + 32)

                def edge():
                    need(dve, s["sx"], e.n - 1)
                    nc.vector.tensor_copy(xa[e.slot][:, :, :, 0], st1[e.slot][:, :, :]).then_inc(s["edge"], 1)
                statistics(e.n, 0, x_in[e.slot], "stats", edge, "aggr")
            scan(1)
            if t:
                dve.wait_ge(res_ready[t.slot], t.use * 32 + 32)
                dve.wait_ge(s["wo"], t.n + 1)
                nc.vector.tensor_tensor(cols(x1), T7[:, :], cols(xres[t.slot]), ALU.add).then_inc(s["x1"], 1)
                dve.wait_ge(s["x1"], t.n + 1)

                def edge():
                    need(dve, s["sx2"], t.n)
                    nc.vector.tensor_copy(xa2[:, :, :, 0], st0[t.slot][:, :, :]).then_inc(s["edgec"], 1)
                statistics(t.n, 1, x1, "stats2", edge, "aggr2")
            mix(6, 8)
            if e:
                need(dve, s["feat"], e.n)
                normalise(e.n, 0, x_in[e.slot], xn, "rstd", "normed")
            scan(2)
            if t:
                need(dve, s["feat2"], t.n)
                normalise(t.n, 1, x1, xn2, "rstd2", "normed2")
            if e:
                need(dve, s["maa"], e.n)
                dve.wait_ge(s["xa"], e.n + 1)
                dve.wait_ge(s["sx"], e.n + 1)
                for eb in range(EB):
                    last = nc.vector.scalar_tensor_tensor(bl(mixin[:, eb, :]), bl(sx[e.slot][:, eb, :]), v("maa_x", eb), xa[e.slot][:, eb, :, 1:L1 + 1], ALU.mult, ALU.add)
                last.then_inc(s["mixin"], 1)
            mix(8, 10)
            scan(3)
            if t:
                need(dve, s["rrp"], t.n)
                dve.wait_ge(s["xc"], t.n + 1)
                dve.wait_ge(s["sx2"], t.n + 1)
                for dst, name in ((xk, "ffn_maa_k"), (xr, "ffn_maa_r")):
                    for eb in range(EB):
                        last = nc.vector.scalar_tensor_tensor(bl(dst[:, eb, :]), bl(sx2[:, eb, :]), v(name, eb), xa2[:, eb, :, 1:L1 + 1], ALU.mult, ALU.add)
                last.then_inc(s["xk"], 1)
            if m:
                dve.wait_ge(s["summed"], m.n * NU + NU)
                nc.vector.tensor_tensor(cols(og[m.slot]), STATE[:, :], cols(og[m.slot]), ALU.add).then_inc(s["og"], 1)
            if t:
                dve.wait_ge(s["th2"], t.n + 1)
                dve.wait_ge(s["fvp"], t.n + 1)
                nc.vector.scalar_tensor_tensor(cols(y), cols(th2), 1.0, T7[:, :], ALU.add, ALU.mult).then_inc(s["y"], 1)
                need(dve, g_out[t.slot], t.use * 16)
                dve.wait_ge(s["y"], t.n + 1)
                nc.vector.scalar_tensor_tensor(cols(out_t[t.slot]), cols(y), 0.5, cols(x1), ALU.mult, ALU.add).then_inc(s["fin"], 1)
        iterations(dve, run)

    return {"tensor": tensor, "scalar": scalar, "vector": vector, "gpsimd": gpsimd, "sync": sync}


def program(nc, W):
    persistent = ExitStack()
    with persistent:
        sem = lambda name: persistent.enter_context(nc.semaphore(name))
        sb = lambda name, shape, dt: persistent.enter_context(nc.sbuf_tensor(name, shape, dt))
        env = {"sem": sem, "in": W, "sb": sb}
        env["pb"] = [persistent.enter_context(nc.psum_tensor(f"bank{i}", [128, 512], F32)) for i in range(8)]
        env["dram"] = {
            "stack": nc.dram_tensor("stack_scratch", [SLOTS, 2, 128, NTERM, T], BF16).ap(),
            "q": nc.dram_tensor("q_scratch", [NB, C, T], F32).ap(),
            "raw": nc.dram_tensor("raw_scratch", [NB, 128, 4, T], F32).ap(),
            "rden": nc.dram_tensor("rden_scratch", [NB, 4, D0, 4, T], F32).ap(),
            "x1": nc.dram_tensor("x1_scratch", [NB, C, T], F32).ap(),
            "v": nc.dram_tensor("v_scratch", [2, EB, 128, GB * L1], F32).ap(),
        }
        ident, ident_b = sb("ident", [128, 128], F32), sb("ident_b", [128, 128], BF16)
        half, epst = sb("minus_half", [128, 128], F32), sb("eps", [128, 16], F32)
        zero = sb("zero", [128, 1, 1], F32)
        env.update(ident=ident, ident_b=ident_b, half=half, epst=epst, zero=zero)
        shapes = {
            "f_wo": [128, C], "f_w1": [128, 2 * C], "f_w2": [128, F0, C], "f_vec": [128, 3 + F0],
            "g_vec": [128, EB, len(VECS)], "g_maa1": [128, EB, NMIX * DM], "g_maa2": [128, E1], "g_maa2b": [DM, E1],
            "g_td1": [128, EB, DD], "g_td2": [DD, E1], "g_esum": [128, S1, 128], "g_blk": [128, 128], "g_cmat": [128, 128],
            "g_blkh": [128, 16], "g_hsel": [H1, EB, 128],
        }
        for name, shape in shapes.items():
            env[name] = sb(name, shape, F32)
        env["g_w"] = {name: sb("g_" + name, [128, EB, E1], F32) for name in MATS}
        env["g_hvec"] = sb("g_hvec", [128, EB, 2], F32)
        loads = [(env[name], W[name]) for name in shapes] + [(env["g_w"][name], W["g_" + name]) for name in MATS]
        weights_in, consts_in, const_set, hvec_set = sem("weights_in"), sem("consts_in"), sem("const_set"), sem("hvec_set")
        ident_cast = sem("ident_cast")
        env.update(consts_in=consts_in, const_set=const_set, nconst=16 * 6)
        phases = []
        for phase in (attention, feed_forward, recurrent):
            with ExitStack() as arena:
                env["sb"] = lambda name, shape, dt: arena.enter_context(nc.sbuf_tensor(name, shape, dt))
                phases.append(phase(nc, env))
        block = persistent.enter_context(nc.Block())

        @block.sync
        def _(sp):
            sp.dma_start(ident[:, :], W["ident"]).then_inc(consts_in, 16)
            phases[0]["tables"](sp)
            for tile, src in loads:
                sp.dma_start(tile[tuple(slice(None) for _ in tile.shape)], src).then_inc(weights_in, 16)
            for phase in phases:
                phase["sync"](sp)

        @block.gpsimd
        def _(pool):
            nc.gpsimd.memset(half[:, :], -0.5).then_inc(const_set, 1)
            nc.gpsimd.memset(epst[:, :], EPS).then_inc(const_set, 1)
            nc.gpsimd.memset(zero[:, :, :], 0.0).then_inc(const_set, 1)
            pool.wait_ge(const_set, 3)
            for phase in phases:
                phase["gpsimd"](pool)

        @block.tensor
        def _(pe):
            pe.wait_ge(consts_in, env["nconst"])
            pe.wait_ge(ident_cast, 1)
            phases[0]["tensor"](pe)
            pe.wait_ge(weights_in, 16 * len(loads))
            phases[1]["tensor"](pe)
            phases[2]["tensor"](pe)

        @block.scalar
        def _(act):
            phases[0]["scalar"](act)
            act.wait_ge(weights_in, 16 * len(loads))
            act.wait_ge(hvec_set, 1)
            phases[1]["scalar"](act)
            phases[2]["scalar"](act)

        @block.vector
        def _(dve):
            phases[0]["clear"](dve)
            dve.wait_ge(consts_in, env["nconst"])
            nc.vector.tensor_copy(ident_b[:, :], ident[:, :]).then_inc(ident_cast, 1)
            phases[0]["vector"](dve)
            dve.wait_ge(weights_in, 16 * len(loads))
            i = VECS.index("gn_w")
            nc.vector.tensor_scalar(env["g_hvec"][:, :, :], env["g_vec"][:, :, i:i + 2], 0.5, None, ALU.mult).then_inc(hvec_set, 1)
            phases[1]["vector"](dve)
            phases[2]["vector"](dve)


MATS = ("Wk", "Wv", "Wr", "Wg", "Wo", "Wfk", "Wfr", "Wfv")


def arrays_for(inputs):
    a = {k: np.asarray(v) for k, v in inputs.items()}
    p0, p1 = "L0_xattn_", "L1_xattn_"
    out = {k: a[k] for k in (p0 + "Wq", p0 + "Wk", p0 + "Wv")}
    out["ln"] = np.stack([a[p0 + k] for k in ("ln_q_g", "ln_q_b", "ln_kv_g", "ln_kv_b")], axis=1)
    x, ctx = a["x"], a["ctx_2048"]
    out["x_ctx"] = np.stack([x, ctx], axis=2)
    pos = np.arange(T, dtype=np.float32)[:, None]
    ang = pos * np.exp(np.arange(0, C, 2, dtype=np.float32) * np.float32(-math.log(10000.0) / C))
    table = np.zeros((T, C), np.float32)
    table[:, 0::2], table[:, 1::2] = np.sin(ang), np.cos(ang)
    out["pos"] = np.ascontiguousarray(table.T)
    out["ident"] = np.eye(128, dtype=np.float32)
    rows = [(2 * g + j % 2 + NTILE * (j // 2)) * D0 + d for j in range(4) for d in range(D0) for g in range(4)]
    out["f_wo"] = a[p0 + "Wo"][rows]
    out["f_w1"] = a[p0 + "W1"]
    out["f_w2"] = np.ascontiguousarray(a[p0 + "W2"].reshape(F0, 128, C).transpose(1, 0, 2))
    out["f_vec"] = np.stack([a[p0 + "ffn_ln_g"], a[p0 + "ffn_ln_b"], a[p0 + "b2"], *a[p0 + "b1"].reshape(F0, 128)], axis=1)

    def halves(m):
        return np.ascontiguousarray(m.reshape(EB, 128, -1).transpose(1, 0, 2))
    vecs = {n: a[p1 + n] for n in VECS if p1 + n in a}
    vecs["u"] = a[p1 + "u"].reshape(E1)
    vecs.update({f"stack{f}": a[p1 + "maa_stack"][0, f] for f in range(NMIX)})
    out["g_vec"] = halves(np.stack([vecs[n] for n in VECS], axis=1))
    out["g_maa1"] = halves(a[p1 + "maa_w1"])
    out["g_maa2"] = a[p1 + "maa_w2"][0:4].reshape(128, E1)
    out["g_maa2b"] = a[p1 + "maa_w2"][4]
    out["g_td1"], out["g_td2"] = halves(a[p1 + "td_w1"]), a[p1 + "td_w2"]
    for n in MATS:
        out["g_" + n] = halves(a[p1 + n].T)
    r = np.arange(128)
    same = r[:, None] // S1 == r[None, :] // S1
    out["g_esum"] = np.stack([(same & (r[None, :] % S1 == j)) for j in range(S1)], axis=1).astype(np.float32)
    out["g_blk"] = same.astype(np.float32)
    out["g_cmat"] = (np.eye(128) - same / S1).astype(np.float32)
    out["g_blkh"] = ((r[:, None] // S1 == np.arange(16)[None, :]) / S1).astype(np.float32)
    heads = np.arange(H1)[:, None, None] == (np.arange(EB)[None, :, None] * 16 + r[None, None, :] // S1)
    out["g_hsel"] = heads.astype(np.float32)
    state = ctx[:, 0:2].reshape(NG, GB, 2, EB, 128).transpose(2, 0, 4, 3, 1).reshape(2, NG, 128, -1)
    out["st0"], out["st1"] = state[0], state[1]
    out["s0"] = np.ascontiguousarray(ctx[:, 2:2 + S1].reshape(NG, GB, EB, 128, S1).transpose(0, 3, 2, 4, 1).reshape(NG, 128, -1))
    return {k: np.ascontiguousarray(v) for k, v in out.items()}


def kernel(**inputs):
    import concourse.bacc as bacc
    from concourse.bass_utils import run_bass_kernel_spmd

    nc = bacc.Bacc("TRN2", target_bir_lowering=False, num_devices=1)
    arrays = {"in_" + k: v for k, v in arrays_for(inputs).items()}
    W = {k[3:]: nc.dram_tensor(k, v.shape, mybir.dt.from_np(v.dtype), kind="ExternalInput").ap() for k, v in arrays.items()}
    W["out"] = nc.dram_tensor("result", (NB, L1, E1), F32, kind="ExternalOutput").ap()
    program(nc, W)
    r = run_bass_kernel_spmd(nc, [arrays], core_ids=[0])
    return r.results[0]["result"]
```

```python
import math
import numpy as np
import concourse.bass as bass
from concourse import mybir
from contextlib import ExitStack

F32 = mybir.dt.float32
BF16 = mybir.dt.bfloat16
ACT = mybir.ActivationFunctionType
ALU = mybir.AluOpType
AX_X = mybir.AxisListType.X

NB, C, T = 16, 128, 256
H0, D0 = 16, 8
NQB = T // 128
EPS = 1e-5

NPART = 3
NTERM = 6
ROWS = D0 * NTERM
NTILE = H0 // 2
SROWS = 64 + ROWS
MROWS = 2
UNITS = 16
PV_LAG = 2
NPROB = 8
LAG = 8
SLOTS = 4


class Turn:

    def __init__(self, it, c):
        self.n = it * SLOTS + c
        self.slot = c % SLOTS
        self.use = it + c // SLOTS


def need(engine, sem, value):
    if isinstance(value, int) and value <= 0:
        return
    engine.wait_ge(sem, value)


def attention(nc, env):
    sb, pb, sem, W = env["sb"], env["pb"], env["sem"], env["in"]
    scr = env["dram"]

    xin = [sb(f"xin{s}", [128, 2, T], F32) for s in range(2)] * 2
    xpe = [sb(f"xpe{s}", [128, 2, T], F32) for s in range(2)] * 2
    pe_tab = sb("pe_tab", [128, 2, T], F32)
    wq, wk, wv = sb("wq", [128, 128], F32), sb("wk", [128, 128], F32), sb("wv", [128, 128], F32)
    lnc = sb("ln_consts", [128, 4], F32)
    stats = sb("stats", [128, 4, 6], F32)
    mv = sb("mv", [128, 4, 2], F32)
    rstd = sb("rstd", [128, 4], F32)
    xn = sb("xn", [128, 4, 128], F32)
    qkvT = [sb(f"qkvT{s}", [128, 2, T], F32) for s in range(2)] * 2
    parts = [sb(f"parts{s}", [128, 2, NPART, T], BF16) for s in range(2)] * 2
    rest = sb("rest", [128, 2, T], F32)
    KS = [sb(f"KS{s}", [128, NTILE, T], BF16) for s in range(SLOTS)]
    QS = [sb(f"QS{s}", [128, 2, NTILE, T], BF16) for s in range(SLOTS)]
    VA = [sb(f"VA{s}", [128, NQB, H0, 32], F32) for s in range(SLOTS)]
    mx = sb("mx", [128, NQB, H0], F32)
    mparts = sb("mparts", [128, NQB, MROWS, H0], BF16)
    mT = [sb(f"mT{s}", [32, T], BF16) for s in range(2)] * 2
    prob = [sb(f"prob{s}", [128, 2, T], F32) for s in range(NPROB)]
    raw = [sb(f"raw{s}", [128, 4, T], F32) for s in range(2)] * 2
    ident, ident_b, half, epst, zero = env["ident"], env["ident_b"], env["half"], env["epst"], env["zero"]

    SM, SC, VB = pb[0:2], pb[2:4], pb[4:6]
    M0, M1 = pb[6], pb[7]
    m0 = M0[:, :].rearrange("p (a t) -> p a t", a=4)
    m1 = M1[:, :].rearrange("p (a t) -> p a t", a=4)
    m1b = M1[:, 0:128].bitcast(BF16)

    consts_in, const_set = env["consts_in"], env["const_set"]
    NCONST = env["nconst"]
    va_set, stack_set = sem("va_set"), sem("stack_set")
    x_in = [sem(f"x_in{s}") for s in range(SLOTS)]
    pos_added = sem("pos_added")
    tokens_ready = sem("tokens_ready")
    stats_done, aggr_done, var_done = sem("stats_done"), sem("aggr_done"), sem("var_done")
    rstd_ready, normed = sem("rstd_ready"), sem("normed")
    channels_ready, qkvT_ready = sem("channels_ready"), sem("qkvT_ready")
    qk_ready, v_ready = sem("qk_ready"), sem("v_ready")
    part1_done, rest_done, part2_done, part3_done = sem("part1_done"), sem("rest_done"), sem("part2_done"), sem("part3_done")
    va_ready = sem("va_ready")
    q_kept = [sem(f"q_kept{s}") for s in range(SLOTS)]
    stack_out = [sem(f"stack_out{s}") for s in range(SLOTS)]
    stack_in = [sem(f"stack_in{s}") for s in range(SLOTS)]
    m_in = [sem(f"m_in{s}") for s in range(SLOTS)]
    raw_out = [sem(f"raw_out{s}") for s in range(SLOTS)]
    smax_ready, max_done = sem("smax_ready"), sem("max_done")
    mhigh_done, mparts_ready, mT_psum, mT_ready = sem("mhigh_done"), sem("mparts_ready"), sem("mT_psum"), sem("mT_ready")
    scores_ready, exp_done, pv_done, raw_ready = sem("scores_ready"), sem("exp_done"), sem("pv_done"), sem("raw_ready")

    STACK_OUT, STACK_IN, M_IN, RAW_OUT = 6 * 16, 4 * 16, MROWS * 16, 16

    def in_range(v, c_off, static):
        return not static or 0 <= v + c_off < NB

    def plan(it, c, static):
        def turn(off):
            return Turn(it, c + off) if in_range(c, off, static) else None
        return {"x": turn(3), "a": turn(2), "l": turn(1), "b": turn(0), "h": turn(-1), "t": turn(-2)}

    def stream(p, s):
        return (p["t"], s + UNITS - LAG) if s < LAG else (p["h"], s - LAG)

    def iterations(engine, run, then={}):
        for v in range(-3, 1 + SLOTS):
            run(plan(0, v, True))
        with engine.Fori(1, NB // SLOTS - 1) as it:
            for c in range(1, 1 + SLOTS):
                run(plan(it, c, False))
        for v in range(NB - SLOTS + 1, NB + 2):
            run(plan(0, v, True))
            if v in then:
                then[v]()

    def unit(u):
        return u // 8, (u % 8) // 2, u % 2

    def cunit(u):
        return (u % 4) // 2, u // 4, u % 2

    def tensor(pe):
        def run(p):
            for s in range(UNITS):
                if p["b"]:
                    b = p["b"]
                    if s == 0:
                        pe.wait_ge(stack_in[b.slot], b.use * STACK_IN + STACK_IN)
                    qb, tp, hh = unit(s)
                    need(pe, max_done, b.n * UNITS + s - 1)
                    for a in range(2):
                        last = nc.tensor.matmul(SM[hh][:, a * T:(a + 1) * T], QS[b.slot][0:SROWS, hh, 2 * tp + a, qb * 128:(qb + 1) * 128],
                                                KS[b.slot][0:SROWS, 2 * tp + a, :], start=True, stop=True)
                    last.then_inc(smax_ready, 1)
                cur, u = stream(p, s)
                if cur:
                    kb, tp, hh = cunit(u)
                    if u == 0:
                        pe.wait_ge(m_in[cur.slot], cur.use * M_IN + M_IN)
                    need(pe, exp_done, cur.n * UNITS + u - 1)
                    for a in range(2):
                        last = nc.tensor.matmul(SC[hh][:, a * T:(a + 1) * T], KS[cur.slot][0:SROWS + MROWS, 2 * tp + a, kb * 128:(kb + 1) * 128],
                                                QS[cur.slot][0:SROWS + MROWS, hh, 2 * tp + a, :], start=True, stop=True)
                    last.then_inc(scores_ready, 1)
                prev, u = stream(p, s - PV_LAG)
                if prev and u % 2 == 1:
                    kb, tp, _ = cunit(u)
                    if u == 1:
                        pe.wait_ge(va_ready, prev.n + 1)
                    if u % 8 == 1:
                        need(pe, raw_ready, prev.n * 2 - 1 + u // 8)
                    pe.wait_ge(exp_done, prev.n * UNITS + u + 1)
                    for j in range(4):
                        hh, a = j // 2, j % 2
                        last = nc.tensor.matmul(VB[tp // 2][32 * j:32 * j + 32, (tp % 2) * T:(tp % 2 + 1) * T],
                                                VA[prev.slot][:, kb, 2 * tp + a + NTILE * hh, :], prob[(u - 1 + hh) % NPROB][:, a, :],
                                                start=(kb == 0), stop=(kb == 1))
                    last.then_inc(pv_done, 2)
                a_ = p["a"]
                if s == 0 and a_:
                    pe.wait_ge(pos_added, a_.n + 1)
                    need(pe, rest_done, a_.n)
                    for j in range(4):
                        last = nc.tensor.transpose(m0[:, j, :], xpe[a_.slot][:, j // 2, (j % 2) * 128:(j % 2 + 1) * 128], ident[:, :])
                    last.then_inc(tokens_ready, 1)
                if s == 2 and p["h"]:
                    h = p["h"]
                    pe.wait_ge(mparts_ready, h.n + 1)
                    need(pe, va_ready, h.n + (3 if p["l"] else 2 if p["b"] else 1))
                    for qb in range(NQB):
                        last = nc.tensor.transpose(m1b[0:32, qb * 128:(qb + 1) * 128], mparts[:, qb, :, :], ident_b[:, :])
                    last.then_inc(mT_psum, 1)
                if s == 6 and a_:
                    pe.wait_ge(normed, a_.n + 1)
                    need(pe, mT_ready, a_.n - 2)
                    need(pe, va_ready, a_.n)
                    for j in range(4):
                        last = nc.tensor.transpose(m1[:, j, :], xn[:, j, :], ident[:, :])
                    last.then_inc(channels_ready, 1)
                if s == 9 and a_:
                    pe.wait_ge(qkvT_ready, a_.n + 1)
                    nc.tensor.matmul(M0[:, 0:T], wq[:, :], qkvT[a_.slot][:, 0, :], start=True, stop=True)
                if s == 10 and a_:
                    nc.tensor.matmul(M0[:, T:2 * T], wk[:, :], qkvT[a_.slot][:, 1, :], start=True, stop=True).then_inc(qk_ready, 1)
                if s == 12 and a_:
                    for kb in range(NQB):
                        last = nc.tensor.matmul(M1[:, kb * 128:(kb + 1) * 128], qkvT[a_.slot][:, 1, kb * 128:(kb + 1) * 128], wv[:, :],
                                                start=True, stop=True)
                    last.then_inc(v_ready, 1)
        iterations(pe, run)

    def scalar(act):
        def clear_queries():
            for k in range(SLOTS):
                q = QS[k][:, :, :, :].rearrange("p h t q -> p (h t q)").bitcast(F32)
                nc.scalar.activation(q, zero[:, :, 0].broadcast_to((128, NTILE * T)), ACT.Copy).then_inc(stack_set, 1)

        def run(p):
            if p["x"]:
                x = p["x"]
                if isinstance(x.n, int) and x.n == 1:
                    act.wait_ge(const_set, 3)
                    clear_queries()
                need(act, pos_added, x.n - 1)
                act.dma_start(xin[x.slot][:, :, :], W["x_ctx"][bass.ds(x.n, 1), :, :, :].rearrange("o c w t -> (o c) w t")).then_inc(x_in[x.slot], 16)
            for s in range(UNITS):
                cur, u = stream(p, s)
                if cur:
                    act.wait_ge(scores_ready, cur.n * UNITS + u + 1)
                    need(act, pv_done, cur.n * UNITS + u - NPROB + 1 + u % 2)
                    nc.scalar.activation(prob[u % NPROB][:, :, :].rearrange("p a t -> p (a t)"), SC[u % 2][:, :], ACT.Exp,
                                         scale=1.0 / math.sqrt(D0)).then_inc(exp_done, 1)
                if s in (PV_LAG, LAG + PV_LAG) and p["t"]:
                    t, half_ = p["t"], s // LAG
                    act.wait_ge(pv_done, t.n * UNITS + 8 * half_ + 8)
                    if half_ == 0:
                        need(act, raw_out[(t.slot + 2) % SLOTS], (t.use + (t.slot + 2) // SLOTS) * RAW_OUT)
                    nc.scalar.activation(raw[t.slot][:, 2 * half_:2 * half_ + 2, :].rearrange("p a t -> p (a t)"), VB[half_][:, :],
                                         ACT.Copy).then_inc(raw_ready, 1)
                if s == 3 and p["h"]:
                    h = p["h"]
                    act.wait_ge(mT_psum, h.n + 1)
                    need(act, m_in[(h.slot + 2) % SLOTS], (h.use + (h.slot + 2) // SLOTS) * M_IN)
                    nc.scalar.activation(mT[h.slot][:, :], m1b[0:32, :], ACT.Copy).then_inc(mT_ready, 1)
                if s == 4 and p["h"]:
                    h = p["h"]
                    act.wait_ge(mT_ready, h.n + 1)
                    for part in range(MROWS):
                        row = SROWS + part
                        act.dma_start(QS[h.slot][row:row + 1, :, :, :].rearrange("o h t q -> o (h t q)"),
                                      mT[h.slot][H0 * part:H0 * part + H0, :]).then_inc(m_in[h.slot], 16)
                a = p["a"]
                if s == 7 and a:
                    act.wait_ge(channels_ready, a.n + 1)
                    if isinstance(a.n, int) and a.n == 0:
                        act.wait_ge(consts_in, NCONST)
                    need(act, q_kept[(a.slot + 2) % SLOTS], (a.use + (a.slot + 2) // SLOTS) * 16)
                    for w in range(2):
                        last = nc.scalar.activation(qkvT[a.slot][:, w, :], M1[:, w * T:(w + 1) * T], ACT.Identity,
                                                    bias=lnc[:, 2 * w + 1:2 * w + 2], scale=lnc[:, 2 * w:2 * w + 1])
                    last.then_inc(qkvT_ready, 1)
                if s == 11 and a:
                    act.wait_ge(qk_ready, a.n + 1)
                    need(act, stack_out[(a.slot + 2) % SLOTS], (a.use + (a.slot + 2) // SLOTS) * STACK_OUT)
                    nc.scalar.activation(parts[a.slot][:, :, 0, :], M0[:, :].rearrange("p (w t) -> p w t", w=2),
                                         ACT.Copy).then_inc(part1_done, 1)
                if s == 13 and a:
                    act.wait_ge(v_ready, a.n + 1)
                    if isinstance(a.n, int) and a.n < SLOTS:
                        act.wait_ge(va_set, 2 * SLOTS)
                    need(act, pv_done, a.n * UNITS - (SLOTS - 1) * UNITS)
                    nc.scalar.activation(VA[a.slot][:, :, :, 0:D0], M1[:, 0:T].rearrange("p (k h d) -> p k h d", k=NQB, h=H0),
                                         ACT.Copy).then_inc(va_ready, 1)
        iterations(act, run)

    def vector(dve, then):
        def run(p):
            for s in range(UNITS):
                a = p["a"]
                if s == 2 and a:
                    dve.wait_ge(stats_done, a.n + 1)
                    need(dve, rstd_ready, a.n)
                    need(dve, normed, a.n)
                if p["b"]:
                    b = p["b"]
                    qb, tp, hh = unit(s)
                    dve.wait_ge(smax_ready, b.n * UNITS + s + 1)
                    if s == 0:
                        need(dve, mparts_ready, b.n)
                    nc.vector.tensor_reduce(mx[:, qb, NTILE * hh + 2 * tp:NTILE * hh + 2 * tp + 2], SM[hh][:, :].rearrange("p (a t) -> p a t", a=2),
                                            AX_X, ALU.max, negate=True).then_inc(max_done, 1)
                if s == 1 and a:
                    dve.wait_ge(tokens_ready, a.n + 1)
                    need(dve, aggr_done, a.n)
                    for j in range(4):
                        last = nc.vector.bn_stats(stats[:, j, :], m0[:, j, :])
                    last.then_inc(stats_done, 1)
                if s == 2 and a:
                    for j in range(4):
                        last = nc.vector.bn_aggr(mv[:, j, :], stats[:, j, :])
                    last.then_inc(aggr_done, 1)
                if s == 4 and a:
                    dve.wait_ge(rstd_ready, a.n + 1)
                    need(dve, channels_ready, a.n)
                    for j in range(4):
                        last = nc.vector.tensor_scalar(xn[:, j, :], m0[:, j, :], mv[:, j, 0:1], rstd[:, j:j + 1], ALU.subtract, ALU.mult)
                    last.then_inc(normed, 1)
                if s == 12 and a:
                    dve.wait_ge(part1_done, a.n + 1)
                    need(dve, part3_done, a.n)
                    nc.vector.tensor_tensor(rest[:, :, :], M0[:, :].rearrange("p (w t) -> p w t", w=2),
                                            parts[a.slot][:, :, 0, :], ALU.subtract).then_inc(rest_done, 1)
                if s == UNITS - 1 and p["b"]:
                    b = p["b"]
                    dve.wait_ge(max_done, b.n * UNITS + UNITS)
                    need(dve, mT_psum, b.n)
                    nc.vector.tensor_copy(mparts[:, :, 0, :], mx[:, :, :]).then_inc(mhigh_done, 1)
                    dve.wait_ge(mhigh_done, b.n + 1)
                    nc.vector.tensor_tensor(mparts[:, :, 1, :], mx[:, :, :], mparts[:, :, 0, :], ALU.subtract).then_inc(mparts_ready, 1)
        iterations(dve, run, then)

    def gpsimd(pool):
        def run(p):
            a, x = p["a"], p["x"]
            if a:
                pool.wait_ge(aggr_done, a.n + 1)
                need(pool, normed, a.n)
                nc.gpsimd.tensor_tensor(rstd[:, :], mv[:, :, 1], epst[:, 0:4], ALU.add).then_inc(var_done, 1)
                pool.wait_ge(var_done, a.n + 1)
                nc.gpsimd.tensor_tensor(rstd[:, :], rstd[:, :], half[:, 0:4], ALU.pow).then_inc(rstd_ready, 1)
            if x:
                pool.wait_ge(x_in[x.slot], x.use * 16 + 16)
                if isinstance(x.n, int) and x.n == 0:
                    pool.wait_ge(consts_in, NCONST)
                need(pool, tokens_ready, x.n - 1)
                nc.gpsimd.tensor_tensor(xpe[x.slot][:, :, :], xin[x.slot][:, :, :], pe_tab[:, :, :], ALU.add).then_inc(pos_added, 1)
            if a:
                pool.wait_ge(rest_done, a.n + 1)
                part = parts[a.slot]
                nc.gpsimd.tensor_tensor(part[:, :, 1, :], rest[:, :, :], zero[:, :, :].broadcast_to((128, 2, T)), ALU.add).then_inc(part2_done, 1)
                pool.wait_ge(part2_done, a.n + 1)
                nc.gpsimd.tensor_tensor(part[:, :, 2, :], rest[:, :, :], part[:, :, 1, :], ALU.subtract).then_inc(part3_done, 1)
        iterations(pool, run)

    def stored(engine, batches):
        for k in range(SLOTS):
            engine.wait_ge(raw_out[k], batches // SLOTS * RAW_OUT)
            engine.wait_ge(q_kept[k], batches // SLOTS * 16)

    def tables(sp):
        sp.dma_start(pe_tab[:, :, :], W["pos"].unsqueeze(1).broadcast_to((128, 2, T))).then_inc(consts_in, 16)
        for dst, src in ((wq, "L0_xattn_Wq"), (wk, "L0_xattn_Wk"), (wv, "L0_xattn_Wv")):
            sp.dma_start(dst[:, :], W[src]).then_inc(consts_in, 16)
        sp.dma_start(lnc[:, :], W["ln"]).then_inc(consts_in, 16)

    def sync(sp, then):
        def run(p):
            a, t, l = p["a"], p["t"], p["l"]
            raw_dst = scr["raw"][bass.ds(t.n, 1), :, :, :].rearrange("o p g q -> (o p) g q") if t else None
            q_dst = scr["q"][bass.ds(a.n, 1), :, :].rearrange("o c t -> (o c) t") if a else None
            if l:
                sp.wait_ge(stack_out[l.slot], l.use * STACK_OUT + STACK_OUT)
                need(sp, scores_ready, l.n * UNITS - (SLOTS - 1) * UNITS)
                if isinstance(l.n, int) and l.n < SLOTS:
                    sp.wait_ge(stack_set, 2 * SLOTS)
                for w in range(2):
                    view = scr["stack"][l.slot, w].rearrange("(hh t d) m q -> hh (d m) t q", hh=2, d=D0)
                    for hh in range(2):
                        rows = slice(64 * hh, 64 * hh + ROWS)
                        dst = KS[l.slot][rows, :, :] if w else QS[l.slot][rows, hh, :, :]
                        sp.dma_start(dst, view[hh]).then_inc(stack_in[l.slot], 16)
            if t:
                sp.wait_ge(raw_ready, t.n * 2 + 2)
                sp.dma_start(raw_dst, raw[t.slot][:, :, :]).then_inc(raw_out[t.slot], 16)
            if a:
                sp.wait_ge(qkvT_ready, a.n + 1)
                sp.dma_start(q_dst, qkvT[a.slot][:, 0, :]).then_inc(q_kept[a.slot], 16)
                need(sp, stack_in[a.slot], a.use * STACK_IN)
                sp.wait_ge(part3_done, a.n + 1)
                dst, part = scr["stack"][a.slot], parts[a.slot]
                for w, m, n, p0 in ((0, 0, 3, 0), (0, 3, 2, 1), (0, 5, 1, 2), (1, 0, 3, None), (1, 3, 2, None), (1, 5, 1, None)):
                    src = part[:, w, 0:n, :] if p0 is None else part[:, w, p0:p0 + 1, :].broadcast_to((128, n, T))
                    sp.dma_start(dst[w, :, m:m + n, :], src).then_inc(stack_out[a.slot], 16)
        iterations(sp, run, then)
        stored(sp, NB)

    def clear(dve):
        for k in range(SLOTS):
            nc.vector.memset(KS[k][:, :, :], 1.0).then_inc(stack_set, 1)
            nc.vector.memset(VA[k][:, :, :, :], 0.0).then_inc(va_set, 1)
        dve.wait_ge(va_set, SLOTS)
        for k in range(SLOTS):
            nc.vector.memset(VA[k][:, :, :, D0:D0 + 1], 1.0).then_inc(va_set, 1)

    return {"tensor": tensor, "scalar": scalar, "vector": vector, "gpsimd": gpsimd, "sync": sync, "clear": clear, "tables": tables, "stored": stored}


FP = 2
NPAIR = NB // FP
F0 = 2 * C // 128
DEN_CHUNKS = ((0, 12), (12, 16))


class Pair:

    def __init__(self, it, c):
        self.n = it * 2 + c
        self.slot = c % 2
        self.use = it + c // 2


def feed_forward(nc, env):
    sb, pb, sem, W, scr = env["sb"], env["pb"], env["sem"], env["in"], env["dram"]
    ident, half, epst = env["ident"], env["half"], env["epst"]
    wo, w1, w2, fvec = env["f_wo"], env["f_w1"], env["f_w2"], env["f_vec"]

    keep = env["keep"]
    den = [keep(f"den{k}", [128, 512], F32) for k in range(len(DEN_CHUNKS))]
    ctx_t = [keep(f"f_ctx{s}", [128, FP, T], F32) for s in range(2)]
    rden = [keep(f"f_rden{s}", [128, FP, T], F32) for s in range(2)]
    q_t = [keep(f"f_q{s}", [128, FP, T], F32) for s in range(2)]
    cn = [sb(f"f_cn{s}", [128, FP * T], F32) for s in range(2)]
    xn = sb("f_xn", [128, 4, 128], F32)
    hT = [sb(f"f_h{s}", [128, FP * T], F32) for s in range(2)]
    ge = [sb(f"f_ge{s}", [128, F0, FP * T], F32) for s in range(2)]
    o = [sb(f"f_o{s}", [128, FP, T], F32) for s in range(2)]
    r = [sb(f"f_res{s}", [128, FP * T], F32) for s in range(2)]
    rk = [sb(f"f_resk{s}", [128, FP * T], F32) for s in range(2)]
    stats, mv, rstd = sb("f_stats", [128, 4, 6], F32), sb("f_mv", [128, 4, 2], F32), sb("f_rstd", [128, 4], F32)
    first = sb("f_first", [128, 1], F32)
    Y, T1, T2, FF, O = pb[0], (pb[1], pb[6]), pb[2], pb[3:5], pb[5]
    t2 = T2[:, :].rearrange("p (a t) -> p a t", a=4)
    t1 = [bank[:, :].rearrange("p (a t) -> p a t", a=4) for bank in T1]

    den_in, den_done, den_out = sem("den_in"), sem("den_done"), sem("den_out")
    f_in = [sem(f"f_in{s}") for s in range(2)]
    f_kept = [sem(f"f_kept{s}") for s in range(2)]
    f_ctx, f_y, f_r, f_tok = sem("f_ctx_ready"), sem("f_y_ready"), sem("f_r_ready"), sem("f_tokens_ready")
    f_stats, f_aggr, f_var, f_rstd = sem("f_stats_done"), sem("f_aggr_done"), sem("f_var_done"), sem("f_rstd_ready")
    f_normed, f_chan, f_h = sem("f_normed"), sem("f_channels_ready"), sem("f_h_ready")
    f_hid, f_ge, f_ff, f_out, f_rk = sem("f_hidden_ready"), sem("f_gelu_ready"), sem("f_ff_ready"), sem("f_out_ready"), sem("f_r_biased")
    IN = 6 * 16

    def plan(it, c, static):
        def pair(off):
            return Pair(it, c + off) if not static or 0 <= c + off < NPAIR else None
        return pair(1), pair(0), pair(-1), pair(-2)

    def iterations(engine, run, then):
        for v in (0, 1):
            run(*plan(0, v, True))
            for step in then.get(v, ()):
                step()
        with engine.Fori(1, NPAIR // 2 - 1) as it:
            for c in (0, 1):
                run(*plan(it, c, False))
        for v in range(NPAIR - 2, NPAIR + 2):
            run(*plan(0, v, True))
            for step in then.get(v, ()):
                step()

    def load_denominators(sp, k):
        b0, b1 = DEN_CHUNKS[k]
        n = 4 * (b1 - b0)
        for g2 in range(2):
            src = scr["raw"][b0:b1].rearrange("b (j r) g q -> (b j) r g q", j=4)[:, D0, 2 * g2:2 * g2 + 2, :]
            sp.dma_start(den[k][n * g2:n * g2 + n, :].rearrange("p (g q) -> p g q", g=2), src).then_inc(den_in, 16)

    def store_reciprocals(sp, k):
        b0, b1 = DEN_CHUNKS[k]
        n = 4 * (b1 - b0)
        sp.wait_ge(den_done, k + 1)
        view = scr["rden"][b0:b1].rearrange("b j d (h g) q -> h (b j) d (g q)", h=2)
        for g2 in range(2):
            sp.dma_start(view[g2], den[k][n * g2:n * g2 + n, :].unsqueeze(1).broadcast_to((n, D0, 512))).then_inc(den_out, 16)

    def load(sp, a):
        raw = scr["raw"][bass.ds(a.n * 2, 2), :, :, :].rearrange("b (j r) g q -> j r g b q", j=4)
        src_r = scr["rden"][bass.ds(a.n * 2, 2)].rearrange("b j d g q -> (j d g) b q")
        src_q = scr["q"][bass.ds(a.n * 2, 2), :, :].rearrange("b c q -> c b q")
        need(sp, f_ctx, a.n - 1)
        need(sp, f_r, a.n - 1)
        for j in range(4):
            sp.dma_start(ctx_t[a.slot][32 * j:32 * j + 32, :, :], raw[j, 0:D0].rearrange("r g b q -> (r g) b q")).then_inc(f_in[a.slot], 16)
        sp.dma_start(rden[a.slot][:, :, :], src_r).then_inc(f_in[a.slot], 16)
        sp.dma_start(q_t[a.slot][:, :, :], src_q).then_inc(f_in[a.slot], 16)

    def early_denominators(sp):
        load_denominators(sp, 0)
        store_reciprocals(sp, 0)

    def early_pairs(sp):
        sp.wait_ge(den_out, 32)
        load(sp, Pair(0, 0))
        load(sp, Pair(0, 1))

    def sync(sp):
        load_denominators(sp, 1)
        with sp.Fori(1, NPAIR // 2 - 1) as it:
            for c in (0, 1):
                load(sp, Pair(it, c))
        store_reciprocals(sp, 1)
        sp.wait_ge(den_out, 64)
        for c in (NPAIR - 2, NPAIR - 1):
            load(sp, Pair(0, c))

    def kept(engine, pairs):
        for k in range(2):
            need(engine, f_kept[k], (pairs + 1 - k) // 2 * 16)

    def gpsimd(pool, then):
        def context(a):
            pool.wait_ge(f_in[a.slot], a.use * IN + IN)
            need(pool, f_y, a.n - 1)
            nc.gpsimd.tensor_tensor(cn[a.slot][:, :], ctx_t[a.slot][:, :, :].rearrange("p b q -> p (b q)"),
                                    rden[a.slot][:, :, :].rearrange("p b q -> p (b q)"), ALU.mult).then_inc(f_ctx, 1)

        def run(nxt, a, b, c):
            if nxt:
                context(nxt)
            if a:
                pool.wait_ge(f_aggr, a.n + 1)
                nc.gpsimd.tensor_tensor(rstd[:, :], mv[:, :, 1], epst[:, 0:4], ALU.add).then_inc(f_var, 1)
                pool.wait_ge(f_var, a.n + 1)
                nc.gpsimd.tensor_tensor(rstd[:, :], rstd[:, :], half[:, 0:4], ALU.pow).then_inc(f_rstd, 1)
        context(Pair(0, 0))
        iterations(pool, run, then)

    def tensor(pe, then):
        def run(nxt, a, b, c):
            if a:
                pe.wait_ge(f_ctx, a.n + 1)
                need(pe, f_r, a.n)
                nc.tensor.matmul(Y[:, :], wo[:, :], cn[a.slot][:, :], start=True, stop=True).then_inc(f_y, 1)
            if b:
                pe.wait_ge(f_normed, b.n + 1)
                need(pe, f_h, b.n)
                for j in range(4):
                    last = nc.tensor.transpose(t2[:, j, :], xn[:, j, :], ident[:, :])
                last.then_inc(f_chan, 1)
            if a:
                need(pe, f_normed, a.n - 1)
                pe.wait_ge(f_r, a.n + 1)
                for j in range(4):
                    last = nc.tensor.transpose(t1[a.slot][:, j, :], r[a.slot][:, j * 128:(j + 1) * 128], ident[:, :])
                last.then_inc(f_tok, 1)
            if c:
                pe.wait_ge(f_ge, c.n + 1)
                need(pe, f_out, c.n)
                for f in range(F0):
                    last = nc.tensor.matmul(O[:, :], w2[:, f, :], ge[c.slot][:, f, :], start=(f == 0), stop=(f == F0 - 1))
                last.then_inc(f_ff, 1)
            if b:
                pe.wait_ge(f_h, b.n + 1)
                need(pe, f_ge, b.n)
                for f in range(F0):
                    last = nc.tensor.matmul(FF[f][:, :], w1[:, f * 128:(f + 1) * 128], hT[b.slot][:, :], start=True, stop=True)
                last.then_inc(f_hid, 1)
        iterations(pe, run, then)

    def scalar(act, then):
        def run(nxt, a, b, c):
            if b:
                act.wait_ge(f_chan, b.n + 1)
                nc.scalar.activation(hT[b.slot][:, :], T2[:, :], ACT.Identity, bias=fvec[:, 1:2], scale=fvec[:, 0:1]).then_inc(f_h, 1)
            if b:
                act.wait_ge(f_hid, b.n + 1)
                need(act, f_ff, b.n - 1)
                for f in range(F0):
                    last = nc.scalar.activation(ge[b.slot][:, f, :], FF[f][:, :], ACT.Gelu, bias=fvec[:, 3 + f:4 + f])
                last.then_inc(f_ge, 1)
            if c:
                act.wait_ge(f_out, c.n + 1)
                act.dma_start(scr["x1"][bass.ds(c.n * 2, 2), :, :].rearrange("b c q -> c b q"), o[c.slot][:, :, :]).then_inc(f_kept[c.slot], 16)
        iterations(act, run, then)

    def invert(dve, k):
        n = 8 * (DEN_CHUNKS[k][1] - DEN_CHUNKS[k][0])
        dve.wait_ge(den_in, 32 * k + 32)
        nc.vector.reciprocal(den[k][0:n, :], den[k][0:n, :]).then_inc(den_done, 1)

    def vector(dve, then):

        def run(nxt, a, b, c):
            if a:
                dve.wait_ge(f_y, a.n + 1)
                nc.vector.tensor_tensor(r[a.slot][:, :], Y[:, :], q_t[a.slot][:, :, :].rearrange("p b q -> p (b q)"), ALU.add).then_inc(f_r, 1)
                dve.wait_ge(f_tok, a.n + 1)
                for j in range(4):
                    last = nc.vector.bn_stats(stats[:, j, :], t1[a.slot][:, j, :])
                last.then_inc(f_stats, 1)
                dve.wait_ge(f_stats, a.n + 1)
                need(dve, f_rstd, a.n)
                need(dve, f_normed, a.n)
                nc.vector.tensor_copy(first[:, :], stats[:, 3, 0:1])
                for j in range(4):
                    last = nc.vector.bn_aggr(mv[:, j, :], stats[:, j, :])
                last.then_inc(f_aggr, 1)
            if c:
                dve.wait_ge(f_ff, c.n + 1)
                dve.wait_ge(f_rk, c.n + 1)
                need(dve, f_kept[c.slot], c.use * 16)
                nc.vector.tensor_tensor(o[c.slot][:, :, :].rearrange("p b q -> p (b q)"), O[:, :], rk[c.slot][:, :], ALU.add).then_inc(f_out, 1)
            if a:
                need(dve, f_out, a.n - 1)
                dve.wait_ge(f_r, a.n + 1)
                nc.vector.tensor_scalar(rk[a.slot][:, :], r[a.slot][:, :], fvec[:, 2:3], None, ALU.add).then_inc(f_rk, 1)
                dve.wait_ge(f_rstd, a.n + 1)
                need(dve, f_chan, a.n)
                for j in range(4):
                    last = nc.vector.tensor_scalar(xn[:, j, :], t1[a.slot][:, j, :], mv[:, j, 0:1], rstd[:, j:j + 1], ALU.subtract, ALU.mult)
                last.then_inc(f_normed, 1)
        iterations(dve, run, {1: [lambda: invert(dve, 1)], **then})

    return {"tensor": tensor, "scalar": scalar, "vector": vector, "gpsimd": gpsimd, "sync": sync,
            "early_denominators": early_denominators, "early_pairs": early_pairs, "invert": invert, "kept": kept}


L1, E1, H1, S1 = 128, 256, 32, 8
EB = E1 // 128
GB = 2
NG = NB // GB
NMIX, DM, DD = 5, 32, 64
JH = 4
VECS = ("ln1_w", "ln1_b", "maa_x", "stack0", "stack1", "stack2", "stack3", "stack4", "time_decay", "u", "gn_w", "gn_b",
        "ln2_w", "ln2_b", "ffn_maa_k", "ffn_maa_r")
MIX_K, MIX_W, MIX_V, MIX_R, MIX_G = range(NMIX)
MIX_ORDER = (MIX_W, MIX_K, MIX_V, MIX_R, MIX_G)


def early_tiles(keep):
    N = GB * L1
    x_in = [keep(f"g_xin{i}", [128, GB, E1], F32) for i in range(2)]
    st1 = [keep(f"g_st1_{i}", [128, EB, GB], F32) for i in range(2)]
    xn, sx = keep("g_xn", [128, GB, E1], F32), [keep(f"g_sx{i}", [128, EB, N], F32) for i in range(2)]
    xa = [keep(f"g_xa_{i}", [128, EB, GB, L1 + 1], F32) for i in range(2)]
    mixin = keep("g_mixin", [128, EB, N], F32)
    th5, th5b = keep("g_th5", [128, N], F32), keep("g_th5b", [DM, N], F32)
    norms = [(keep(f"g_stats{i}", [128, GB, 6], F32), keep(f"g_mv{i}", [128, GB, 2], F32), keep(f"g_rstd{i}", [128, GB], F32)) for i in range(2)]
    return x_in, st1, xn, sx, xa, mixin, th5, th5b, norms


def recurrent(nc, env):
    sb, pb, sem, W, scr = env["sb"], env["pb"], env["sem"], env["in"], env["dram"]
    ident, half, epst = env["ident"], env["half"], env["epst"]
    w, vec, hvec = env["g_w"], env["g_vec"], env["g_hvec"]
    maa1, maa2, maa2b, td1, td2 = env["g_maa1"], env["g_maa2"], env["g_maa2b"], env["g_td1"], env["g_td2"]
    headsum, centre, headmean, hsel = env["g_headsum"], env["g_centre"], env["g_headmean"], env["g_hsel"]
    N = GB * L1

    def v(name, eb):
        return vec[:, eb, VECS.index(name):VECS.index(name) + 1]

    def t3(name):
        return sb(name, [128, EB, N], F32)

    def two(name):
        return [t3(f"{name}{i}") for i in range(2)]

    def bl(ap):
        return ap.rearrange("p (b l) -> p b l", b=GB)

    def cols(tile):
        return tile[:, :, :].rearrange("p a n -> p (a n)")

    x_in, st1, xn, sx, xa, mixin, th5, th5b, norms = env["early_tiles"]
    NZ = 4
    z = [sb(f"g_z{i}", [128, N], F32) for i in range(NZ)]
    xm = [two(f"g_xm{f}_") if f == MIX_G else [t3(f"g_xm{f}")] * 2 for f in range(NMIX)]
    tdh = sb("g_tdh", [DD, N], F32)
    ew = t3("g_ew")
    wS, kT, vT, rT = two("g_wS"), two("g_k"), two("g_v"), two("g_r")
    s0 = [sb(f"g_s0_{i}", [128, EB, S1, GB], F32) for i in range(2)]
    UN = [(hb, jq) for jq in range(S1 // JH) for hb in range(EB)]
    NU = len(UN)
    vbc = [sb(f"g_vbc{i}", [128, JH, N], F32) for i in range(NU)]
    aS = [sb(f"g_a{i}", [128, JH, N], F32) for i in range(2)]
    SS = [sb(f"g_S{i}", [128, JH, N], F32) for i in range(2)]
    gth, ruk = t3("g_gth"), t3("g_ruk")
    gs, og = two("g_gs"), two("g_og")
    xres = [sb(f"g_xres{i}", [128, GB, E1], F32) for i in range(2)]
    st0 = [sb(f"g_st0_{i}", [128, EB, GB], F32) for i in range(2)]
    cent, sq, on, gated = t3("g_cent"), t3("g_sq"), t3("g_on"), t3("g_gated")
    sd, rg, rgT = sb("g_sd", [128, GB * H1], F32), sb("g_rg", [128, GB, H1], F32), sb("g_rgT", [H1, N], F32)
    x1 = sb("g_x1", [128, GB, E1], F32)
    xn2, xa2, sx2 = sb("g_xn2", [128, GB, E1], F32), sb("g_xa2", [128, EB, GB, L1 + 1], F32), t3("g_sx2t")
    xk, xr, kk = t3("g_xk"), t3("g_xr"), t3("g_kk")
    th2, y = sb("g_th2", [128, GB, E1], F32), sb("g_y", [128, GB, E1], F32)
    out_t = [sb(f"g_out{i}", [128, GB, E1], F32) for i in range(2)]

    def pair(bank):
        return bank[:, :].rearrange("p (a n) -> p a n", a=EB)
    FEAT, MIX, PROJ_A, PROJ_B, STATE, T6, T7 = pb[0], pb[1:3], pb[3], pb[4], pb[5], pb[6], pb[7]

    def feat(g):
        return T7 if isinstance(g.n, int) and g.n == 0 else FEAT

    NM = NMIX * EB
    def mix_bank(g, i):
        return pair(MIX[((g.slot * NM + i) // EB) % 2])[:, i % EB, :]

    def mix_buffer(g, i):
        return z[(g.slot * NM + i) % NZ][:, :]

    decay_set = sem("g_decay_set")
    x_ready, res_ready, s0_ready = ([sem(f"g_{k}{i}") for i in range(2)] for k in ("x_ready", "res_ready", "s0_ready"))
    g_out, g_vout = [sem(f"g_out{i}") for i in range(2)], [sem(f"g_vout{i}") for i in range(2)]
    g_vin = [sem(f"g_vin{i}") for i in range(NU)]
    names = ("stats aggr var rstd normed feat xa edge sx mixin maa th5 xxx z xm proj evac projg gth gsd ewd kv edge2 scan rs summed ruk cb "
             "cv og cent sq var2 sd vg rgt rgtc rb on on2 gated wo x1 "
             "stats2 aggr2 var3 rstd2 normed2 feat2 xc edgec sx2 xk kkp kkr kk rrp th2 fvp y fin").split()
    s = {n: sem("g_" + n) for n in names}
    PJ = 5
    J_HID, J_DECAY, J_K, J_V, J_R = range(PJ)

    def plan(it, c, static):
        def group(off):
            return Pair(it, c + off) if not static or 0 <= c + off < NG else None
        return group(2), group(1) if not (static and c == -1) else None, group(0), group(-1), group(-2)

    def iterations(engine, run):
        for c in range(-1, 4):
            run(*plan(0, c, True))
        with engine.Fori(2, NG // 2 - 1) as it:
            for c in (0, 1):
                run(*plan(it, c, False))
        for c in range(NG - 2, NG + 2):
            run(*plan(0, c, True))

    first = Pair(0, 0)

    def sync(sp, kept):
        def x_rows(g):
            return scr["x1"][bass.ds(g.n * GB, GB), :, :].rearrange("b l e -> l b e")

        def small(name, g):
            return W[name][bass.ds(g.n, 1), :, :].rearrange("o p x -> (o p) x")

        def load_front(g):
            src, src_st = x_rows(g), small("st1", g)
            need(sp, s["edge"], g.n - 1)
            need(sp, s["normed"], g.n - 1)
            sp.dma_start(x_in[g.slot][:, :, :], src).then_inc(x_ready[g.slot], 16)
            sp.dma_start(st1[g.slot][:, :, :].rearrange("p a b -> p (a b)"), src_st).then_inc(x_ready[g.slot], 16)

        def run(x, e, f, m, t):
            if m:
                src, src_st = x_rows(m), small("st0", m)
                need(sp, s["edgec"], m.n - 1)
                need(sp, s["x1"], m.n - 1)
                sp.dma_start(xres[m.slot][:, :, :], src).then_inc(res_ready[m.slot], 16)
                sp.dma_start(st0[m.slot][:, :, :].rearrange("p a b -> p (a b)"), src_st).then_inc(res_ready[m.slot], 16)
            if x:
                load_front(x)
            if f:
                src = small("s0", f)
                need(sp, s["edge2"], f.n * NU - NU)
                sp.dma_start(s0[f.slot][:, :, :, :].rearrange("p a j b -> p (a j b)"), src).then_inc(s0_ready[f.slot], 16)
                sp.wait_ge(s["evac"], f.n * PJ + J_V + 1)
                for jl in range(JH):
                    sp.dma_start(scr["v"][f.slot, :, :, jl, :], vT[f.slot][H1 * jl:H1 * jl + H1, :, :]).then_inc(g_vout[f.slot], 16)
                sp.wait_ge(g_vout[f.slot], f.use * 16 * JH + 16 * JH)
                for i, (hb, jq) in enumerate(UN):
                    need(sp, s["kv"], f.n * NU - NU + i + 1)
                    src = scr["v"][f.slot, 16 * hb:16 * hb + 16, jq].rearrange("h j n -> h (j n)")
                    sp.dma_start(vbc[i][:, :, :].rearrange("p j n -> p (j n)"), src.unsqueeze(1).broadcast_to((16, S1, JH * N))).then_inc(g_vin[i], 16)
            if t:
                dst = W["out"][bass.ds(t.n * GB, GB), :, :].rearrange("b l e -> l b e")
                sp.wait_ge(s["fin"], t.n + 1)
                sp.dma_start(dst, out_t[t.slot][:, :, :]).then_inc(g_out[t.slot], 16)
        kept(sp, 1)
        load_front(Pair(0, 0))
        kept(sp, NPAIR)
        iterations(sp, run)
        for i in range(2):
            sp.wait_ge(g_out[i], NG // 2 * 16)

    def gpsimd(pool):
        def rsqrt(n, i, aggr, var, done):
            _, mv, rstd = norms[i]
            pool.wait_ge(s[aggr], n + 1)
            nc.gpsimd.tensor_tensor(rstd[:, :], mv[:, :, 1], epst[:, 0:GB], ALU.add).then_inc(s[var], 1)
            pool.wait_ge(s[var], n + 1)
            nc.gpsimd.tensor_tensor(rstd[:, :], rstd[:, :], half[:, 0:GB], ALU.pow).then_inc(s[done], 1)

        def shift(n, src, dst, ready, edge, done):
            pool.wait_ge(s[ready], n + 1)
            pool.wait_ge(s[edge], n + 1)
            for eb in range(EB):
                last = nc.gpsimd.tensor_tensor(bl(dst[:, eb, :]), src[:, eb, :, 0:L1], src[:, eb, :, 1:L1 + 1], ALU.subtract)
            last.then_inc(s[done], 1)

        def scale(e):
            rsqrt(e.n, 0, "aggr", "var", "rstd")

        def difference(e):
            need(pool, s["z"], e.n * NM - NM)
            need(pool, s["mixin"], e.n - 1)
            shift(e.n, xa[e.slot], sx[e.slot], "xa", "edge", "sx")

        def run(x, e, f, m, t):
            def mixed(i0, i1):
                if not f:
                    return
                for i in range(i0, i1):
                    mix, eb = MIX_ORDER[i // EB], i % EB
                    pool.wait_ge(s["z"], f.n * NM + i + 1)
                    nc.gpsimd.tensor_tensor(bl(xm[mix][f.slot][:, eb, :]), bl(mix_buffer(f, i)), xa[f.slot][:, eb, :, 1:L1 + 1], ALU.add).then_inc(s["xm"], 1)

            def key_value(i):
                if not m:
                    return
                hb = UN[i][0]
                if i == 0:
                    pool.wait_ge(s["evac"], m.n * PJ + J_K + 1)
                pool.wait_ge(g_vin[i], m.n * 16 + 16)
                need(pool, s["summed"], m.n * NU + i - 1)
                key = bl(kT[m.slot][:, hb, :])[:, :, 0:L1 - 1].unsqueeze(1).broadcast_to((128, JH, GB, L1 - 1))
                a4 = aS[i % 2][:, :, :].rearrange("p j (b l) -> p j b l", b=GB)
                v4 = vbc[i][:, :, :].rearrange("p j (b l) -> p j b l", b=GB)
                nc.gpsimd.tensor_tensor(a4[:, :, :, 1:L1], v4[:, :, :, 0:L1 - 1], key, ALU.mult).then_inc(s["kv"], 1)

            key_value(0)
            if f:
                need(pool, s["proj"], f.n * PJ)
                need(pool, s["projg"], f.n - 1)
            mixed(0, 4)
            key_value(1)
            if t:
                pool.wait_ge(s["on2"], t.n + 1)
                pool.wait_ge(s["gsd"], t.n * EB + EB)
                need(pool, s["wo"], t.n)
                nc.gpsimd.tensor_tensor(gated[:, :, :], on[:, :, :], gs[t.slot][:, :, :], ALU.mult).then_inc(s["gated"], 1)
            if e:
                scale(e)
            mixed(4, 6)
            key_value(2)
            if t:
                rsqrt(t.n, 1, "aggr2", "var3", "rstd2")
            mixed(6, 8)
            if e:
                difference(e)
            if t:
                need(pool, s["xk"], t.n)
                shift(t.n, xa2, sx2, "xc", "edgec", "sx2")
            key_value(3)
            mixed(8, 10)
        return {NPAIR - 1: [lambda: scale(first)], NPAIR + 1: [lambda: difference(first)]}, lambda: iterations(pool, run)

    def tensor(pe):
        def to_features(src, bank, ready, n, done):
            pe.wait_ge(s[ready], n + 1)
            for eb in range(EB):
                for b in range(GB):
                    last = nc.tensor.transpose(bank[:, eb * N + b * L1:eb * N + (b + 1) * L1], src[:, b, eb * 128:(eb + 1) * 128], ident[:, :])
            last.then_inc(s[done], 1)

        def features(e):
            need(pe, s["th5"], e.n)
            to_features(xn, feat(e), "normed", e.n, "feat")

        def mixing(e):
            pe.wait_ge(s["mixin"], e.n + 1)
            for eb in range(EB):
                nc.tensor.matmul(feat(e)[:, 0:N], maa1[:, eb, 0:128], mixin[:, eb, :], start=(eb == 0), stop=(eb == EB - 1))
            for eb in range(EB):
                last = nc.tensor.matmul(feat(e)[0:DM, N:2 * N], maa1[:, eb, 128:160], mixin[:, eb, :], start=(eb == 0), stop=(eb == EB - 1))
            last.then_inc(s["maa"], 1)

        def run(x, e, f, m, t):
            def mixes(mix):
                i0 = MIX_ORDER.index(mix) * EB
                need(pe, s["z"], f.n * NM + i0 - EB)
                for i in range(i0, i0 + EB):
                    eb = i - i0
                    if mix == 4:
                        last = nc.tensor.matmul(mix_bank(f, i), maa2b[:, eb * 128:(eb + 1) * 128], th5b[:, :], start=True, stop=True)
                    else:
                        r = slice(DM * mix, DM * mix + DM)
                        last = nc.tensor.matmul(mix_bank(f, i), maa2[r, eb * 128:(eb + 1) * 128], th5[r, :], start=True, stop=True, tile_position=(DM * mix, 0))
                last.then_inc(s["xxx"], 1)

            def project(g, mix, wt, bank, done):
                pe.wait_ge(s["xm"], g.n * NM + (MIX_ORDER.index(mix) + 1) * EB)
                for ob in range(EB):
                    for eb in range(EB):
                        last = nc.tensor.matmul(pair(bank)[:, ob, :], wt[:, eb, ob * 128:(ob + 1) * 128], xm[mix][g.slot][:, eb, :],
                                                start=(eb == 0), stop=(eb == EB - 1))
                last.then_inc(s[done], 1)

            def sums(i):
                if not m:
                    return
                hb, jq = UN[i]
                if i == 0:
                    pe.wait_ge(s["cv"], m.n + 1)
                pe.wait_ge(s["rs"], m.n * NU + i + 1)
                for j in range(JH):
                    last = nc.tensor.matmul(pair(STATE)[H1 * j:H1 * j + H1, jq, :], headsum[:, hb, 0:H1], aS[i % 2][:, j, :],
                                            start=(hb == 0), stop=(hb == EB - 1))
                last.then_inc(s["summed"], 1)

            def to_positions(src, wt, bank, done):
                for b in range(GB):
                    for eb in range(EB):
                        last = nc.tensor.matmul(bank[:, b * E1:(b + 1) * E1], src[:, eb, b * L1:(b + 1) * L1], wt[:, eb, :],
                                                start=(eb == 0), stop=(eb == EB - 1))
                last.then_inc(s[done], 1)

            if t:
                pe.wait_ge(s["og"], t.n + 1)
                need(pe, s["th2"], t.n)
                for jq in range(EB):
                    for k in range(EB):
                        last = nc.tensor.matmul(pair(T6)[:, jq, :], centre[:, (k != jq) * 1, :], og[t.slot][:, k, :], start=(k == 0), stop=(k == EB - 1))
                last.then_inc(s["cent"], 1)
            if f:
                pe.wait_ge(s["th5"], f.n + 1)
                mixes(MIX_W)
                mixes(MIX_K)
            if t:
                pe.wait_ge(s["sq"], t.n + 1)
                need(pe, s["y"], t.n)
                for b in range(GB):
                    for jq in range(EB):
                        last = nc.tensor.matmul(T7[:, b * H1:(b + 1) * H1], sq[:, jq, b * L1:(b + 1) * L1], headmean[:, :],
                                                start=(jq == 0), stop=(jq == EB - 1))
                last.then_inc(s["var2"], 1)
            if m:
                pe.wait_ge(s["ruk"], m.n + 1)
                need(pe, s["og"], m.n)
                for hb in range(EB):
                    last = nc.tensor.matmul(pair(STATE)[:, 0, :], headsum[:, hb, :], ruk[:, hb, :], start=(hb == 0), stop=(hb == EB - 1))
                last.then_inc(s["cb"], 1)
                pe.wait_ge(s["evac"], m.n * PJ + J_V + 1)
                project(m, MIX_G, w["Wg"], PROJ_B, "projg")
            if f:
                mixes(MIX_V)
                pe.wait_ge(s["xm"], f.n * NM + EB)
                need(pe, s["evac"], f.n * PJ)
                for eb in range(EB):
                    last = nc.tensor.matmul(PROJ_A[0:DD, 0:N], td1[:, eb, :], xm[MIX_W][0][:, eb, :], start=(eb == 0), stop=(eb == EB - 1))
                last.then_inc(s["proj"], 1)
            if t:
                pe.wait_ge(s["vg"], t.n + 1)
                for b in range(GB):
                    last = nc.tensor.transpose(T7[0:H1, N + b * L1:N + (b + 1) * L1], rg[:, b, :], ident[:, :])
                last.then_inc(s["rgt"], 1)
            sums(0)
            if t:
                pe.wait_ge(s["rgtc"], t.n + 1)
                nc.tensor.matmul(T6[:, 0:N], hsel[:, :], rgT[:, :], start=True, stop=True).then_inc(s["rb"], 1)
            if f:
                pe.wait_ge(s["evac"], f.n * PJ + J_HID + 1)
                need(pe, s["gsd"], f.n * EB)
                for ob in range(EB):
                    last = nc.tensor.matmul(pair(PROJ_B)[:, ob, :], td2[:, ob * 128:(ob + 1) * 128], tdh[:, :], start=True, stop=True)
                last.then_inc(s["proj"], 1)
                project(f, MIX_K, w["Wk"], PROJ_A, "proj")
            if f:
                mixes(MIX_R)
            if t:
                pe.wait_ge(s["gated"], t.n + 1)
                to_positions(gated, w["Wo"], T7, "wo")
            sums(1)
            if f:
                pe.wait_ge(s["evac"], f.n * PJ + J_DECAY + 1)
                project(f, MIX_V, w["Wv"], PROJ_B, "proj")
                mixes(MIX_G)
            if e:
                features(e)
            if t:
                to_features(xn2, T6, "normed2", t.n, "feat2")
            if f:
                pe.wait_ge(s["evac"], f.n * PJ + J_K + 1)
                project(f, MIX_R, w["Wr"], PROJ_A, "proj")
            sums(2)
            if e:
                mixing(e)
            if t:
                pe.wait_ge(s["xk"], t.n + 1)
                for ob in range(EB):
                    for eb in range(EB):
                        last = nc.tensor.matmul(pair(T7)[:, ob, :], w["Wfk"][:, eb, ob * 128:(ob + 1) * 128], xk[:, eb, :],
                                                start=(eb == 0), stop=(eb == EB - 1))
                last.then_inc(s["kkp"], 1)
                to_positions(xr, w["Wfr"], T6, "rrp")
            sums(3)
            if t:
                pe.wait_ge(s["kk"], t.n + 1)
                to_positions(kk, w["Wfv"], T7, "fvp")
        return {NPAIR: [lambda: features(first)], NPAIR + 1: [lambda: mixing(first)]}, lambda: iterations(pe, run)

    def scalar(act):
        def affine(e):
            need(act, s["sx"], e.n - 1)
            need(act, s["mixin"], e.n - 1)
            need(act, s["xm"], e.n * NM - NM)
            act.wait_ge(s["feat"], e.n + 1)
            for eb in range(EB):
                last = nc.scalar.activation(xa[e.slot][:, eb, :, 1:L1 + 1], bl(pair(feat(e))[:, eb, :]), ACT.Identity, bias=v("ln1_b", eb), scale=v("ln1_w", eb))
            last.then_inc(s["xa"], 1)

        def mixing_tanh(e):
            need(act, s["xxx"], e.n * NMIX)
            act.wait_ge(s["maa"], e.n + 1)
            nc.scalar.activation(th5b[:, :], feat(e)[0:DM, N:2 * N], ACT.Tanh)
            nc.scalar.activation(th5[:, :], feat(e)[:, 0:N], ACT.Tanh).then_inc(s["th5"], 1)

        def run(x, e, f, m, t):
            def ready(j):
                act.wait_ge(s["proj"], f.n * PJ + j + 1)

            if t:
                act.wait_ge(s["cent"], t.n + 1)
                need(act, s["var2"], t.n)
                nc.scalar.activation(cols(sq), T6[:, :], ACT.Square)
                need(act, s["on"], t.n)
                nc.scalar.activation(cols(cent), T6[:, :], ACT.Copy).then_inc(s["sq"], 1)
                need(act, s["vg"], t.n)
                act.wait_ge(s["var2"], t.n + 1)
                nc.scalar.activation(sd[:, :], T7[:, 0:GB * H1], ACT.Sqrt, bias=epst[:, 0:1]).then_inc(s["sd"], 1)
            if m:
                need(act, s["gsd"], m.n * EB)
                act.wait_ge(s["projg"], m.n + 1)
                nc.scalar.activation(cols(gth), PROJ_B[:, :], ACT.Tanh, scale=0.5).then_inc(s["gth"], 1)
            if t:
                need(act, s["rb"], t.n)
                act.wait_ge(s["rgt"], t.n + 1)
                nc.scalar.activation(rgT[:, :], T7[0:H1, N:2 * N], ACT.Copy).then_inc(s["rgtc"], 1)
            if f:
                ready(J_HID)
                nc.scalar.activation(tdh[:, :], PROJ_A[0:DD, 0:N], ACT.Tanh).then_inc(s["evac"], 1)
            if t:
                act.wait_ge(s["on"], t.n + 1)
                for hb in range(EB):
                    last = nc.scalar.activation(on[:, hb, :], on[:, hb, :], ACT.Identity, bias=hvec[:, hb, 1:2], scale=hvec[:, hb, 0:1])
                last.then_inc(s["on2"], 1)
            if f:
                ready(J_DECAY)
                for eb in range(EB):
                    last = nc.scalar.activation(ew[:, eb, :], pair(PROJ_B)[:, eb, :], ACT.Exp, bias=v("time_decay", eb))
                last.then_inc(s["evac"], 1)
                if isinstance(f.n, int) and f.n == 0:
                    act.wait_ge(decay_set, 1)
                need(act, s["scan"], f.n * NU - NU)
                act.wait_ge(s["evac"], f.n * PJ + J_DECAY + 1)
                for eb in range(EB):
                    last = nc.scalar.activation(bl(wS[f.slot][:, eb, :])[:, :, 1:L1], bl(ew[:, eb, :])[:, :, 0:L1 - 1], ACT.Exp, scale=-1.0)
                last.then_inc(s["ewd"], 1)
                need(act, s["kv"], f.n * NU - NU)
                need(act, s["ruk"], f.n - 1)
                ready(J_K)
                nc.scalar.activation(cols(kT[f.slot]), PROJ_A[:, :], ACT.Copy).then_inc(s["evac"], 1)
                need(act, g_vout[f.slot], f.use * 16 * JH)
                need(act, s["cv"], f.n - 1)
                ready(J_V)
                nc.scalar.activation(cols(vT[f.slot]), PROJ_B[:, :], ACT.Copy).then_inc(s["evac"], 1)
            if e:
                affine(e)
            if t:
                need(act, s["xk"], t.n)
                act.wait_ge(s["feat2"], t.n + 1)
                for eb in range(EB):
                    last = nc.scalar.activation(xa2[:, eb, :, 1:L1 + 1], bl(pair(T6)[:, eb, :]), ACT.Identity, bias=v("ln2_b", eb), scale=v("ln2_w", eb))
                last.then_inc(s["xc"], 1)
            if f:
                need(act, s["rs"], f.n * NU - NU)
                ready(J_R)
                nc.scalar.activation(cols(rT[f.slot]), PROJ_A[:, :], ACT.Copy).then_inc(s["evac"], 1)
            if e:
                mixing_tanh(e)
            if t:
                need(act, s["fvp"], t.n)
                act.wait_ge(s["kkp"], t.n + 1)
                nc.scalar.activation(cols(kk), T7[:, :], ACT.Relu).then_inc(s["kkr"], 1)
                act.wait_ge(s["kkr"], t.n + 1)
                nc.scalar.activation(cols(kk), cols(kk), ACT.Square).then_inc(s["kk"], 1)
                need(act, s["y"], t.n)
                act.wait_ge(s["rrp"], t.n + 1)
                nc.scalar.activation(cols(th2), T6[:, :], ACT.Tanh, scale=0.5).then_inc(s["th2"], 1)
        return {NPAIR: [lambda: affine(first)], NPAIR + 1: [lambda: mixing_tanh(first)]}, lambda: iterations(act, run)

    def vector(dve, kept):

        def statistics(n, i, src, st_, edge, ag):
            stats, mv, _ = norms[i]
            for b in range(GB):
                last = nc.vector.bn_stats(stats[:, b, :], src[:, b, :])
            last.then_inc(s[st_], 1)
            dve.wait_ge(s[st_], n + 1)
            edge()
            for b in range(GB):
                last = nc.vector.bn_aggr(mv[:, b, :], stats[:, b, :])
            last.then_inc(s[ag], 1)

        def normalise(n, i, src, dst, ready, done):
            _, mv, rstd = norms[i]
            dve.wait_ge(s[ready], n + 1)
            for b in range(GB):
                last = nc.vector.tensor_scalar(dst[:, b, :], src[:, b, :], mv[:, b, 0:1], rstd[:, b:b + 1], ALU.subtract, ALU.mult)
            last.then_inc(s[done], 1)

        def first_statistics(e):
            dve.wait_ge(x_ready[e.slot], e.use * 32 + 32)

            def edge():
                need(dve, s["sx"], e.n - 1)
                nc.vector.tensor_copy(xa[e.slot][:, :, :, 0], st1[e.slot][:, :, :]).then_inc(s["edge"], 1)
            statistics(e.n, 0, x_in[e.slot], "stats", edge, "aggr")

        def first_norm(e):
            need(dve, s["feat"], e.n)
            normalise(e.n, 0, x_in[e.slot], xn, "rstd", "normed")

        def mixing_input(e):
            need(dve, s["maa"], e.n)
            dve.wait_ge(s["xa"], e.n + 1)
            dve.wait_ge(s["sx"], e.n + 1)
            for eb in range(EB):
                last = nc.vector.scalar_tensor_tensor(bl(mixin[:, eb, :]), bl(sx[e.slot][:, eb, :]), v("maa_x", eb), xa[e.slot][:, eb, :, 1:L1 + 1], ALU.mult, ALU.add)
            last.then_inc(s["mixin"], 1)

        def run(x, e, f, m, t):
            def mix(i0, i1):
                if not f:
                    return
                for i in range(i0, i1):
                    kind, eb = MIX_ORDER[i // EB], i % EB
                    need(dve, s["xm"], f.n * NM + i - NZ + 1)
                    if eb == 0:
                        dve.wait_ge(s["xxx"], f.n * NMIX + i // EB + 1)
                    nc.vector.scalar_tensor_tensor(mix_buffer(f, i), mix_bank(f, i), v(f"stack{kind}", eb), sx[f.slot][:, eb, :], ALU.add, ALU.mult).then_inc(s["z"], 1)

            def scan(i):
                if not m:
                    return
                hb, jq = UN[i]
                if i == 0:
                    dve.wait_ge(s0_ready[m.slot], m.use * 16 + 16)
                    dve.wait_ge(s["ewd"], m.n + 1)
                dve.wait_ge(s["kv"], m.n * NU + i + 1)
                a4 = aS[i % 2][:, :, :].rearrange("p j (b l) -> p j b l", b=GB)
                nc.vector.tensor_copy(a4[:, :, :, 0], s0[m.slot][:, hb, jq * JH:(jq + 1) * JH, :]).then_inc(s["edge2"], 1)
                dve.wait_ge(s["edge2"], m.n * NU + i + 1)
                for j in range(JH):
                    last = nc.vector.tensor_tensor_scan(SS[i % 2][:, j, :], wS[m.slot][:, hb, :], aS[i % 2][:, j, :], 0.0, ALU.mult, ALU.add)
                last.then_inc(s["scan"], 1)
                dve.wait_ge(s["scan"], m.n * NU + i + 1)
                nc.vector.tensor_tensor(aS[i % 2][:, :, :], SS[i % 2][:, :, :], rT[m.slot][:, hb:hb + 1, :].broadcast_to((128, JH, N)), ALU.mult).then_inc(s["rs"], 1)

            if m:
                need(dve, s["cb"], m.n)
                dve.wait_ge(s["evac"], m.n * PJ + J_R + 1)
                for hb in range(EB):
                    last = nc.vector.scalar_tensor_tensor(ruk[:, hb, :], rT[m.slot][:, hb, :], v("u", hb), kT[m.slot][:, hb, :], ALU.mult, ALU.mult)
                last.then_inc(s["ruk"], 1)
            if isinstance(f, Pair) and isinstance(f.n, int) and f.n == 0:
                kept(dve, NPAIR)
                for i in range(2):
                    last = nc.vector.memset(wS[i][:, :, :].rearrange("p a (b l) -> p a b l", b=GB)[:, :, :, 0], 0.0)
                last.then_inc(decay_set, 1)
            mix(0, 4)
            if m:
                need(dve, s["cent"], m.n - 1)
                dve.wait_ge(s["cb"], m.n + 1)
                nc.vector.tensor_tensor(og[m.slot][:, :, :], STATE[:, 0:N].unsqueeze(1).broadcast_to((128, EB, N)), vT[m.slot][:, :, :], ALU.mult).then_inc(s["cv"], 1)
            if t:
                need(dve, s["rgt"], t.n)
                dve.wait_ge(s["sd"], t.n + 1)
                nc.vector.reciprocal(rg[:, :, :].rearrange("p b h -> p (b h)"), sd[:, :]).then_inc(s["vg"], 1)
            scan(0)
            if m:
                need(dve, s["gated"], m.n - 1)
                dve.wait_ge(s["gth"], m.n + 1)
                nc.vector.scalar_tensor_tensor(cols(gs[m.slot]), cols(gth), 1.0, PROJ_B[:, :], ALU.add, ALU.mult).then_inc(s["gsd"], EB)
            mix(4, 6)
            if t:
                need(dve, s["gated"], t.n)
                dve.wait_ge(s["sq"], t.n + 1)
                dve.wait_ge(s["rb"], t.n + 1)
                nc.vector.tensor_tensor(on[:, :, :], cent[:, :, :], T6[:, 0:N].unsqueeze(1).broadcast_to((128, EB, N)), ALU.mult).then_inc(s["on"], 1)
            if e:
                first_statistics(e)
            scan(1)
            mix(6, 8)
            if t:
                dve.wait_ge(res_ready[t.slot], t.use * 32 + 32)
                dve.wait_ge(s["wo"], t.n + 1)
                nc.vector.tensor_tensor(cols(x1), T7[:, :], cols(xres[t.slot]), ALU.add).then_inc(s["x1"], 1)
                dve.wait_ge(s["x1"], t.n + 1)

                def edge():
                    need(dve, s["sx2"], t.n)
                    nc.vector.tensor_copy(xa2[:, :, :, 0], st0[t.slot][:, :, :]).then_inc(s["edgec"], 1)
                statistics(t.n, 1, x1, "stats2", edge, "aggr2")
            if e:
                first_norm(e)
            if t:
                need(dve, s["feat2"], t.n)
                normalise(t.n, 1, x1, xn2, "rstd2", "normed2")
            scan(2)
            if e:
                mixing_input(e)
            if t:
                need(dve, s["rrp"], t.n)
                dve.wait_ge(s["xc"], t.n + 1)
                dve.wait_ge(s["sx2"], t.n + 1)
                for dst, name in ((xk, "ffn_maa_k"), (xr, "ffn_maa_r")):
                    for eb in range(EB):
                        last = nc.vector.scalar_tensor_tensor(bl(dst[:, eb, :]), bl(sx2[:, eb, :]), v(name, eb), xa2[:, eb, :, 1:L1 + 1], ALU.mult, ALU.add)
                last.then_inc(s["xk"], 1)
            scan(3)
            if m:
                dve.wait_ge(s["summed"], m.n * NU + NU)
                nc.vector.tensor_tensor(cols(og[m.slot]), STATE[:, :], cols(og[m.slot]), ALU.add).then_inc(s["og"], 1)
            mix(8, 10)
            if t:
                dve.wait_ge(s["th2"], t.n + 1)
                dve.wait_ge(s["fvp"], t.n + 1)
                nc.vector.scalar_tensor_tensor(cols(y), cols(th2), 1.0, T7[:, :], ALU.add, ALU.mult).then_inc(s["y"], 1)
                need(dve, g_out[t.slot], t.use * 16)
                dve.wait_ge(s["y"], t.n + 1)
                nc.vector.scalar_tensor_tensor(cols(out_t[t.slot]), cols(y), 0.5, cols(x1), ALU.mult, ALU.add).then_inc(s["fin"], 1)
        return {NPAIR - 1: [lambda: first_statistics(first)], NPAIR: [lambda: first_norm(first)],
                NPAIR + 1: [lambda: mixing_input(first)]}, lambda: iterations(dve, run)

    return {"tensor": tensor, "scalar": scalar, "vector": vector, "gpsimd": gpsimd, "sync": sync}


def program(nc, W):
    persistent = ExitStack()
    with persistent:
        sem = lambda name: persistent.enter_context(nc.semaphore(name))
        sb = lambda name, shape, dt: persistent.enter_context(nc.sbuf_tensor(name, shape, dt))
        env = {"sem": sem, "in": W, "sb": sb}
        env["pb"] = [persistent.enter_context(nc.psum_tensor(f"bank{i}", [128, 512], F32)) for i in range(8)]
        env["dram"] = {
            "stack": nc.dram_tensor("stack_scratch", [SLOTS, 2, 128, NTERM, T], BF16).ap(),
            "q": nc.dram_tensor("q_scratch", [NB, C, T], F32).ap(),
            "raw": nc.dram_tensor("raw_scratch", [NB, 128, 4, T], F32).ap(),
            "rden": nc.dram_tensor("rden_scratch", [NB, 4, D0, 4, T], F32).ap(),
            "x1": nc.dram_tensor("x1_scratch", [NB, C, T], F32).ap(),
            "v": nc.dram_tensor("v_scratch", [2, H1, S1 // JH, JH, GB * L1], F32).ap(),
        }
        ident, ident_b = sb("ident", [128, 128], F32), sb("ident_b", [128, 128], BF16)
        half, epst = sb("minus_half", [128, 128], F32), sb("eps", [128, 16], F32)
        zero = sb("zero", [128, 1, 1], F32)
        env.update(ident=ident, ident_b=ident_b, half=half, epst=epst, zero=zero)
        shapes = {
            "f_wo": [128, C], "f_w1": [128, 2 * C], "f_w2": [128, F0, C], "f_vec": [128, 3 + F0],
            "g_vec": [128, EB, len(VECS)], "g_maa1": [128, EB, NMIX * DM], "g_maa2": [128, E1], "g_maa2b": [DM, E1],
            "g_td1": [128, EB, DD], "g_td2": [DD, E1], "g_headsum": [128, EB, 128], "g_centre": [128, 2, 128],
            "g_headmean": [128, H1], "g_hsel": [H1, 128],
        }
        for name, shape in shapes.items():
            env[name] = sb(name, shape, F32)
        env["g_w"] = {name: sb("g_" + name, [128, EB, E1], F32) for name in MATS}
        env["g_hvec"] = sb("g_hvec", [128, EB, 2], F32)
        loads = [(env[name], W[name]) for name in shapes] + [(env["g_w"][name], W["g_" + name]) for name in MATS]
        weights_in, consts_in, const_set, hvec_set = sem("weights_in"), sem("consts_in"), sem("const_set"), sem("hvec_set")
        ident_cast = sem("ident_cast")
        env.update(consts_in=consts_in, const_set=const_set, nconst=16 * 6)
        env["keep"] = sb
        env["early_tiles"] = early_tiles(sb)
        phases = []
        for phase in (attention, feed_forward, recurrent):
            with ExitStack() as arena:
                env["sb"] = lambda name, shape, dt: arena.enter_context(nc.sbuf_tensor(name, shape, dt))
                phases.append(phase(nc, env))
        block = persistent.enter_context(nc.Block())

        @block.sync
        def _(sp):
            sp.dma_start(ident[:, :], W["ident"]).then_inc(consts_in, 16)
            phases[0]["tables"](sp)
            for tile, src in loads:
                sp.dma_start(tile[tuple(slice(None) for _ in tile.shape)], src).then_inc(weights_in, 16)
            def denominators():
                phases[0]["stored"](sp, DEN_CHUNKS[0][1])
                phases[1]["early_denominators"](sp)
            phases[0]["sync"](sp, {NB - 1: denominators, NB: lambda: phases[1]["early_pairs"](sp)})
            phases[1]["sync"](sp)
            phases[2]["sync"](sp, phases[1]["kept"])

        @block.gpsimd
        def _(pool):
            nc.gpsimd.memset(half[:, :], -0.5).then_inc(const_set, 1)
            nc.gpsimd.memset(epst[:, :], EPS).then_inc(const_set, 1)
            nc.gpsimd.memset(zero[:, :, :], 0.0).then_inc(const_set, 1)
            pool.wait_ge(const_set, 3)
            phases[0]["gpsimd"](pool)
            first_group, rest = phases[2]["gpsimd"](pool)
            phases[1]["gpsimd"](pool, first_group)
            rest()

        @block.tensor
        def _(pe):
            pe.wait_ge(consts_in, env["nconst"])
            pe.wait_ge(ident_cast, 1)
            phases[0]["tensor"](pe)
            pe.wait_ge(weights_in, 16 * len(loads))
            first_group, rest = phases[2]["tensor"](pe)
            phases[1]["tensor"](pe, first_group)
            rest()

        @block.scalar
        def _(act):
            phases[0]["scalar"](act)
            act.wait_ge(weights_in, 16 * len(loads))
            act.wait_ge(hvec_set, 1)
            first_group, rest = phases[2]["scalar"](act)
            phases[1]["scalar"](act, first_group)
            rest()

        @block.vector
        def _(dve):
            phases[0]["clear"](dve)
            dve.wait_ge(consts_in, env["nconst"])
            nc.vector.tensor_copy(ident_b[:, :], ident[:, :]).then_inc(ident_cast, 1)
            phases[0]["vector"](dve, {NB - 1: lambda: phases[1]["invert"](dve, 0)})
            dve.wait_ge(weights_in, 16 * len(loads))
            i = VECS.index("gn_w")
            nc.vector.tensor_scalar(env["g_hvec"][:, :, :], env["g_vec"][:, :, i:i + 2], 0.5, None, ALU.mult).then_inc(hvec_set, 1)
            first_group, rest = phases[2]["vector"](dve, phases[1]["kept"])
            phases[1]["vector"](dve, first_group)
            rest()


MATS = ("Wk", "Wv", "Wr", "Wg", "Wo", "Wfk", "Wfr", "Wfv")


def arrays_for(inputs):
    a = {k: np.asarray(v) for k, v in inputs.items()}
    p0, p1 = "L0_xattn_", "L1_xattn_"
    out = {k: a[k] for k in (p0 + "Wq", p0 + "Wk", p0 + "Wv")}
    out["ln"] = np.stack([a[p0 + k] for k in ("ln_q_g", "ln_q_b", "ln_kv_g", "ln_kv_b")], axis=1)
    x, ctx = a["x"], a["ctx_2048"]
    out["x_ctx"] = np.stack([x, ctx], axis=2)
    pos = np.arange(T, dtype=np.float32)[:, None]
    ang = pos * np.exp(np.arange(0, C, 2, dtype=np.float32) * np.float32(-math.log(10000.0) / C))
    table = np.zeros((T, C), np.float32)
    table[:, 0::2], table[:, 1::2] = np.sin(ang), np.cos(ang)
    out["pos"] = np.ascontiguousarray(table.T)
    out["ident"] = np.eye(128, dtype=np.float32)
    rows = [(2 * g + j % 2 + NTILE * (j // 2)) * D0 + d for j in range(4) for d in range(D0) for g in range(4)]
    out["f_wo"] = a[p0 + "Wo"][rows]
    out["f_w1"] = a[p0 + "W1"]
    out["f_w2"] = np.ascontiguousarray(a[p0 + "W2"].reshape(F0, 128, C).transpose(1, 0, 2))
    out["f_vec"] = np.stack([a[p0 + "ffn_ln_g"], a[p0 + "ffn_ln_b"], a[p0 + "b2"], *a[p0 + "b1"].reshape(F0, 128)], axis=1)

    def halves(m):
        return np.ascontiguousarray(m.reshape(EB, 128, -1).transpose(1, 0, 2))
    by_j = np.arange(E1).reshape(H1, S1).T.reshape(-1)
    vecs = {n: a[p1 + n] for n in VECS if p1 + n in a}
    vecs.update({n: a[p1 + n][by_j] for n in ("gn_w", "gn_b")})
    vecs["u"] = a[p1 + "u"].reshape(E1)
    vecs.update({f"stack{f}": a[p1 + "maa_stack"][0, f] for f in range(NMIX)})
    out["g_vec"] = halves(np.stack([vecs[n] for n in VECS], axis=1))
    out["g_maa1"] = halves(a[p1 + "maa_w1"])
    out["g_maa2"] = a[p1 + "maa_w2"][0:4].reshape(128, E1)
    out["g_maa2b"] = a[p1 + "maa_w2"][4]
    out["g_td1"], out["g_td2"] = halves(a[p1 + "td_w1"]), a[p1 + "td_w2"]
    for n in MATS:
        m = a[p1 + n].T
        out["g_" + n] = halves(m[:, by_j] if n in ("Wv", "Wg") else m[by_j] if n == "Wo" else m)
    r = np.arange(128)
    out["g_headsum"] = np.stack([r[:, None] // S1 + 16 * hb == r[None, :] % H1 for hb in range(EB)], axis=1).astype(np.float32)
    same = (r[:, None] % H1 == r[None, :] % H1).astype(np.float32)
    out["g_centre"] = np.stack([np.eye(128) - same / S1, -same / S1], axis=1).astype(np.float32)
    out["g_headmean"] = (r[:, None] % H1 == np.arange(H1)[None, :]).astype(np.float32) / np.float32(S1)
    out["g_hsel"] = (np.arange(H1)[:, None] == r[None, :] % H1).astype(np.float32)
    state = ctx[:, 0:2].reshape(NG, GB, 2, EB, 128).transpose(2, 0, 4, 3, 1).reshape(2, NG, 128, -1)
    out["st0"], out["st1"] = state[0], state[1]
    out["s0"] = np.ascontiguousarray(ctx[:, 2:2 + S1].reshape(NG, GB, EB, 128, S1).transpose(0, 3, 2, 4, 1).reshape(NG, 128, -1))
    return {k: np.ascontiguousarray(v) for k, v in out.items()}


def kernel(**inputs):
    import concourse.bacc as bacc
    from concourse.bass_utils import run_bass_kernel_spmd

    nc = bacc.Bacc("TRN2", target_bir_lowering=False, num_devices=1)
    arrays = {"in_" + k: v for k, v in arrays_for(inputs).items()}
    W = {k[3:]: nc.dram_tensor(k, v.shape, mybir.dt.from_np(v.dtype), kind="ExternalInput").ap() for k, v in arrays.items()}
    W["out"] = nc.dram_tensor("result", (NB, L1, E1), F32, kind="ExternalOutput").ap()
    program(nc, W)
    r = run_bass_kernel_spmd(nc, [arrays], core_ids=[0])
    return r.results[0]["result"]
```
